# Optimizing a Trainium2 kernel written in Bass

```python
import numpy as np
import jax
import jax.numpy as jnp

def _softmax(x, axis=-1):
    return jax.nn.softmax(x, axis=axis)
def _gelu(x):
    return jax.nn.gelu(x, approximate=True)
def _silu(x):
    return jax.nn.silu(x)
def _sigmoid(x):
    return jax.nn.sigmoid(x)
def _layernorm(x, axis=-1, eps=1e-5):
    m = jnp.mean(x, axis=axis, keepdims=True)
    v = jnp.var(x, axis=axis, keepdims=True)
    return (x - m) / jnp.sqrt(v + eps)
def _scatter_add(tgt, idx, src, axis=0):
    return tgt.at[idx].add(src)
def _segment_sum(src, seg, n):
    return jax.ops.segment_sum(src, seg, n)

kernel_name = 'mk_conv_preact_d2_conv_nchw1024_41eff1'

def setup_inputs(seed: int = 0):
    np.random.seed(seed)
    _w = jnp.asarray
    def _rec_inputs():
        import jax
        import jax.numpy as jnp
        _gk = jax.random.key(seed)
        x = -0.0003482 + 1 * jax.random.normal(jax.random.fold_in(_gk, 1), (8, 1024, 48, 48), jnp.float32)
        return x
    x = _rec_inputs()
    def _L0_conv_setup():
        import jax, jax.numpy as jnp
        import numpy as np
        N_CHUNKS = 16
        D_STATE = 16
        D_CONV = 4
        EXPAND = 2
        INPUT_DIM = 1024
        OUTPUT_DIM = 1024
        D_MODEL = INPUT_DIM // N_CHUNKS
        D_INNER = EXPAND * D_MODEL
        DT_RANK = max(1, -(-D_MODEL // 16))

        def _ln(x, g, b, eps=1e-05):
            mu = x.mean(-1, keepdims=True)
            var = ((x - mu) ** 2).mean(-1, keepdims=True)
            return (x - mu) / jnp.sqrt(var + eps) * g + b

        def _mamba(xc, in_proj_w, conv_w, conv_b, x_proj_w, dt_proj_w, dt_proj_b, A_log, D_p, out_proj_w):
            Bc, L, _ = xc.shape
            d_inner, d_conv = conv_w.shape
            d_state = A_log.shape[1]
            dt_rank = dt_proj_w.shape[1]
            xz = jnp.einsum('bld,ed->ble', xc, in_proj_w)
            xm, z = jnp.split(xz, 2, axis=-1)
            xpad = jnp.pad(xm, ((0, 0), (d_conv - 1, 0), (0, 0)))
            xconv = conv_b + sum((conv_w[:, k] * xpad[:, k:k + L, :] for k in range(d_conv)))
            xconv = jax.nn.silu(xconv)
            x_dbl = jnp.einsum('bld,ed->ble', xconv, x_proj_w)
            dt_raw = x_dbl[..., :dt_rank]
            Bm = x_dbl[..., dt_rank:dt_rank + d_state]
            Cm = x_dbl[..., dt_rank + d_state:]
            delta = jax.nn.softplus(jnp.einsum('blr,dr->bld', dt_raw, dt_proj_w) + dt_proj_b)
            A = -jnp.exp(A_log)

            def step(h, inp):
                d_t, B_t, C_t, u_t = inp
                dA = jnp.exp(d_t[:, :, None] * A)
                h = dA * h + d_t[:, :, None] * B_t[:, None, :] * u_t[:, :, None]
                y = jnp.einsum('bds,bs->bd', h, C_t)
                return (h, y)
            h0 = jnp.zeros((Bc, d_inner, d_state), xc.dtype)
            _, ys = jax.lax.scan(step, h0, (delta.swapaxes(0, 1), Bm.swapaxes(0, 1), Cm.swapaxes(0, 1), xconv.swapaxes(0, 1)))
            y = ys.swapaxes(0, 1) + xconv * D_p
            y = y * jax.nn.silu(z)
            return jnp.einsum('bld,md->blm', y, out_proj_w)
        key = jax.random.key(seed)
        ks = jax.random.split(key, 12)
        s = 0.02
        x = jax.random.normal(ks[0], (8, INPUT_DIM, 48, 48), dtype=jnp.float32)
        ln_gamma = jnp.ones((INPUT_DIM,), jnp.float32)
        ln_beta = jnp.zeros((INPUT_DIM,), jnp.float32)
        skip_scale = jnp.ones((1,), jnp.float32)
        in_proj_w = s * jax.random.normal(ks[1], (2 * D_INNER, D_MODEL), dtype=jnp.float32)
        conv_w = s * jax.random.normal(ks[2], (D_INNER, D_CONV), dtype=jnp.float32)
        conv_b = jnp.zeros((D_INNER,), jnp.float32)
        x_proj_w = s * jax.random.normal(ks[3], (DT_RANK + 2 * D_STATE, D_INNER), dtype=jnp.float32)
        dt_proj_w = s * jax.random.normal(ks[4], (D_INNER, DT_RANK), dtype=jnp.float32)
        dt_proj_b = 0.1 * jax.random.normal(ks[5], (D_INNER,), dtype=jnp.float32)
        A_log = jnp.log(jnp.tile(jnp.arange(1, D_STATE + 1, dtype=jnp.float32), (D_INNER, 1)))
        D_p = jnp.ones((D_INNER,), jnp.float32)
        out_proj_w = s * jax.random.normal(ks[6], (D_MODEL, D_INNER), dtype=jnp.float32)
        proj_w = s * jax.random.normal(ks[7], (OUTPUT_DIM, INPUT_DIM), dtype=jnp.float32)
        proj_b = jnp.zeros((OUTPUT_DIM,), jnp.float32)
        return {'x': x, 'ln_gamma': ln_gamma, 'ln_beta': ln_beta, 'skip_scale': skip_scale, 'in_proj_w': in_proj_w, 'conv_w': conv_w, 'conv_b': conv_b, 'x_proj_w': x_proj_w, 'dt_proj_w': dt_proj_w, 'dt_proj_b': dt_proj_b, 'A_log': A_log, 'D_p': D_p, 'out_proj_w': out_proj_w, 'proj_w': proj_w, 'proj_b': proj_b}
    _L0_conv_all = _L0_conv_setup()
    _L0_conv_in = {k: v for k, v in _L0_conv_all.items() if k in ('ln_gamma', 'ln_beta', 'skip_scale', 'in_proj_w', 'conv_w', 'conv_b', 'x_proj_w', 'dt_proj_w', 'dt_proj_b', 'A_log', 'D_p', 'out_proj_w', 'proj_w', 'proj_b', )}
    del _L0_conv_all

    def _L1_conv_setup():
        import jax, jax.numpy as jnp
        import numpy as np
        from jax import lax
        GROUPS = 32
        EPS = 1e-05

        def _bilinear_resize(img, oh, ow):
            H, W = (img.shape[-2], img.shape[-1])

            def idx(n_in, n_out):
                x = (jnp.arange(n_out, dtype=jnp.float32) + 0.5) * (n_in / n_out) - 0.5
                x = jnp.clip(x, 0.0, n_in - 1)
                i0 = jnp.floor(x).astype(jnp.int32)
                i1 = jnp.minimum(i0 + 1, n_in - 1)
                return (i0, i1, x - i0)
            r0, r1, tr = idx(H, oh)
            c0, c1, tc = idx(W, ow)
            top = img[..., r0, :]
            bot = img[..., r1, :]
            row = top + (bot - top) * tr[:, None]
            left = row[..., c0]
            right = row[..., c1]
            return left + (right - left) * tc
        key = jax.random.key(seed)
        ks = jax.random.split(key, 12)
        b, c, h, w = (8, 1024, 64, 64)
        cg = c // GROUPS
        s = 1.0 / np.sqrt(cg)
        inp = {'x': jax.random.normal(ks[0], (b, c, h, w), jnp.float32), 'w1': jax.random.normal(ks[1], (cg, cg), jnp.float32) * s, 'b1': jax.random.normal(ks[2], (cg,), jnp.float32) * 0.01, 'gn_gamma': jnp.ones((cg,), jnp.float32), 'gn_beta': jnp.zeros((cg,), jnp.float32), 'w_dw': jax.random.normal(ks[3], (cg, 1, 3, 3), jnp.float32) * (1.0 / 3.0), 'b_dw': jax.random.normal(ks[4], (cg,), jnp.float32) * 0.01, 'w_pw': jax.random.normal(ks[5], (cg, cg), jnp.float32) * s, 'b_pw': jax.random.normal(ks[6], (cg,), jnp.float32) * 0.01, 'w_fp': jax.random.normal(ks[7], (cg, cg), jnp.float32) * s, 'b_fp': jax.random.normal(ks[8], (cg,), jnp.float32) * 0.01}
        return inp
    _L1_conv_all = _L1_conv_setup()
    _L1_conv_in = {k: v for k, v in _L1_conv_all.items() if k in ('w1', 'b1', 'gn_gamma', 'gn_beta', 'w_dw', 'b_dw', 'w_pw', 'b_pw', 'w_fp', 'b_fp', )}
    del _L1_conv_all

    return {
        "x": x,
        "L0_conv_ln_gamma": _L0_conv_in["ln_gamma"],
        "L0_conv_ln_beta": _L0_conv_in["ln_beta"],
        "L0_conv_skip_scale": _L0_conv_in["skip_scale"],
        "L0_conv_in_proj_w": _L0_conv_in["in_proj_w"],
        "L0_conv_conv_w": _L0_conv_in["conv_w"],
        "L0_conv_conv_b": _L0_conv_in["conv_b"],
        "L0_conv_x_proj_w": _L0_conv_in["x_proj_w"],
        "L0_conv_dt_proj_w": _L0_conv_in["dt_proj_w"],
        "L0_conv_dt_proj_b": _L0_conv_in["dt_proj_b"],
        "L0_conv_A_log": _L0_conv_in["A_log"],
        "L0_conv_D_p": _L0_conv_in["D_p"],
        "L0_conv_out_proj_w": _L0_conv_in["out_proj_w"],
        "L0_conv_proj_w": _L0_conv_in["proj_w"],
        "L0_conv_proj_b": _L0_conv_in["proj_b"],
        "L1_conv_w1": _L1_conv_in["w1"],
        "L1_conv_b1": _L1_conv_in["b1"],
        "L1_conv_gn_gamma": _L1_conv_in["gn_gamma"],
        "L1_conv_gn_beta": _L1_conv_in["gn_beta"],
        "L1_conv_w_dw": _L1_conv_in["w_dw"],
        "L1_conv_b_dw": _L1_conv_in["b_dw"],
        "L1_conv_w_pw": _L1_conv_in["w_pw"],
        "L1_conv_b_pw": _L1_conv_in["b_pw"],
        "L1_conv_w_fp": _L1_conv_in["w_fp"],
        "L1_conv_b_fp": _L1_conv_in["b_fp"],
    }

def reference(x, L0_conv_ln_gamma, L0_conv_ln_beta, L0_conv_skip_scale, L0_conv_in_proj_w, L0_conv_conv_w, L0_conv_conv_b, L0_conv_x_proj_w, L0_conv_dt_proj_w, L0_conv_dt_proj_b, L0_conv_A_log, L0_conv_D_p, L0_conv_out_proj_w, L0_conv_proj_w, L0_conv_proj_b, L1_conv_w1, L1_conv_b1, L1_conv_gn_gamma, L1_conv_gn_beta, L1_conv_w_dw, L1_conv_b_dw, L1_conv_w_pw, L1_conv_b_pw, L1_conv_w_fp, L1_conv_b_fp):
    import jax
    import jax.numpy as jnp
    def _L0_conv_ref(x, ln_gamma, ln_beta, skip_scale, in_proj_w, conv_w, conv_b, x_proj_w, dt_proj_w, dt_proj_b, A_log, D_p, out_proj_w, proj_w, proj_b):
        import jax, jax.numpy as jnp
        import numpy as np
        N_CHUNKS = 16
        D_STATE = 16
        D_CONV = 4
        EXPAND = 2
        INPUT_DIM = 1024
        OUTPUT_DIM = 1024
        D_MODEL = INPUT_DIM // N_CHUNKS
        D_INNER = EXPAND * D_MODEL
        DT_RANK = max(1, -(-D_MODEL // 16))

        def _ln(x, g, b, eps=1e-05):
            mu = x.mean(-1, keepdims=True)
            var = ((x - mu) ** 2).mean(-1, keepdims=True)
            return (x - mu) / jnp.sqrt(var + eps) * g + b

        def _mamba(xc, in_proj_w, conv_w, conv_b, x_proj_w, dt_proj_w, dt_proj_b, A_log, D_p, out_proj_w):
            Bc, L, _ = xc.shape
            d_inner, d_conv = conv_w.shape
            d_state = A_log.shape[1]
            dt_rank = dt_proj_w.shape[1]
            xz = jnp.einsum('bld,ed->ble', xc, in_proj_w)
            xm, z = jnp.split(xz, 2, axis=-1)
            xpad = jnp.pad(xm, ((0, 0), (d_conv - 1, 0), (0, 0)))
            xconv = conv_b + sum((conv_w[:, k] * xpad[:, k:k + L, :] for k in range(d_conv)))
            xconv = jax.nn.silu(xconv)
            x_dbl = jnp.einsum('bld,ed->ble', xconv, x_proj_w)
            dt_raw = x_dbl[..., :dt_rank]
            Bm = x_dbl[..., dt_rank:dt_rank + d_state]
            Cm = x_dbl[..., dt_rank + d_state:]
            delta = jax.nn.softplus(jnp.einsum('blr,dr->bld', dt_raw, dt_proj_w) + dt_proj_b)
            A = -jnp.exp(A_log)

            def step(h, inp):
                d_t, B_t, C_t, u_t = inp
                dA = jnp.exp(d_t[:, :, None] * A)
                h = dA * h + d_t[:, :, None] * B_t[:, None, :] * u_t[:, :, None]
                y = jnp.einsum('bds,bs->bd', h, C_t)
                return (h, y)
            h0 = jnp.zeros((Bc, d_inner, d_state), xc.dtype)
            _, ys = jax.lax.scan(step, h0, (delta.swapaxes(0, 1), Bm.swapaxes(0, 1), Cm.swapaxes(0, 1), xconv.swapaxes(0, 1)))
            y = ys.swapaxes(0, 1) + xconv * D_p
            y = y * jax.nn.silu(z)
            return jnp.einsum('bld,md->blm', y, out_proj_w)
        B, C, H, W = x.shape
        L = H * W
        dm = C // N_CHUNKS
        xf = x.reshape(B, C, L).transpose(0, 2, 1)
        xn = _ln(xf, ln_gamma, ln_beta)
        xc = xn.reshape(B, L, N_CHUNKS, dm).transpose(0, 2, 1, 3).reshape(B * N_CHUNKS, L, dm)
        ym = _mamba(xc, in_proj_w, conv_w, conv_b, x_proj_w, dt_proj_w, dt_proj_b, A_log, D_p, out_proj_w) + skip_scale * xc
        ym = ym.reshape(B, N_CHUNKS, L, dm).transpose(0, 2, 1, 3).reshape(B, L, C)
        ym = _ln(ym, ln_gamma, ln_beta)
        out = jnp.einsum('blc,oc->blo', ym, proj_w) + proj_b
        return out.transpose(0, 2, 1).reshape(B, proj_w.shape[0], H, W)

    def _L1_conv_ref(x, w1, b1, gn_gamma, gn_beta, w_dw, b_dw, w_pw, b_pw, w_fp, b_fp):
        import jax, jax.numpy as jnp
        import numpy as np
        from jax import lax
        GROUPS = 32
        EPS = 1e-05

        def _bilinear_resize(img, oh, ow):
            H, W = (img.shape[-2], img.shape[-1])

            def idx(n_in, n_out):
                x = (jnp.arange(n_out, dtype=jnp.float32) + 0.5) * (n_in / n_out) - 0.5
                x = jnp.clip(x, 0.0, n_in - 1)
                i0 = jnp.floor(x).astype(jnp.int32)
                i1 = jnp.minimum(i0 + 1, n_in - 1)
                return (i0, i1, x - i0)
            r0, r1, tr = idx(H, oh)
            c0, c1, tc = idx(W, ow)
            top = img[..., r0, :]
            bot = img[..., r1, :]
            row = top + (bot - top) * tr[:, None]
            left = row[..., c0]
            right = row[..., c1]
            return left + (right - left) * tc
        b, c, h, w = x.shape
        cg = c // GROUPS
        bg = b * GROUPS
        gx = x.reshape(bg, cg, h, w)
        x_h = gx.mean(axis=3, keepdims=True)
        x_w = gx.mean(axis=2, keepdims=True)
        cat = jnp.concatenate([x_h, jnp.transpose(x_w, (0, 1, 3, 2))], axis=2)
        hw = jnp.einsum('oc,bcln->boln', w1, cat) + b1[None, :, None, None]
        xh_g, xw_g = (hw[:, :, :h], hw[:, :, h:])
        gated = gx * jax.nn.sigmoid(xh_g) * jax.nn.sigmoid(jnp.transpose(xw_g, (0, 1, 3, 2)))
        mu = gated.mean(axis=(-2, -1), keepdims=True)
        var = gated.var(axis=(-2, -1), keepdims=True)
        x1 = (gated - mu) / jnp.sqrt(var + EPS) * gn_gamma[None, :, None, None] + gn_beta[None, :, None, None]
        dw = lax.conv_general_dilated(gx, w_dw, window_strides=(1, 1), padding=((1, 1), (1, 1)), feature_group_count=cg, dimension_numbers=('NCHW', 'OIHW', 'NCHW'))
        dw = dw + b_dw[None, :, None, None]
        x2 = jnp.einsum('oc,bchw->bohw', w_pw, dw) + b_pw[None, :, None, None]
        freq_mag = jnp.abs(jnp.fft.rfft2(gx, norm='ortho'))
        fm = freq_mag.mean(axis=-1)
        fmap = _bilinear_resize(fm, h, w)
        freq_feat = fmap[:, None] * w_fp.sum(axis=1)[None, :, None, None] + b_fp[None, :, None, None]
        s1 = jax.nn.softmax(x1.mean(axis=(-2, -1)), axis=-1)
        s2 = jax.nn.softmax(x2.mean(axis=(-2, -1)), axis=-1)
        wts = jnp.einsum('bc,bchw->bhw', s1, x2) + jnp.einsum('bc,bchw->bhw', s2, x1)
        weights = wts[:, None] + freq_feat
        return (gx * jax.nn.sigmoid(weights)).reshape(b, c, h, w)

    def _gn(v, G=32, eps=1e-5):
        B_, C_, H_, W_ = v.shape
        g = v.reshape(B_, G, C_ // G, H_, W_)
        m = jnp.mean(g, axis=(2, 3, 4), keepdims=True)
        s = jnp.var(g, axis=(2, 3, 4), keepdims=True)
        return ((g - m) / jnp.sqrt(s + eps)).reshape(v.shape)

    def _ln_c(v, eps=1e-6):
        m = jnp.mean(v, axis=1, keepdims=True)
        s = jnp.var(v, axis=1, keepdims=True)
        return (v - m) / jnp.sqrt(s + eps)

    def _ln_t(v, eps=1e-5):
        m = jnp.mean(v, axis=-1, keepdims=True)
        s = jnp.var(v, axis=-1, keepdims=True)
        return (v - m) / jnp.sqrt(s + eps)

    def _to_tokens(v):
        B_, C_, H_, W_ = v.shape
        return v.reshape(B_, C_, H_ * W_).transpose(0, 2, 1)
    def _from_tokens(t, like):
        B_, C_, H_, W_ = like.shape
        return t.transpose(0, 2, 1).reshape(B_, C_, H_, W_)

    x = x + _L0_conv_ref(_gn(x), L0_conv_ln_gamma, L0_conv_ln_beta, L0_conv_skip_scale, L0_conv_in_proj_w, L0_conv_conv_w, L0_conv_conv_b, L0_conv_x_proj_w, L0_conv_dt_proj_w, L0_conv_dt_proj_b, L0_conv_A_log, L0_conv_D_p, L0_conv_out_proj_w, L0_conv_proj_w, L0_conv_proj_b)
    x = x + _L1_conv_ref(_gn(x), L1_conv_w1, L1_conv_b1, L1_conv_gn_gamma, L1_conv_gn_beta, L1_conv_w_dw, L1_conv_b_dw, L1_conv_w_pw, L1_conv_b_pw, L1_conv_w_fp, L1_conv_b_fp)
    return x


_drawn_inputs = setup_inputs


def setup_inputs(seed=0):
    import zlib

    import numpy as np

    out = dict(_drawn_inputs(seed))
    spreads = {'L0_conv_ln_gamma': (1.0, 0.2),
     'L0_conv_ln_beta': (0.0, 0.1),
     'L0_conv_conv_b': (0.0, 0.8),
     'L0_conv_D_p': (1.0, 0.6),
     'L0_conv_proj_b': (0.0, 0.1),
     'L1_conv_gn_gamma': (1.0, 0.6),
     'L1_conv_gn_beta': (0.0, 0.8)}
    factors = {'L0_conv_in_proj_w': 8.0,
     'L0_conv_conv_w': 8.0,
     'L0_conv_x_proj_w': 8.0,
     'L0_conv_dt_proj_w': 8.0,
     'L0_conv_dt_proj_b': 8.0,
     'L0_conv_A_log': 8.0,
     'L0_conv_out_proj_w': 8.0,
     'L1_conv_w1': 8.0,
     'L1_conv_b1': 64.0,
     'L1_conv_w_dw': 2.971,
     'L1_conv_b_dw': 41.336,
     'L1_conv_w_pw': 3.283,
     'L1_conv_b_pw': 61.815,
     'L1_conv_b_fp': 54.833}
    for name, (base, spread) in spreads.items():
        noise = np.random.default_rng([zlib.crc32(name.encode()), seed]).standard_normal(out[name].shape)
        drawn = base * np.exp(spread * noise) if base else spread * noise
        out[name] = jnp.asarray(drawn.astype(out[name].dtype))
    for name, factor in factors.items():
        out[name] = (out[name] * factor).astype(out[name].dtype)
    return out
```

```python
import concourse.bass as bass
from concourse import mybir
from contextlib import ExitStack
import numpy as np

fp32 = mybir.dt.float32
bf16 = mybir.dt.bfloat16
ALU = mybir.AluOpType
ACT = mybir.ActivationFunctionType

B, C, H, W = 8, 1024, 48, 48
L = H * W
P = 128
NT = C // P
DM = 64
DI = 128
DS = 16
RANK = 4
CH = 3
LC = L // CH
HB = LC // 2
NBC = 2 * DS
LOADS = 25
SPLIT = 3


STEPS = CH * DS
PAIR = 2 * STEPS
CREDIT = 96

SG = 4
DB = DI // 32
RUN = DB
DA_RING, DBU_RING = 6, 3
H_RING = 2 * RUN

LEAD_SCAN = 6
LEAD_C = 5
LEAD_KEEP = 5
LEAD_DBU = LEAD_SCAN + DBU_RING
LEAD_DA = LEAD_SCAN + DA_RING
LEAD_BC = LEAD_DBU + 3
LEAD_B = LEAD_BC + 1
GATE_AT, OUT_AT, OUT_READ_AT = DS - 3, DS - 2, DS - 1

PSUM_W = dict(zip((4, 5, 7), (("u", c) for c in range(CH)))) | dict(zip((8, 9, 11), (("z", c) for c in range(CH))))
PSUM_W |= dict(zip((16, 17, 19), (("v", c) for c in range(CH))))
PSUM_W |= dict(zip((24, 25, 27, 33, 35, 37, 39, 41, 43), ((f"p{r}", c) for c in range(CH) for r in range(SPLIT))))
READ_W = {k + 1: e for k, e in PSUM_W.items()}
SILU_AT, LN_AT, DELTA_AT, DU_AT = 12, 20, 23, 24
ORDER = [PSUM_W[k] for k in sorted(PSUM_W)]


def clear_semaphores(nc, sems):
    with nc.Block() as block:
        @block.sync
        def _(sp):
            for s in sems:
                sp.sem_clear(s)


def mamba(nc, d, pairs):
    with ExitStack() as ctx:
        def sb(name, shape, dt=fp32):
            return ctx.enter_context(nc.sbuf_tensor(name, shape, dt))

        def ps(name):
            return ctx.enter_context(nc.psum_tensor(name, [P, 2, 512], fp32))

        sems = []

        def sem(name):
            sems.append(ctx.enter_context(nc.semaphore(name)))
            return sems[-1]

        w_conv_a, w_conv_b = sb("w_conv_a", [P, DI]), sb("w_conv_b", [P, DI])
        w_z = sb("w_z", [DM, DI])
        w_step = sb("w_step", [DI, DI])
        w_bc = sb("w_bc", [DI, SPLIT * NBC])
        w_out = sb("w_out", [DI, DM])
        w_skip = sb("w_skip", [DM, DM])
        diag_d = sb("diag_d", [P, P])
        ident = sb("ident", [P, P])
        pick = sb("pick", [SPLIT * NBC, 2 * DB, P], bf16)
        fold = sb("fold", [P, 32])
        minus_hi, minus_mid = sb("minus_hi", [96, 96], bf16), sb("minus_mid", [96, 96], bf16)
        conv_b, step_b, d_col, skip_col = (sb(n, [P, 1]) for n in ("conv_b", "step_b", "d_col", "skip_col"))
        a_neg = sb("a_neg", [P, DS])
        xs = [sb(f"xs{j}", [P, 3 + L]) for j in range(2)]
        u = [sb(f"u{j}", [P, L]) for j in range(2)]
        z = [sb(f"z{j}", [P, L]) for j in range(2)]
        parts = [sb(f"parts{j}", [96, L], bf16) for j in range(2)]
        hi, mid = sb("hi", [96, LC], bf16), sb("mid", [96, LC], bf16)
        delta = sb("delta", [P, L])
        du = sb("du", [P, L])
        delta4 = [sb(f"delta4_{j}", [P, DB, LC]) for j in range(2)]
        du4 = [sb(f"du4_{j}", [P, DB, LC]) for j in range(2)]
        da = [sb(f"da{j}", [P, LC]) for j in range(DA_RING)]
        bb = [sb(f"bb{j}", [P, LC]) for j in range(2)]
        dbu = [sb(f"dbu{j}", [P, LC]) for j in range(DBU_RING)]
        h = [sb(f"h{j}", [P, LC + 1]) for j in range(H_RING)]
        carry = sb("carry", [P, DS])
        ym = [sb(f"ym{j}", [DM, LC]) for j in range(2)]
        psum_b, psum_c, psum_y, psum_w = ps("psum_b"), ps("psum_c"), ps("psum_y"), ps("psum_w")
        wt = h[0]

        s_w, s_wd, s_wp, s_wa = (sem(n) for n in ("weights_loaded", "weights_by_vector", "weights_by_tensor", "decay_exp"))
        s_pad = sem("padding_cleared")
        s_xs = [sem("xs0_loaded"), sem("xs1_loaded")]
        s_fill = sem("prelude_filled")
        s_u, s_z, s_v, s_min, s_split = (sem(n) for n in (
            "u_evacuated", "z_evacuated", "v_evacuated", "min_done", "bc_split"))
        s_silu, s_exp, s_ln, s_delta, s_du = (sem(n) for n in (
            "silu_done", "exp_done", "ln_done", "delta_ready", "du_ready"))
        s_spilled = [sem("delta_in_dram"), sem("du_in_dram")]
        s_delta4 = [sem("delta4_0_filled"), sem("delta4_1_filled")]
        s_du4 = [sem("du4_0_filled"), sem("du4_1_filled")]
        s_bb, s_cb, s_y = (sem(n) for n in ("b_broadcast", "c_broadcast", "y_added"))
        s_bc, s_da, s_dbu, s_scan, s_carry, s_mul = (sem(n) for n in (
            "b_copied", "da_ready", "dbu_ready", "scan_done", "carry_kept", "hc_ready"))
        s_gate, s_of, s_oe = (sem(n) for n in ("gated_ready", "out_filled", "out_evacuated"))
        s_st = [sem("ym0_stored"), sem("ym1_stored")]

        def halves(t):
            return t.rearrange("p (a n) -> p a n", a=2)

        def cut(t, c, p=P):
            return t[0:p, c * LC:(c + 1) * LC]

        def banks(t, p=P):
            return t[0:p, :, 0:HB]

        def bodies(eng, body):
            if pairs > 1:
                with eng.Fori(0, pairs - 1) as i:
                    body(i, False)
            body(pairs - 1, True)

        def where(k):
            k %= PAIR
            return k // STEPS, k % STEPS // DS, k % DS // DB, k % DB

        def filled(i, k):
            return i * (3 * DB * 16) + (k // DS // 2 + 1) * DB * 16

        def copied(full, m, j):
            if isinstance(m, int) and m == 0:
                return ()
            return ((full[0], (m - j) * (3 * DB * 8) + 2 * DB * 16 * j), (full[1], (m - j) * (3 * DB * 8) + DB * 16 * j))

        def wait_for(eng, *pairs):
            values = [v if isinstance(v, int) else eng.to_reg(v) for _, v in pairs]
            for (s, _), v in zip(pairs, values):
                eng.wait_ge(s, v)

        ctx.callback(clear_semaphores, nc, sems)
        block = ctx.enter_context(nc.Block())

        @block.sync
        def _(sp):
            loads = [(w_conv_a[0:DM, :], d["win_t"][:, 0:DI]), (w_conv_a[DM:P, :], d["win_t"][:, 0:DI]),
                     (w_conv_b[0:DM, :], d["win_t"][:, 0:DI]), (w_conv_b[DM:P, :], d["win_t"][:, 0:DI]),
                     (w_z[:], d["win_t"][:, DI:2 * DI]),
                     (w_out[:], d["wout_t"]), (ident[:], d["ident"]), (fold[:], d["fold"]),
                     (z[0][0:96, 0:2 * DB * P], d["pick"]), (z[0][0:96, 1024:1120], d["minus_hi"]),
                     (z[0][0:96, 1120:1216], d["minus_mid"]),
                     (conv_b[:], d["conv_b"]), (step_b[:], d["dt_b"]), (d_col[:], d["dp"]),
                     (skip_col[:], d["skip"].broadcast_to([P, 1])), (a_neg[:], d["a_log"]),
                     (wt[0:RANK, 0:DI], d["xproj"][0:RANK, :]), (wt[0:RANK, DI:2 * DI], d["dtw_t"])]
            loads += [(wt[r * DM:(r + 1) * DM, (2 + q) * DI:(3 + q) * DI], d["conv_t"][3 - 2 * q - r:4 - 2 * q - r, :].broadcast_to([DM, DI]))
                      for q in range(2) for r in range(2)]
            loads += [(w_bc[:, r * NBC:(r + 1) * NBC], d["xproj_t"][:, RANK:RANK + NBC]) for r in range(SPLIT)]
            assert len(loads) == LOADS
            for dst, src in loads:
                sp.dma_start(dst, src).then_inc(s_w, 16)

            def load(n, j):
                sp.dma_start(xs[j][0:DM, 3:3 + L], d["xn"][bass.ds(n * DM, DM), :]).then_inc(s_xs[j], 16)
                sp.dma_start(xs[j][DM:P, 4:3 + L], d["xn"][bass.ds(n * DM, DM), 0:L - 1]).then_inc(s_xs[j], 16)

            def spill(m, j):
                for q, (src, ready, full) in enumerate(((delta, s_delta, s_delta4), (du, s_du, s_du4))):
                    wait_for(sp, (ready, m * 3 + (3 + CREDIT)), *copied(full, m, j))
                    sp.dma_start(d["spill"][q, j], src[:]).then_inc(s_spilled[q], 16)

            def copy4(i, k):
                j, c, _, _ = where(k)
                slot = k // DS % 2
                for q, (dst, used, full) in enumerate(((delta4, s_da, s_delta4), (du4, s_dbu, s_du4))):
                    wait_for(sp, (s_spilled[q], i * 32 + (k // STEPS + 1) * 16), (used, i * PAIR + (k - DS + CREDIT)))
                    for b in range(SG):
                        sp.dma_start(dst[slot][32 * b:32 * b + 32, :, :],
                                     d["spill"][q, j, :, c * LC:(c + 1) * LC].rearrange("(b q) t -> q b t", q=32)
                                     ).then_inc(full[slot], 16)

            sp.wait_ge(s_pad, 4)
            load(0, 0)
            load(1, 1)
            spill(0, 0)
            copy4(0, 0)
            copy4(0, DS)

            def body(i, last):
                for p in range(2):
                    n = i * 2 + p
                    for c in range(CH):
                        if c == 0:
                            copy4(i, p * STEPS + 2 * DS)
                        elif not (last and p == 1):
                            if c == 1:
                                spill(n + 1, 1 - p)
                            copy4(i, p * STEPS + (2 + c) * DS)
                        if c == CH - 1 and not last:
                            sp.wait_ge(s_of, n * 3 + (3 + CREDIT))
                            load(n + 2, p)
                        sp.wait_ge(s_oe, n * 3 + (c + 1 + CREDIT))
                        sp.dma_start(d["ym"][bass.ds(n * DM, DM), c * LC:(c + 1) * LC],
                                     ym[(3 * p + c) % 2][:]).then_inc(s_st[(3 * p + c) % 2], 16)

            bodies(sp, body)
            for j in range(2):
                sp.wait_ge(s_st[j], 16 * 3 * pairs)

        @block.tensor
        def _(pe):
            for s in (s_bb, s_cb, s_y, s_of, s_fill):
                pe.sem_inc(s, CREDIT)
            pe.wait_ge(s_w, 16 * LOADS)
            pe.matmul(psum_b[:, 0, 0:DI], wt[0:RANK, 0:DI], wt[0:RANK, DI:2 * DI], start=True, stop=True).then_inc(s_wp, 1)
            pe.wait_ge(s_wd, 8)

            def freed(e, m, n):
                kind, c = e
                if kind == "u":
                    pe.wait_ge(s_u, m * 3 + (c + 1 + CREDIT))
                elif kind == "z":
                    pe.wait_ge(s_z, m * 3 + (c + 1 + CREDIT))
                elif kind == "v":
                    pe.wait_ge(s_v, m * 3 + (c + 1 + CREDIT))
                elif kind == "o":
                    pe.wait_ge(s_oe, n * 3 + (c + 1 + CREDIT))
                else:
                    pe.wait_ge(s_split, m * 9 + (3 * c + int(kind[1]) + 1 + CREDIT))

            def fill(e, m, j):
                kind, c = e
                for a in range(2):
                    t = c * LC + a * HB
                    now = u[j][:, t:t + HB]
                    if kind == "u":
                        if e == ("u", 0) and a == 0:
                            pe.wait_ge(s_xs[j], (m - j) * 16 + 32)
                        pe.matmul(psum_w[:, a, 0:HB], w_conv_a[:], xs[j][:, 3 + t:3 + t + HB], start=True, stop=False)
                        ins = pe.matmul(psum_w[:, a, 0:HB], w_conv_b[:], xs[j][:, 1 + t:1 + t + HB], start=False, stop=True)
                    elif kind == "z":
                        ins = pe.matmul(psum_w[:, a, 0:HB], w_z[:], xs[j][0:DM, 3 + t:3 + t + HB], start=True, stop=True)
                    elif kind == "v":
                        if a == 0:
                            pe.wait_ge(s_silu, m * 2 + (1 + CREDIT))
                        ins = pe.matmul(psum_w[:, a, 0:HB], w_step[:], now, start=True, stop=True)
                    elif kind == "p0":
                        ins = pe.matmul(psum_w[0:96, a, 0:HB], w_bc[:], now, start=True, stop=True)
                    else:
                        src, minus = (hi, minus_hi) if kind == "p1" else (mid, minus_mid)
                        ins = pe.matmul(psum_w[0:96, a, 0:HB], minus[:], src[:, a * HB:(a + 1) * HB], start=False,
                                        stop=True, skip_group_check=True)
                ins.then_inc(s_fill, 1)

            def b_row(i, k):
                j, c, g, _ = where(k)
                pe.wait_ge(s_bc, i * (PAIR // RUN) + (k // RUN + CREDIT))
                if g == 0:
                    pe.wait_ge(s_split, i * 18 + (k // STEPS * 9 + 3 * c + 3 + CREDIT))
                for a in range(2):
                    t = c * LC + a * HB
                    ins = pe.matmul(psum_b[:, a, 0:HB], pick[:, g, :], parts[j][:, t:t + HB], start=True, stop=True)
                ins.then_inc(s_bb, 1)

            def c_row(i, k):
                j, c, g, _ = where(k)
                pe.wait_ge(s_mul, i * PAIR + (k + CREDIT))
                for a in range(2):
                    t = c * LC + a * HB
                    ins = pe.matmul(psum_c[:, a, 0:HB], pick[:, DB + g, :], parts[j][:, t:t + HB], start=True, stop=True)
                ins.then_inc(s_cb, 1)

            def y_add(i, k):
                j, c, g, _ = where(k)
                if g == 0:
                    pe.wait_ge(s_gate, i * 6 + (k // DS + CREDIT))
                    for a in range(2):
                        pe.matmul(psum_y[:, a, 0:HB], diag_d[:], u[j][:, c * LC + a * HB:c * LC + (a + 1) * HB],
                                  start=True, stop=False)
                pe.wait_ge(s_mul, i * PAIR + (k + RUN + CREDIT))
                for a in range(2):
                    for b in range(DB):
                        ins = pe.matmul(psum_y[32 * b:32 * b + 32, a, 0:HB], fold[:],
                                        h[(k + b) % H_RING][:, a * HB:(a + 1) * HB], start=False, stop=(g == DB - 1),
                                        tile_position=(0, 32 * b))
                ins.then_inc(s_y, 1)

            def out(n, p, c):
                pe.wait_ge(s_gate, n * 3 + (c + 1 + CREDIT))
                for a in range(2):
                    t = 3 + c * LC + a * HB
                    pe.matmul(psum_w[0:DM, a, 0:HB], w_out[:], z[p][:, t - 3:t - 3 + HB], start=True, stop=False)
                    ins = pe.matmul(psum_w[0:DM, a, 0:HB], w_skip[:], xs[p][0:DM, t:t + HB], start=False, stop=True)
                ins.then_inc(s_of, 1)

            for q, e in enumerate(ORDER):
                if q:
                    freed(ORDER[q - 1], 0, 0)
                fill(e, 0, 0)

            def step(i, k, last):
                if (k + LEAD_B) % RUN == 0 and k + LEAD_B >= 0 and not (last and k + LEAD_B >= PAIR):
                    b_row(i, k + LEAD_B)
                if (k + LEAD_C) % RUN == 0 and k + LEAD_C >= 0:
                    if not (last and k + LEAD_C >= PAIR):
                        c_row(i, k + LEAD_C)
                    if k + LEAD_C >= RUN and not (last and k + LEAD_C > PAIR):
                        y_add(i, k + LEAD_C - RUN)

            for k in range(-LEAD_B, 0):
                step(0, k, False)

            def body(i, last):
                for p in range(2):
                    n = i * 2 + p
                    before = None
                    for st in range(STEPS):
                        step(i, p * STEPS + st, last)
                        if not (last and p == 1):
                            for e in [PSUM_W[st]] if st in PSUM_W else ():
                                if before is None:
                                    pe.wait_ge(s_oe, n * 3 + CREDIT)
                                    pe.wait_ge(s_split, n * 9 + (9 + CREDIT))
                                else:
                                    freed(before, n + 1, n)
                                fill(e, n + 1, 1 - p)
                                before = e
                        if st % DS == OUT_AT:
                            if before is not None:
                                freed(before, n + 1, n)
                            else:
                                pe.wait_ge(s_oe, n * 3 + CREDIT)
                                pe.wait_ge(s_split, n * 9 + (9 + CREDIT))
                            out(n, p, st // DS)
                            before = ("o", st // DS)

            bodies(pe, body)

        @block.scalar
        def _(act):
            for s in (s_bc, s_da, s_carry, s_u, s_z, s_v, s_split, s_silu, s_exp, s_ln, s_oe):
                act.sem_inc(s, CREDIT)
            act.wait_ge(s_w, 16 * LOADS)
            act.activation(a_neg[:], a_neg[:], ACT.Exp).then_inc(s_wa, 1)
            act.wait_ge(s_wd, 9)

            def evacuate_u(m, j, c):
                act.wait_ge(s_fill, m * 18 + (c + 1 + CREDIT))
                act.wait_ge(s_y, m * (STEPS // RUN) + (CREDIT - PAIR // RUN + 2 * DB + 1))
                act.activation(halves(cut(u[j], c)), banks(psum_w), ACT.Identity, bias=conv_b[:]).then_inc(s_u, 1)

            def evacuate_z(m, j, c):
                act.wait_ge(s_fill, m * 18 + (3 + c + 1 + CREDIT))
                act.wait_ge(s_of, m * 3 + (CREDIT - 3))
                act.activation(halves(cut(z[j], c)), banks(psum_w), ACT.Identity).then_inc(s_z, 1)

            def evacuate_v(m, j, c):
                act.wait_ge(s_min, m * 3 + (c + 1 + CREDIT))
                act.wait_ge(s_spilled[0], m * 16)
                act.wait_ge(s_du, m * 3 + CREDIT)
                act.activation(halves(cut(delta, c)), banks(psum_w), ACT.Identity, bias=step_b[:]).then_inc(s_v, 1)

            def silus(m, j):
                act.wait_ge(s_u, m * 3 + (3 + CREDIT))
                act.activation(u[j][:], u[j][:], ACT.Silu).then_inc(s_silu, 1)
                act.wait_ge(s_z, m * 3 + (3 + CREDIT))
                act.activation(z[j][:], z[j][:], ACT.Silu).then_inc(s_silu, 1)

            def split(m, j, r, c):
                act.wait_ge(s_fill, m * 18 + (9 + 3 * c + r + 1 + CREDIT))
                if r == SPLIT - 1:
                    act.wait_ge(s_cb, (m - 1) * (STEPS // RUN) + CREDIT)
                dst = (hi[:], mid[:], cut(parts[j], c, 96))[r]
                act.activation(halves(dst), banks(psum_w, 96), ACT.Identity).then_inc(s_split, 1)

            def softplus(m):
                act.wait_ge(s_min, m * 3 + (3 + CREDIT))
                act.activation(du[:], du[:], ACT.Exp).then_inc(s_exp, 1)
                act.wait_ge(s_exp, m + (1 + CREDIT))
                act.activation(du[:], du[:], ACT.Ln, bias=1.0).then_inc(s_ln, 1)

            def copy_b(i, k):
                run = k // RUN
                act.wait_ge(s_bb, i * (PAIR // RUN) + (run + 1 + CREDIT))
                act.wait_ge(s_dbu, i * PAIR + ((run - 1) * RUN + CREDIT))
                act.activation(halves(bb[run % 2][:]), banks(psum_b), ACT.Identity).then_inc(s_bc, 1)

            def decay(i, k):
                j, c, g, b = where(k)
                r = k % DA_RING
                if g == 0 and b == 0:
                    act.wait_ge(s_delta4[k // DS % 2], filled(i, k))
                act.wait_ge(s_scan, i * PAIR + (k + 1 - DA_RING + CREDIT))
                act.activation(da[r][:], delta4[k // DS % 2][:, b, :], ACT.Exp,
                               scale=a_neg[:, g * DB + b:g * DB + b + 1]).then_inc(s_da, 1)

            def keep(i, k):
                j, c, g, b = where(k)
                act.wait_ge(s_scan, i * PAIR + (k + 1 + CREDIT))
                act.activation(carry[:, g * DB + b:g * DB + b + 1], h[k % H_RING][:, LC:LC + 1], ACT.Identity).then_inc(s_carry, 1)

            def step(i, k, last):
                if (k + LEAD_BC) % RUN == 0 and k + LEAD_BC >= 0 and not (last and k + LEAD_BC >= PAIR):
                    copy_b(i, k + LEAD_BC)
                if k + LEAD_DA >= 0 and not (last and k + LEAD_DA >= PAIR):
                    decay(i, k + LEAD_DA)
                if k + LEAD_KEEP >= 0 and not (last and k + LEAD_KEEP >= PAIR):
                    keep(i, k + LEAD_KEEP)

            def out(n, p, c):
                q = (3 * p + c) % 2
                act.wait_ge(s_of, n * 3 + (c + 1 + CREDIT))
                act.wait_ge(s_st[q], (n - p) * 24 + 16 * ((3 * p + c) // 2))
                act.activation(halves(ym[q][:]), banks(psum_w, DM), ACT.Identity).then_inc(s_oe, 1)

            for c in range(CH):
                evacuate_u(0, 0, c)
            for c in range(CH):
                evacuate_z(0, 0, c)
            silus(0, 0)
            for c in range(CH):
                evacuate_v(0, 0, c)
            softplus(0)
            for c in range(CH):
                for r in range(SPLIT):
                    split(0, 0, r, c)
            for k in range(-max(LEAD_BC, LEAD_DA), 0):
                step(0, k, False)

            def body(i, last):
                for p in range(2):
                    n = i * 2 + p
                    for st in range(STEPS):
                        step(i, p * STEPS + st, last)
                        if not (last and p == 1):
                            for kind, c in [READ_W[st]] if st in READ_W else ():
                                if kind == "u":
                                    evacuate_u(n + 1, 1 - p, c)
                                elif kind == "z":
                                    evacuate_z(n + 1, 1 - p, c)
                                elif kind == "v":
                                    evacuate_v(n + 1, 1 - p, c)
                                else:
                                    split(n + 1, 1 - p, int(kind[1]), c)
                            if st == SILU_AT:
                                silus(n + 1, 1 - p)
                            if st == LN_AT:
                                softplus(n + 1)
                        if st % DS == OUT_READ_AT:
                            out(n, p, st // DS)

            bodies(act, body)

        @block.gpsimd
        def _(pool):
            for s in (s_dbu, s_du):
                pool.sem_inc(s, CREDIT)

            def product(m, j, c):
                pool.wait_ge(s_delta, m * 3 + (c + 1 + CREDIT))
                pool.tensor_tensor(cut(du, c), cut(delta, c), cut(u[j], c), ALU.mult).then_inc(s_du, 1)

            def step(i, k):
                j, c, g, b = where(k)
                r = k % DBU_RING
                if b == 0:
                    pool.wait_ge(s_bc, i * (PAIR // RUN) + (k // RUN + 1 + CREDIT))
                    if g == 0:
                        pool.wait_ge(s_du4[k // DS % 2], filled(i, k))
                pool.wait_ge(s_scan, i * PAIR + (k + 1 - DBU_RING + CREDIT))
                pool.tensor_tensor(dbu[r][:], du4[k // DS % 2][:, b, :], bb[k // RUN % 2][:], ALU.mult).then_inc(s_dbu, 1)

            for c in range(CH):
                product(0, 0, c)
            for k in range(LEAD_DBU):
                step(0, k)

            def body(i, last):
                for p in range(2):
                    for st in range(STEPS):
                        k = p * STEPS + st
                        if not (last and k + LEAD_DBU >= PAIR):
                            step(i, k + LEAD_DBU)
                        if not (last and p == 1) and DU_AT <= st < DU_AT + CH:
                            product(i * 2 + (p + 1), 1 - p, st - DU_AT)

            bodies(pool, body)

        @block.vector
        def _(dve):
            for j in range(2):
                dve.memset(xs[j][0:DM, 0:3], 0.0).then_inc(s_pad, 1)
                dve.memset(xs[j][DM:P, 0:4], 0.0).then_inc(s_pad, 1)
            for s in (s_scan, s_mul, s_gate, s_min, s_delta):
                dve.sem_inc(s, CREDIT)
            dve.wait_ge(s_w, 16 * LOADS)
            dve.tensor_copy(pick[:].rearrange("p g q -> p (g q)"), z[0][0:96, 0:1024]).then_inc(s_wd, 1)
            dve.tensor_copy(minus_hi[:], z[0][0:96, 1024:1120]).then_inc(s_wd, 1)
            dve.tensor_copy(minus_mid[:], z[0][0:96, 1120:1216]).then_inc(s_wd, 1)
            dve.tensor_tensor(w_conv_a[:], w_conv_a[:], wt[:, 2 * DI:3 * DI], ALU.mult).then_inc(s_wd, 1)
            dve.tensor_tensor(w_conv_b[:], w_conv_b[:], wt[:, 3 * DI:4 * DI], ALU.mult).then_inc(s_wd, 1)
            dve.tensor_scalar(diag_d[:], ident[:], d_col[:], None, ALU.mult).then_inc(s_wd, 1)
            dve.tensor_scalar(w_skip[:], ident[0:DM, 0:DM], skip_col[0:DM, :], None, ALU.mult).then_inc(s_wd, 1)
            dve.wait_ge(s_wp, 1)
            dve.tensor_copy(w_step[:], psum_b[:, 0, 0:DI]).then_inc(s_wd, 1)
            dve.wait_ge(s_wa, 1)
            dve.tensor_scalar(a_neg[:], a_neg[:], -1.0, None, ALU.mult).then_inc(s_wd, 1)

            def clamp(m, j, c):
                dve.wait_ge(s_fill, m * 18 + (6 + c + 1 + CREDIT))
                dve.wait_ge(s_spilled[1], m * 16)
                dve.tensor_scalar(halves(cut(du, c)), banks(psum_w), step_b[:], 40.0, ALU.add, ALU.min).then_inc(s_min, 1)

            def finish_delta(m, c):
                dve.wait_ge(s_ln, m + (1 + CREDIT))
                dve.wait_ge(s_v, m * 3 + (3 + CREDIT))
                dve.tensor_tensor(cut(delta, c), cut(delta, c), cut(du, c), ALU.max).then_inc(s_delta, 1)

            def scan(i, k):
                j, c, g, b = where(k)
                dve.wait_ge(s_da, i * PAIR + (k + 1 + CREDIT))
                dve.wait_ge(s_dbu, i * PAIR + (k + 1 + CREDIT))
                dve.wait_ge(s_carry, i * PAIR + (k + 1 - H_RING + CREDIT))
                dve.wait_ge(s_y, i * (PAIR // RUN) + (k // RUN - 1 + CREDIT))
                dve.tensor_tensor_scan(h[k % H_RING][:, 1:LC + 1], da[k % DA_RING][:], dbu[k % DBU_RING][:],
                                       carry[:, g * DB + b:g * DB + b + 1] if c else 0.0, ALU.mult,
                                       ALU.add).then_inc(s_scan, 1)

            def times_c(i, k):
                dve.wait_ge(s_scan, i * PAIR + (k + 1 + CREDIT))
                if k % RUN == 0:
                    dve.wait_ge(s_cb, i * (PAIR // RUN) + (k // RUN + 1 + CREDIT))
                hk = h[k % H_RING]
                dve.tensor_tensor(halves(hk[:, 0:LC]), halves(hk[:, 1:LC + 1]), banks(psum_c), ALU.mult).then_inc(s_mul, 1)

            def gate(i, n, p, c):
                dve.wait_ge(s_y, i * (PAIR // RUN) + (p * STEPS // RUN + (c + 1) * DB + CREDIT))
                dve.wait_ge(s_silu, n * 2 + (2 + CREDIT))
                zc = halves(cut(z[p], c))
                dve.tensor_tensor(zc, zc, banks(psum_y), ALU.mult).then_inc(s_gate, 1)

            def step(i, k, last):
                if not (last and k + LEAD_SCAN >= PAIR):
                    scan(i, k + LEAD_SCAN)
                if k % DS == GATE_AT and k >= 0:
                    gate(i, i * 2 + k // STEPS, k // STEPS, k % STEPS // DS)
                if k + LEAD_C >= 0 and not (last and k + LEAD_C >= PAIR):
                    times_c(i, k + LEAD_C)

            for c in range(CH):
                clamp(0, 0, c)
            for c in range(CH):
                finish_delta(0, c)
            for k in range(-LEAD_SCAN, 0):
                step(0, k, False)

            def body(i, last):
                for p in range(2):
                    n = i * 2 + p
                    for st in range(STEPS):
                        step(i, p * STEPS + st, last)
                        if not (last and p == 1):
                            for kind, c in [READ_W[st]] if st in READ_W else ():
                                if kind == "v":
                                    clamp(n + 1, 1 - p, c)
                            if DELTA_AT <= st < DELTA_AT + CH:
                                finish_delta(n + 1, st - DELTA_AT)

            bodies(dve, body)

EPS = 1e-5
TG = B // 2


def pair_bodies(eng, body, count=TG):
    with eng.Fori(0, count - 1) as i:
        body(i, False)
    body(count - 1, True)


def normalise(nc, d, name, src, dst, group_norm):
    with ExitStack() as ctx:
        def sb(n, shape, dt=fp32):
            return ctx.enter_context(nc.sbuf_tensor(f"{name}_{n}", shape, dt))

        sems = []

        def sem(n):
            sems.append(ctx.enter_context(nc.semaphore(f"{name}_{n}")))
            return sems[-1]

        ones, group = sb("ones", [P, P]), sb("group", [P, P])
        gamma, beta = sb("gamma", [P, NT]), sb("beta", [P, NT])
        eps = sb("eps", [P, 1])
        chunks_in = sb("chunks_in", [P, 1])
        x = [[sb(f"x{j}_{k}", [P, L]) for k in range(NT)] for j in range(2)]
        sq = [sb(f"sq{r}", [P, LC]) for r in range(4)]
        rstd = [sb(f"rstd{r}", [P, LC]) for r in range(2)]
        stats, mv = sb("stats", [P, 6, 6]), sb("mv", [P, NT, 2])
        gmean, spread, scale, shift = (sb(n, [P, NT]) for n in ("gmean", "spread", "scale", "shift"))
        psum_mu = [ctx.enter_context(nc.psum_tensor(f"{name}_mu{r}", [P, 2, 512], fp32)) for r in range(2)]
        psum_var = [ctx.enter_context(nc.psum_tensor(f"{name}_var{r}", [P, 2, 512], fp32)) for r in range(2)]
        s_w, s_eps = sem("constants_loaded"), sem("eps_set")
        s_ld, s_st = [sem(f"x{j}_loaded") for j in range(2)], [sem(f"x{j}_stored") for j in range(2)]
        s_bn, s_stat, s_small = sem("bn_chunks"), sem("tile_stats"), sem("group_terms")
        s_bn2, s_lv = sem("spread_terms"), sem("log_variance")
        s_avg, s_rs, s_app = sem("group_averages"), sem("group_rstd"), sem("group_normed")
        s_mu, s_xc, s_sq, s_var = sem("mu_ready"), sem("centred"), sem("squared"), sem("variance_added")
        s_r, s_xn, s_af = sem("rstd_ready"), sem("normed"), sem("scaled")

        def cut(t, c):
            return t[:, c * LC:(c + 1) * LC]

        def halves(t):
            return t.rearrange("p (a n) -> p a n", a=2)

        def banks(t):
            return t[:, :, 0:HB]

        ctx.callback(clear_semaphores, nc, sems)
        block = ctx.enter_context(nc.Block())

        @block.sync
        def _(sp):
            for a, b in ((ones[:], d["ones"]), (group[:], d["group"]), (gamma[:], d["gamma"]), (beta[:], d["beta"])):
                sp.dma_start(a, b).then_inc(s_w, 16)

            def load(n, j, uses, fresh=False):
                if not fresh:
                    sp.wait_ge(s_st[j], uses * (16 * NT * CH))
                for k in range(NT):
                    sp.dma_start(x[j][k][:], src[bass.ds(n * NT + k, 1), :, :].rearrange("a p t -> (a p) t")).then_inc(s_ld[j], 16)

            def store(n, j):
                for c in range(CH):
                    for k in range(NT):
                        sp.wait_ge(s_af, n * 24 + (c * NT + k + 1 + CREDIT))
                        sp.dma_start(dst[bass.ds(n * NT + k, 1), :, c * LC:(c + 1) * LC].rearrange("a p t -> (a p) t"),
                                     cut(x[j][k], c)).then_inc(s_st[j], 16)

            load(0, 0, 0, True)
            load(1, 1, 0, True)

            def body(i, last):
                for j in range(2):
                    store(i * 2 + j, j)
                    if not last:
                        load(i * 2 + j + 2, j, i + 1)

            pair_bodies(sp, body)
            for j in range(2):
                sp.wait_ge(s_st[j], TG * 16 * NT * CH)

        @block.tensor
        def _(pe):
            for s in (s_avg, s_mu, s_var):
                pe.sem_inc(s, CREDIT)
            pe.wait_ge(s_w, 64)

            def averages(n):
                pe.wait_ge(s_stat, n * NT + (NT + CREDIT))
                pe.wait_ge(s_xc, n * 24 + CREDIT)
                pe.matmul(psum_mu[0][:, 0, 0:NT], group[:], mv[:, :, 0], start=True, stop=True).then_inc(s_avg, 1)
                pe.wait_ge(s_small, n * 3 + (2 + CREDIT))
                pe.matmul(psum_mu[0][:, 1, 0:NT], group[:], spread[:], start=True, stop=True).then_inc(s_avg, 1)

            def mean(n, c):
                r = c % 2
                if c < 2:
                    pe.wait_ge(s_xc, n * 24 + CREDIT)
                    if group_norm:
                        pe.wait_ge(s_small, n * 3 + (3 + CREDIT))
                else:
                    pe.wait_ge(s_xc, n * 24 + (NT + CREDIT))
                for k in range(NT):
                    if c == 0:
                        if group_norm:
                            pe.wait_ge(s_app, n * NT + (k + 1 + CREDIT))
                    for a in range(2):
                        ins = pe.matmul(psum_mu[r][:, a, 0:HB], ones[:], x_of(n, k)[:, c * LC + a * HB:c * LC + (a + 1) * HB],
                                        start=(k == 0), stop=(k == NT - 1))
                ins.then_inc(s_mu, 1)

            def variance(n, c):
                r = c % 2
                pe.wait_ge(s_r, n * 3 + (max(0, c - 1) + CREDIT))
                for k in range(NT):
                    pe.wait_ge(s_sq, n * 24 + (c * NT + k + 1 + CREDIT))
                    for a in range(2):
                        ins = pe.matmul(psum_var[r][:, a, 0:HB], ones[:], sq[k % 4][:, a * HB:(a + 1) * HB],
                                        start=(k == 0), stop=(k == NT - 1))
                    ins.then_inc(s_var, 1)

            slot = [0]

            def x_of(n, k):
                return x[slot[0]][k]

            if group_norm:
                averages(0)

            def body(i, last):
                for j in range(2):
                    n = i * 2 + j
                    slot[0] = j
                    if not group_norm:
                        pe.wait_ge(s_ld[j], i * (16 * NT) + 16 * NT)
                    mean(n, 0)
                    mean(n, 1)
                    variance(n, 0)
                    mean(n, 2)
                    variance(n, 1)
                    variance(n, 2)
                    if group_norm and not (last and j == 1):
                        averages(n + 1)

            pair_bodies(pe, body)

        @block.vector
        def _(dve):
            for s in (s_bn, s_stat, s_small, s_xc):
                dve.sem_inc(s, CREDIT)
            dve.memset(eps[:], EPS).then_inc(s_eps, 1)

            def statistics(n, j, uses):
                for k in range(NT):
                    if k == 0:
                        dve.wait_ge(s_avg, n * 2 + CREDIT)
                        dve.wait_ge(s_ld[j], uses * (16 * NT) + 16 * NT)
                    dve.wait_ge(s_stat, n * NT + (k + CREDIT))
                    for q in range(6):
                        ins = dve.bn_stats(stats[:, q, :], x[j][k][:, q * HB:(q + 1) * HB])
                    ins.then_inc(s_bn, 1)
                    dve.wait_ge(s_bn, n * NT + (k + 1 + CREDIT))
                    dve.tensor_copy(chunks_in[:], stats[:, 5, 0:1])
                    dve.bn_aggr(mv[:, k, :], stats[:, :, :].rearrange("p a b -> p (a b)")).then_inc(s_stat, 1)
                dve.wait_ge(s_avg, n * 2 + (1 + CREDIT))
                dve.wait_ge(s_rs, n * 2 + CREDIT)
                dve.tensor_copy(gmean[:], psum_mu[0][:, 0, 0:NT]).then_inc(s_small, 1)
                dve.wait_ge(s_small, n * 3 + (1 + CREDIT))
                dve.tensor_tensor(shift[:], mv[:, :, 0], gmean[:], ALU.subtract).then_inc(s_bn2, 1)
                dve.wait_ge(s_bn2, n * 2 + 1)
                dve.tensor_tensor(shift[:], shift[:], shift[:], ALU.mult).then_inc(s_bn2, 1)
                dve.wait_ge(s_bn2, n * 2 + 2)
                dve.tensor_tensor(spread[:], shift[:], mv[:, :, 1], ALU.add).then_inc(s_small, 1)
                dve.wait_ge(s_rs, n * 2 + (2 + CREDIT))
                dve.scalar_tensor_tensor(out=shift[:], in0=gmean[:], scalar=-1.0, in1=scale[:], op0=ALU.mult,
                                         op1=ALU.mult).then_inc(s_small, 1)

            def centre(n, j, c):
                dve.wait_ge(s_mu, n * 3 + (c + 1 + CREDIT))
                for k in range(NT):
                    xc = halves(cut(x[j][k], c))
                    dve.tensor_tensor(xc, xc, banks(psum_mu[c % 2]), ALU.subtract).then_inc(s_xc, 1)

            if group_norm:
                statistics(0, 0, 0)

            def body(i, last):
                for j in range(2):
                    n = i * 2 + j
                    for c in range(CH):
                        centre(n, j, c)
                    if group_norm and not (last and j == 1):
                        statistics(n + 1, 1 - j, i + j)

            pair_bodies(dve, body)

        @block.scalar
        def _(act):
            for s in (s_rs, s_app, s_sq, s_r, s_af, s_lv):
                act.sem_inc(s, CREDIT)
            act.wait_ge(s_w, 64)
            act.wait_ge(s_eps, 1)

            def apply(n, j):
                act.wait_ge(s_avg, n * 2 + (2 + CREDIT))
                act.activation(scale[:], psum_mu[0][:, 1, 0:NT], ACT.Ln, bias=eps[:]).then_inc(s_rs, 1)
                act.wait_ge(s_rs, n * 2 + (1 + CREDIT))
                act.activation(scale[:], scale[:], ACT.Exp, scale=-0.5).then_inc(s_rs, 1)
                act.wait_ge(s_rs, n * 2 + (2 + CREDIT))
                act.wait_ge(s_small, n * 3 + (3 + CREDIT))
                for k in range(NT):
                    act.activation(x[j][k][:], x[j][k][:], ACT.Identity, scale=scale[:, k:k + 1],
                                   bias=shift[:, k:k + 1]).then_inc(s_app, 1)

            def square(n, j, c):
                for k in range(NT):
                    act.wait_ge(s_xc, n * 24 + (c * NT + k + 1 + CREDIT))
                    act.wait_ge(s_var, n * 24 + (c * NT + k - 3 + CREDIT))
                    act.activation(sq[k % 4][:], cut(x[j][k], c), ACT.Square).then_inc(s_sq, 1)

            def root(n, c):
                act.wait_ge(s_var, n * 24 + ((c + 1) * NT + CREDIT))
                act.wait_ge(s_xn, n * 24 + ((c - 1) * NT + CREDIT))
                act.activation(halves(rstd[c % 2][:]), banks(psum_var[c % 2]), ACT.Ln, bias=eps[:]).then_inc(s_lv, 1)
                act.wait_ge(s_lv, n * 3 + (c + 1 + CREDIT))
                act.activation(rstd[c % 2][:], rstd[c % 2][:], ACT.Exp, scale=-0.5).then_inc(s_r, 1)

            def affine(n, j, c):
                for k in range(NT):
                    act.wait_ge(s_xn, n * 24 + (c * NT + k + 1 + CREDIT))
                    act.activation(cut(x[j][k], c), cut(x[j][k], c), ACT.Identity, scale=gamma[:, k:k + 1],
                                   bias=beta[:, k:k + 1]).then_inc(s_af, 1)

            if group_norm:
                apply(0, 0)

            def body(i, last):
                for j in range(2):
                    n = i * 2 + j
                    square(n, j, 0)
                    square(n, j, 1)
                    root(n, 0)
                    affine(n, j, 0)
                    square(n, j, 2)
                    root(n, 1)
                    affine(n, j, 1)
                    root(n, 2)
                    if group_norm and not (last and j == 1):
                        apply(n + 1, 1 - j)
                    affine(n, j, 2)

            pair_bodies(act, body)

        @block.gpsimd
        def _(pool):
            pool.sem_inc(s_xn, CREDIT)

            def body(i, last):
                for j in range(2):
                    n = i * 2 + j
                    for c in range(CH):
                        pool.wait_ge(s_r, n * 3 + (c + 1 + CREDIT))
                        for k in range(NT):
                            xc = cut(x[j][k], c)
                            pool.tensor_tensor(xc, xc, rstd[c % 2][:], ALU.mult).then_inc(s_xn, 1)

            pair_bodies(pool, body)


def project(nc, d, src, res, dst):
    with ExitStack() as ctx:
        def sb(n, shape, dt=fp32):
            return ctx.enter_context(nc.sbuf_tensor(f"proj_{n}", shape, dt))

        sems = []

        def sem(n):
            sems.append(ctx.enter_context(nc.semaphore(f"proj_{n}")))
            return sems[-1]

        w = sb("w", [P, NT, C])
        bias = sb("bias", [P, NT])
        y = [[sb(f"y{j}_{k}", [P, L]) for k in range(NT)] for j in range(2)]
        xin = [sb(f"xin{r}", [P, LC]) for r in range(4)]
        psum = [ctx.enter_context(nc.psum_tensor(f"proj_psum{r}", [P, 2, 512], fp32)) for r in range(4)]
        s_w = sem("weights_loaded")
        s_y = [sem(f"y{j}_loaded") for j in range(2)]
        s_x = [sem(f"x{r}_loaded") for r in range(4)]
        s_st = [sem(f"x{r}_stored") for r in range(4)]
        s_mm, s_ev = sem("products"), sem("evacuated")
        UNITS = NT * CH

        ctx.callback(clear_semaphores, nc, sems)
        block = ctx.enter_context(nc.Block())

        @block.sync
        def _(sp):
            for k in range(NT):
                sp.dma_start(w[:, k, :], d["proj_t"][k * P:(k + 1) * P, :]).then_inc(s_w, 16)
            sp.dma_start(bias[:], d["proj_b"]).then_inc(s_w, 16)

            def load(n, j):
                sp.wait_ge(s_mm, n * UNITS + (CREDIT - UNITS))
                for k in range(NT):
                    sp.dma_start(y[j][k][:], src[bass.ds(n * NT + k, 1), :, :].rearrange("a p t -> (a p) t")).then_inc(s_y[j], 16)

            load(0, 0)

            def body(i, last):
                for j in range(2):
                    if not (last and j == 1):
                        load(i * 2 + (j + 1), 1 - j)
                    for m in range(NT):
                        for c in range(CH):
                            q = m * CH + c
                            n = i * 2 + j
                            sp.wait_ge(s_ev, n * UNITS + (q + 1 + CREDIT))
                            sp.dma_start(dst[bass.ds(n * NT + m, 1), :, c * LC:(c + 1) * LC].rearrange("a p t -> (a p) t"),
                                         xin[q % 4][:]).then_inc(s_st[q % 4], 16)

            pair_bodies(sp, body)
            for r in range(4):
                sp.wait_ge(s_st[r], B * UNITS // 4 * 16)

        @block.scalar
        def _(act):
            def body(i, last):
                for j in range(2):
                    n = i * 2 + j
                    for m in range(NT):
                        for c in range(CH):
                            q = m * CH + c
                            r = q % 4
                            act.wait_ge(s_st[r], n * (UNITS // 4 * 16) + q // 4 * 16)
                            act.dma_start(xin[r][:], res[bass.ds(n * NT + m, 1), :, c * LC:(c + 1) * LC].rearrange("a p t -> (a p) t")
                                          ).then_inc(s_x[r], 16)

            pair_bodies(act, body)

        @block.tensor
        def _(pe):
            pe.sem_inc(s_mm, CREDIT)
            pe.wait_ge(s_w, 16 * (NT + 1))

            def body(i, last):
                for j in range(2):
                    pe.wait_ge(s_y[j], i * (16 * NT) + 16 * NT)
                    for m in range(NT):
                        for c in range(CH):
                            q = m * CH + c
                            pe.wait_ge(s_ev, i * (2 * UNITS) + (j * UNITS + q - 3 + CREDIT))
                            for k in range(NT):
                                for a in range(2):
                                    t = c * LC + a * HB
                                    ins = pe.matmul(psum[q % 4][:, a, 0:HB], w[:, k, m * P:(m + 1) * P], y[j][k][:, t:t + HB],
                                                    start=(k == 0), stop=(k == NT - 1))
                            ins.then_inc(s_mm, 1)

            pair_bodies(pe, body)

        @block.vector
        def _(dve):
            dve.sem_inc(s_ev, CREDIT)
            dve.wait_ge(s_w, 16 * (NT + 1))

            def body(i, last):
                for j in range(2):
                    n = i * 2 + j
                    for m in range(NT):
                        for c in range(CH):
                            q = m * CH + c
                            r = q % 4
                            dve.wait_ge(s_mm, n * UNITS + (q + 1 + CREDIT))
                            dve.wait_ge(s_x[r], n * (UNITS // 4 * 16) + (q // 4 + 1) * 16)
                            xr = xin[r][:].rearrange("p (a n) -> p a n", a=2)
                            dve.scalar_tensor_tensor(out=xr, in0=psum[r][:, :, 0:HB], scalar=bias[:, m:m + 1], in1=xr,
                                                     op0=ALU.add, op1=ALU.add).then_inc(s_ev, 1)

            pair_bodies(dve, body)

G = 4
CG = P // G
KW = W // 2 + 1
NTILES = B * NT
WP = W + 2
TAPS = 9
VROWS = 68
UN = 4
STAT, FREQ, GATE, OUT = 3, 2, 1, 0


def gated_group(nc, d):
    with ExitStack() as ctx:
        def sb(n, shape, dt=fp32):
            return ctx.enter_context(nc.sbuf_tensor(f"gate_{n}", shape, dt))

        sems = []

        def sem(n):
            sems.append(ctx.enter_context(nc.semaphore(f"gate_{n}")))
            return sems[-1]

        def ps(n):
            return ctx.enter_context(nc.psum_tensor(f"gate_{n}", [P, 2, 512], fp32))

        ident, group, ones4 = sb("ident", [P, P]), sb("group", [P, P]), sb("ones4", [P, P])
        mask4 = sb("mask4", [P, G])
        dft_w, dft_h, dft_0 = sb("dft_w", [96, 96]), sb("dft_h", [96, 96]), sb("dft_0", [96, 192])
        resize = sb("resize", [P, H])
        sel_a, sel_b, sel = sb("sel_a", [VROWS, P]), sb("sel_b", [VROWS, P]), sb("sel", [VROWS, P])
        fp_rows, wfp = sb("fp_rows", [CG, VROWS]), sb("wfp", [CG, P])
        w1a, w1b = sb("w1a", [P, P]), sb("w1b", [P, P])
        wpw, wpw_t = sb("wpw", [P, P]), sb("wpw_t", [P, P])
        taps = sb("taps", [P, TAPS])
        vec = sb("vec", [P, 6])
        srow = sb("srow", [1, 3, P])
        s1 = sb("s1", [P, 1])
        vcol, k1, b2, bias0 = sb("vcol", [P, 1]), sb("k1", [P, TAPS]), sb("b2", [P, 1]), sb("bias0", [P, 1])
        lhs_u = sb("lhs_u", [P, TAPS * G])
        coef = sb("coef", [P, 10])
        eps = sb("eps", [P, 1])
        x = [sb(f"x{j}", [P, L]) for j in range(2)]
        res = [sb(f"res{j}", [P, L]) for j in range(2)]
        gx = [sb(f"gx{j}", [P, L]) for j in range(UN)]
        gated = [sb(f"gated{j}", [P, L]) for j in range(2)]
        out = [sb(f"out{j}", [P, L]) for j in range(2)]
        xt = sb("xt", [96, 24 * P])
        y = sb("y", [P, KW - 1, H, 2])
        yt = sb("yt", [96, 24 * P])
        zsq = sb("zsq", [P, KW, 2, H])
        mag = sb("mag", [P, KW, H])
        up = sb("up", [TAPS * G, (H + 2) * WP])
        v = [sb(f"v{j}", [VROWS, H * WP]) for j in range(2)]
        fmap = sb("fmap", [H, G, W])
        stats, mv = sb("stats", [P, 6, 6]), sb("mv", [P, 2])
        gmean, diff, spread, std, rstd, nb = (sb(n, [P, 1]) for n in ("gmean", "diff", "spread", "std", "rstd", "nb"))
        gstats, gmv = sb("gstats", [P, 6, 6]), sb("gmv", [P, 2])
        gstd, grstd, ga, gc, sa, s2c = (sb(n, [P, 1]) for n in ("gstd", "grstd", "ga", "gc", "sa", "s2c"))
        chunks_in = sb("chunks_in", [P, 2])
        norm_in = sb("norm_in", [P, 1])
        cols = sb("cols", [P, W])
        feat, fprod, mdw, m2 = sb("feat", [P, 10]), sb("fprod", [P, 10]), sb("mdw", [P, 1]), sb("m2", [P, 1])
        srow_t = sb("srow_t", [1, P])
        smax, ssum, srec = (sb(n, [1, G]) for n in ("smax", "ssum", "srec"))
        s2 = sb("s2", [P, 1])
        gates = sb("gates", [P, H + W])
        fm, fmx = sb("fm", [P, H]), sb("fmx", [P, G, H])
        lhs_g = sb("lhs_g", [P, G])
        bias = sb("bias", [P, 1])
        ring = [ps(f"ring{r}") for r in range(3)]
        small = ps("small")
        mean_ps, m2_ps, bias_ps, gates_ps = small[:, 0, 0:1], small[:, 0, 1:2], small[:, 0, 2:3], small[:, 0, 8:8 + H + W]
        var_ps, s2_ps = small[:, 1, 0:1], small[:, 1, 1:2]
        row_ps, fmap_ps = small[0:1, 1, 128:256], small[0:H, 1, 256:256 + G * W]

        names = ("xt_filled xt_copied gsum_filled gsum_copied y_filled y_copied sel_filled sigmoid_done yt_filled yt_copied "
                 "u_filled u_padded z_filled z_squared "
                 "bn_chunks tile_stats fenced mean_averaged mean_read spread_ready var_averaged std_ready rstd_ready shift_ready "
                 "gx_ready cols_ready features products mean_dw mean_x2_filled mean_x2 row_filled row_max row_shifted "
                 "row_exp row_sum row_inverse softmax_row softmax_filled softmax_ready gates_filled gates_ready gated_rows "
                 "gated_ready gated_chunks gated_stats gated_std gated_rstd gated_scale gated_shift gated_weights gated_bias "
                 "bias_filled bias_ready mag2_ready mag_ready fm_ready fm_spread fmap_filled fmap_ready product_done out_ready")
        S = {n: sem(n) for n in names.split()}
        s_w, s_set, s_setd, s_seta, s_setp = (sem(n) for n in (
            "weights_loaded", "cleared", "set_by_vector", "set_by_scalar", "set_by_tensor"))
        s_x, s_res, s_st, s_v = ([sem(f"{n}{j}") for j in range(2)] for n in ("x_loaded", "res_loaded", "stored", "fmap_loaded"))
        s_fd, s_shift = sem("fmap_in_dram"), sem("taps_shifted")

        def wait(eng, name, i, k, n=None, per=1):
            eng.wait_ge(S[name], i * (UN * per) + (k * per + (per if n is None else n) + CREDIT))

        def slot_uses(eng, s, i, k, each):
            eng.wait_ge(s, i * (UN // 2 * each * 16) + (k // 2 + 1) * each * 16)

        def shifted(eng, i, k):
            if k >= 0 or not isinstance(i, int):
                eng.wait_ge(s_shift, i * (UN * TAPS * 16) + (k + 1) * TAPS * 16)

        def steps(eng, step):
            bodies = NTILES // UN
            for k in range(-STAT - 1, 0):
                step(0, k, lambda a, k=k: k + a >= 0)
            with eng.Fori(0, bodies - 1) as i:
                for k in range(UN):
                    step(i, k, lambda a: True)
            for k in range(UN):
                step(bodies - 1, k, lambda a, k=k: k + a < UN)

        def credit(eng, names):
            for n in names.split():
                eng.sem_inc(S[n], CREDIT)

        def two(t):
            return t.rearrange("p (a n) -> p a n", a=2)

        def tile_of(ap, i, k):
            return ap[bass.ds(i * UN + k, 1), :, :].rearrange("a p t -> (a p) t")

        ctx.callback(clear_semaphores, nc, sems)
        block = ctx.enter_context(nc.Block())

        @block.sync
        def _(sp):
            sp.wait_ge(s_set, 3)
            loads = [(ident[:], d["ident"]), (group[:], d["group"]), (ones4[:], d["ones4"]), (mask4[:], d["mask4"]),
                     (dft_w[:], d["dft_w"]), (dft_h[:], d["dft_h"]), (dft_0[:], d["dft_0"]), (resize[:], d["resize"]),
                     (sel_a[:], d["sel_a"]), (sel_b[:], d["sel_b"]), (fp_rows[:], d["fp_rows"])]
            for g in range(G):
                r = slice(g * CG, (g + 1) * CG)
                loads += [(w1a[r, r], d["w1_t"]), (wpw[r, r], d["w_pw"]), (wpw_t[r, r], d["w_pw_t"]), (wfp[:, r], d["w_fp_t"]),
                          (taps[r, :], d["w_dw"]), (srow[:, 0, r], d["gn_beta_row"])]
                loads += [(vec[r, q:q + 1], d[n]) for q, n in enumerate(("b1", "gn_gamma", "gn_beta", "b_dw", "b_pw", "b_fp"))]
            assert len(loads) == SETUP_LOADS
            for a, b in loads:
                sp.dma_start(a, b).then_inc(s_w, 16)

            def step(i, k, on):
                t = k + STAT + 1
                if on(STAT + 1):
                    if not (isinstance(i, int) and t < 2):
                        wait(sp, "gx_ready", i, t - 2)
                    sp.dma_start(x[t % 2][:], tile_of(d["x1"], i, t)).then_inc(s_x[t % 2], 16)
                if on(OUT + 1):
                    wait(sp, "out_ready", i, k - 1)
                    sp.dma_start(res[(k + 1) % 2][:], tile_of(d["x1"], i, k + 1)).then_inc(s_res[(k + 1) % 2], 16)
                if on(GATE):
                    t = k + GATE
                    wait(sp, "u_padded", i, t, per=3)
                    for tap in range(TAPS):
                        off = tap // 3 * WP + tap % 3
                        r = slice(tap * G, (tap + 1) * G)
                        n = H * WP - 2
                        sp.dma_start(v[t % 2][r, 0:n], up[r, off:off + n]).then_inc(s_shift, 16)
                    wait(sp, "fmap_ready", i, t)
                    sp.dma_start(d["fmap"][t % 2].rearrange("g i j -> i g j"), fmap[:]).then_inc(s_fd, 16)
                    sp.wait_ge(s_fd, i * (UN * 16) + (t + 1) * 16)
                    sp.dma_start(v[t % 2][TAPS * G:TAPS * G + G, :].rearrange("g (i w) -> g i w", w=WP)[:, :, 0:W],
                                 d["fmap"][t % 2]).then_inc(s_v[t % 2], 16)
                if on(OUT):
                    wait(sp, "out_ready", i, k)
                    sp.dma_start(tile_of(d["out"], i, k), out[k % 2][:]).then_inc(s_st[k % 2], 16)

            steps(sp, step)
            for j in range(2):
                sp.wait_ge(s_st[j], NTILES // 2 * 16)

        @block.tensor
        def _(pe):
            credit(pe, "xt_filled gsum_filled y_filled sel_filled yt_filled u_filled z_filled mean_averaged var_averaged "
                       "mean_x2_filled row_filled softmax_filled gates_filled bias_filled fmap_filled")
            pe.wait_ge(s_w, 16 * SETUP_LOADS)
            pe.wait_ge(s_setd, 6)
            pe.matmul(s2_ps, srow[:, 0, :], srow[:, 2, 0:1], start=True, stop=True).then_inc(s_setp, 1)
            pe.wait_ge(s_setd, 7)
            pe.matmul(m2_ps, wpw[:], s1[:], start=True, stop=True)
            pe.matmul(bias_ps, wpw_t[:], vec[:, 3:4], start=True, stop=True)
            pe.matmul(small[0:VROWS, 1, 128:256], fp_rows[:], wfp[:], start=True, stop=True).then_inc(s_setp, 1)
            pe.wait_ge(s_setd, 11)
            pe.matmul(s2_ps, ones4[:], b2[:], start=True, stop=True).then_inc(s_setp, 1)
            pe.wait_ge(s_setd, SETUP_OPS)

            before = [None]
            reader = dict(xt="xt_copied", gsum="gsum_copied", y="y_copied", sel="sigmoid_done", yt="yt_copied",
                          u="u_padded", z="z_squared")

            def take(kind, i, k, e):
                if before[0] is not None:
                    kind0, k0 = before[0]
                    wait(pe, reader[kind0], i, k0, e + 1, 3)
                if e == 2:
                    before[0] = (kind, k)
                return ring[e]

            def shift():
                before[0] = (before[0][0], before[0][1] - UN)
                for b in range(2):
                    small_before[b] = (small_before[b][0], small_before[b][1] - UN)

            small_before = [None, None]
            small_reader = dict(bias="bias_ready", mean="mean_read", x2="mean_x2", gates="gates_ready", var="std_ready",
                                softmax="softmax_ready", fmap="fmap_ready", row="row_shifted")

            def take_small(bank, kind, i, k):
                if small_before[bank] is not None:
                    kind0, k0 = small_before[bank]
                    wait(pe, small_reader[kind0], i, k0)
                small_before[bank] = (kind, k)

            def step(i, k, on):
                f, g = k + FREQ, k + GATE
                if on(FREQ):
                    wait(pe, "gx_ready", i, f)
                    for e in range(3):
                        dst = take("xt", i, f, e)
                        for s in range(8):
                            ins = pe.transpose(dst[0:96, s // 4, s % 4 * P:(s % 4 + 1) * P],
                                               gx[f % UN][:, (8 * e + s) * 96:(8 * e + s + 1) * 96], ident[:])
                        ins.then_inc(S["xt_filled"], 1)
                if on(OUT):
                    wait(pe, "gated_bias", i, k)
                    take_small(0, "bias", i, k)
                    pe.matmul(bias_ps, ones4[:], s2c[:], start=True, stop=True).then_inc(S["bias_filled"], 1)
                    wait(pe, "gated_weights", i, k)
                    for e in range(3):
                        dst = take("gsum", i, k, e)
                        for a in range(2):
                            t = e * LC + a * HB
                            ins = pe.matmul(dst[0:G, a, 0:HB], lhs_g[:], gated[k % 2][:, t:t + HB], start=True, stop=True)
                        ins.then_inc(S["gsum_filled"], 1)
                if on(STAT):
                    wait(pe, "tile_stats", i, k + STAT)
                    take_small(0, "mean", i, k + STAT)
                    pe.matmul(mean_ps, group[:], mv[:, 0:1], start=True, stop=True).then_inc(S["mean_averaged"], 1)
                if on(FREQ):
                    for e in range(3):
                        dst = take("y", i, f, e)
                        wait(pe, "xt_copied", i, f, e + 1, 3)
                        for s in range(8):
                            ins = pe.matmul(dst[:, s // 4, s % 4 * 96:(s % 4 + 1) * 96], xt[:, (8 * e + s) * P:(8 * e + s + 1) * P],
                                            dft_w[:], start=True, stop=True)
                        ins.then_inc(S["y_filled"], 1)
                if on(OUT):
                    for e in range(3):
                        dst = take("sel", i, k, e)
                        if e == 0:
                            shifted(pe, i, k)
                            slot_uses(pe, s_v[k % 2], i, k, 1)
                            wait(pe, "gsum_copied", i, k, per=3)
                        for a in range(2):
                            r = (2 * e + a) * 8
                            ins = pe.matmul(dst[:, a, 0:8 * WP], sel[:], v[k % 2][:, r * WP:(r + 8) * WP], start=True, stop=True)
                        ins.then_inc(S["sel_filled"], 1)
                if on(STAT):
                    wait(pe, "spread_ready", i, k + STAT)
                    take_small(1, "var", i, k + STAT)
                    pe.matmul(var_ps, group[:], spread[:], start=True, stop=True).then_inc(S["var_averaged"], 1)
                if on(FREQ):
                    for e in range(3):
                        dst = take("yt", i, f, e)
                        wait(pe, "y_copied", i, f, per=3)
                        for s in range(8):
                            q = 8 * e + s
                            ins = pe.transpose(dst[0:96, s // 4, s % 4 * P:(s % 4 + 1) * P],
                                               y[:, q, :, :].rearrange("p h r -> p (h r)"), ident[:])
                        ins.then_inc(S["yt_filled"], 1)
                    for e in range(3):
                        dst = take("u", i, f, e)
                        for a in range(2):
                            t = e * LC + a * HB
                            ins = pe.matmul(dst[0:TAPS * G, a, 0:HB], lhs_u[:], gx[f % UN][:, t:t + HB], start=True, stop=True)
                        ins.then_inc(S["u_filled"], 1)
                if on(GATE):
                    wait(pe, "softmax_row", i, g)
                    take_small(1, "softmax", i, g)
                    pe.matmul(s2_ps, srow_t[:], ident[0:1, 0:1], start=True, stop=True).then_inc(S["softmax_filled"], 1)
                if on(FREQ):
                    wait(pe, "mean_dw", i, f)
                    take_small(0, "x2", i, f)
                    pe.matmul(m2_ps, wpw_t[:], mdw[:], start=True, stop=True).then_inc(S["mean_x2_filled"], 1)
                    for e in range(3):
                        dst = take("z", i, f, e)
                        wait(pe, "yt_copied", i, f, min(3, e + 2), 3)
                        for p in range(10 * e, min(10 * e + 10, KW)):
                            o = (p // 5 % 2, p % 5 * 96)
                            if p == 0:
                                ins = pe.matmul(dst[:, 0, 0:192], yt[:, 0:P], dft_0[:], start=True, stop=True)
                            elif p > 1:
                                ins = pe.matmul(dst[:, o[0], o[1]:o[1] + 96], yt[:, (p - 1) * P:p * P], dft_h[:], start=True, stop=True)
                        ins.then_inc(S["z_filled"], 1)
                if on(GATE):
                    wait(pe, "fm_spread", i, g)
                    take_small(1, "fmap", i, g)
                    pe.matmul(fmap_ps, resize[:], fmx[:].rearrange("p g j -> p (g j)"), start=True, stop=True).then_inc(S["fmap_filled"], 1)
                if on(FREQ):
                    wait(pe, "cols_ready", i, f)
                    take_small(0, "gates", i, f)
                    pe.matmul(small[:, 0, 8:8 + H], w1a[:], y[:, 0, :, 0], start=True, stop=True)
                    pe.matmul(small[:, 0, 8 + H:8 + H + W], w1b[:], cols[:], start=True, stop=True).then_inc(S["gates_filled"], 1)
                    take_small(1, "row", i, f)
                    pe.transpose(row_ps, m2[:], ident[:]).then_inc(S["row_filled"], 1)
                if k == UN - 1:
                    shift()

            steps(pe, step)

        @block.vector
        def _(dve):
            dve.memset(w1a[:], 0.0).then_inc(s_set, 1)
            dve.memset(wpw[:], 0.0).then_inc(s_set, 1)
            dve.memset(wpw_t[:], 0.0).then_inc(s_set, 1)
            credit(dve, "y_copied u_padded bn_chunks tile_stats fenced mean_read spread_ready rstd_ready shift_ready cols_ready "
                        "features products mean_dw mean_x2 row_max row_shifted row_sum row_inverse softmax_row softmax_ready "
                        "gated_rows gated_chunks gated_stats gated_rstd gated_scale gated_shift gated_weights gated_bias bias_ready "
                        "fm_ready fm_spread fmap_ready out_ready")
            for t in (up, v[0], v[1]):
                dve.memset(t[:], 0.0).then_inc(s_setd, 1)
            dve.memset(eps[:], EPS)
            dve.memset(feat[:, 9:10], 1.0)
            dve.memset(srow[:, 2, 0:1], 1.0).then_inc(s_setd, 1)
            dve.wait_ge(s_w, 16 * SETUP_LOADS)
            dve.tensor_reduce(smax[:], srow[:, 0, :].rearrange("p (g c) -> p g c", g=G), mybir.AxisListType.X, ALU.max).then_inc(s_setd, 1)
            dve.wait_ge(s_setd, 5)
            dve.tensor_tensor(srow[:, 1, :].rearrange("p (g c) -> p g c", g=G), srow[:, 0, :].rearrange("p (g c) -> p g c", g=G),
                              smax[:].rearrange("p (g o) -> p g o", o=1).broadcast_to([1, G, CG]), ALU.subtract).then_inc(s_set, 1)
            dve.wait_ge(s_seta, 1)
            dve.tensor_reduce(ssum[:], srow[:, 1, :].rearrange("p (g c) -> p g c", g=G), mybir.AxisListType.X, ALU.add).then_inc(s_set, 1)
            dve.wait_ge(s_set, 5)
            dve.reciprocal(srec[:], ssum[:]).then_inc(s_set, 1)
            dve.wait_ge(s_set, 6)
            dve.tensor_tensor(srow[:, 0, :].rearrange("p (g c) -> p g c", g=G), srow[:, 1, :].rearrange("p (g c) -> p g c", g=G),
                              srec[:].rearrange("p (g o) -> p g o", o=1).broadcast_to([1, G, CG]), ALU.mult).then_inc(s_setd, 1)
            dve.wait_ge(s_setp, 1)
            dve.tensor_copy(s1[:], s2_ps).then_inc(s_setd, 1)
            dve.wait_ge(s_setp, 2)
            dve.tensor_copy(vcol[:], m2_ps).then_inc(s_setd, 1)
            dve.tensor_tensor(b2[:], bias_ps, vec[:, 4:5], ALU.add).then_inc(s_setd, 1)
            dve.wait_ge(s_setd, 9)
            dve.tensor_tensor(b2[:], b2[:], s1[:], ALU.mult).then_inc(s_setd, 1)
            dve.tensor_tensor(sel[:], small[0:VROWS, 1, 128:256], sel_a[:], ALU.mult).then_inc(s_setd, 1)
            dve.wait_ge(s_setd, 11)
            dve.tensor_tensor(sel[:], sel[:], sel_b[:], ALU.add).then_inc(s_setd, 1)
            dve.wait_ge(s_setp, 3)
            dve.tensor_tensor(bias0[:], s2_ps, vec[:, 5:6], ALU.add).then_inc(s_setd, 1)
            dve.tensor_scalar(k1[:], taps[:], vcol[:], None, ALU.mult).then_inc(s_setd, 1)
            dve.wait_ge(s_setd, 14)
            dve.tensor_tensor(lhs_u[:].rearrange("p (t g) -> p t g", g=G), k1[:].rearrange("p (t o) -> p t o", o=1).broadcast_to([P, TAPS, G]),
                              mask4[:].rearrange("p (o g) -> p o g", o=1).broadcast_to([P, TAPS, G]), ALU.mult).then_inc(s_setd, 1)
            dve.tensor_scalar(w1b[:], w1a[:], 1.0 / H, None, ALU.mult).then_inc(s_setd, 1)
            t33 = taps[:].rearrange("p (a b) -> p a b", a=3)
            X = mybir.AxisListType.X
            dve.tensor_reduce(coef[:, 0:1], taps[:], X, ALU.add).then_inc(s_setd, 1)
            dve.tensor_reduce(coef[:, 1:2], taps[:, 6:9], X, ALU.add).then_inc(s_setd, 1)
            dve.tensor_reduce(coef[:, 2:3], taps[:, 0:3], X, ALU.add).then_inc(s_setd, 1)
            dve.tensor_reduce(coef[:, 3:4], t33[:, :, 2], X, ALU.add).then_inc(s_setd, 1)
            dve.tensor_reduce(coef[:, 4:5], t33[:, :, 0], X, ALU.add).then_inc(s_setd, 1)
            dve.tensor_scalar(coef[:, 5:6], taps[:, 8:9], 1.0 / L, None, ALU.mult).then_inc(s_setd, 1)
            dve.tensor_scalar(coef[:, 6:7], taps[:, 6:7], 1.0 / L, None, ALU.mult).then_inc(s_setd, 1)
            dve.tensor_scalar(coef[:, 7:8], taps[:, 2:3], 1.0 / L, None, ALU.mult).then_inc(s_setd, 1)
            dve.tensor_scalar(coef[:, 8:9], taps[:, 0:1], 1.0 / L, None, ALU.mult).then_inc(s_setd, 1)
            dve.tensor_copy(coef[:, 9:10], vec[:, 3:4]).then_inc(s_setd, 1)
            dve.wait_ge(s_setd, 26)
            dve.tensor_scalar(coef[:, 0:1], coef[:, 0:1], 1.0 / H, None, ALU.mult).then_inc(s_setd, 1)
            dve.tensor_scalar(coef[:, 1:3], coef[:, 1:3], -1.0 / H, None, ALU.mult).then_inc(s_setd, 1)
            dve.tensor_scalar(coef[:, 3:5], coef[:, 3:5], -1.0 / L, None, ALU.mult).then_inc(s_setd, 1)
            dve.wait_ge(s_setd, SETUP_OPS)

            def groups(t):
                return t.rearrange("p (g c) -> p g c", g=G)

            def spread_of(t):
                return t.rearrange("p (g o) -> p g o", o=1).broadcast_to([1, G, CG])

            def image(t):
                return t.rearrange("p (h w) -> p h w", w=W)

            def step(i, k, on):
                s_, f, g = k + STAT, k + FREQ, k + GATE
                if on(GATE):
                    wait(dve, "row_filled", i, g)
                    dve.tensor_reduce(smax[:], groups(row_ps), X, ALU.max).then_inc(S["row_max"], 1)
                    wait(dve, "row_max", i, g)
                    wait(dve, "softmax_filled", i, g - 1)
                    dve.tensor_tensor(groups(srow_t[:]), groups(row_ps), spread_of(smax[:]), ALU.subtract).then_inc(S["row_shifted"], 1)
                    wait(dve, "gates_ready", i, g)
                    wait(dve, "gsum_filled", i, g - 2, per=3)
                    dve.tensor_tensor(image(gated[g % 2][:]), image(gx[g % UN][:]),
                                      gates[:, 0:H].rearrange("p (h o) -> p h o", o=1).broadcast_to([P, H, W]), ALU.mult
                                      ).then_inc(S["gated_rows"], 1)
                if on(STAT):
                    slot_uses(dve, s_x[s_ % 2], i, s_, 1)
                    wait(dve, "spread_ready", i, s_ - 1)
                    for q in range(6):
                        ins = dve.bn_stats(stats[:, q, :], x[s_ % 2][:, q * HB:(q + 1) * HB])
                    ins.then_inc(S["bn_chunks"], 1)
                    wait(dve, "bn_chunks", i, s_)
                    dve.tensor_copy(chunks_in[:, 0:1], stats[:, 5, 0:1])
                    dve.bn_aggr(mv[:], stats[:].rearrange("p a b -> p (a b)")).then_inc(S["tile_stats"], 1)
                if on(OUT):
                    wait(dve, "bias_filled", i, k)
                    wait(dve, "sigmoid_done", i, k - 1, per=3)
                    dve.tensor_tensor(bias[:], bias_ps, bias0[:], ALU.add).then_inc(S["bias_ready"], 1)
                if on(FREQ):
                    for e in range(3):
                        wait(dve, "y_filled", i, f, e + 1, 3)
                        if e == 0:
                            wait(dve, "gates_filled", i, f - 1)
                        for a in range(2):
                            r = 16 * e + 8 * a
                            ins = dve.tensor_copy(y[:, :, r:r + 8, :].rearrange("p k h r -> p h k r"),
                                                  ring[e][:, a, 0:HB].rearrange("p (h k r) -> p h k r", k=KW - 1, r=2))
                        ins.then_inc(S["y_copied"], 1)
                if on(STAT):
                    wait(dve, "mean_averaged", i, s_)
                    wait(dve, "shift_ready", i, s_ - 1)
                    dve.tensor_copy(gmean[:], mean_ps)
                    dve.tensor_tensor(diff[:], mv[:, 0:1], mean_ps, ALU.subtract).then_inc(S["mean_read"], 1)
                    wait(dve, "mean_read", i, s_)
                    wait(dve, "var_averaged", i, s_ - 1)
                    dve.scalar_tensor_tensor(out=spread[:], in0=diff[:], scalar=diff[:], in1=mv[:, 1:2], op0=ALU.mult,
                                             op1=ALU.add).then_inc(S["spread_ready"], 1)
                if on(GATE):
                    wait(dve, "gated_ready", i, g)
                    for q in range(6):
                        ins = dve.bn_stats(gstats[:, q, :], gated[g % 2][:, q * HB:(q + 1) * HB])
                    ins.then_inc(S["gated_chunks"], 1)
                    wait(dve, "gated_chunks", i, g)
                    dve.tensor_copy(chunks_in[:, 1:2], gstats[:, 5, 0:1])
                    dve.bn_aggr(gmv[:], gstats[:].rearrange("p a b -> p (a b)")).then_inc(S["gated_stats"], 1)
                if on(FREQ):
                    gf = image(gx[f % UN][:])
                    dve.tensor_reduce(cols[:], gf.rearrange("p h w -> p w h"), X, ALU.add).then_inc(S["cols_ready"], 1)
                    wait(dve, "y_copied", i, f, per=3)
                    wait(dve, "products", i, f - 1)
                    dve.tensor_reduce(feat[:, 0:1], y[:, 0, :, 0], X, ALU.add)
                    dve.tensor_copy(feat[:, 1:3], y[:, 0, 0:H:H - 1, 0])
                    dve.tensor_copy(feat[:, 5:9].rearrange("p (a b) -> p a b", a=2), gf[:, 0:H:H - 1, 0:W:W - 1])
                    wait(dve, "cols_ready", i, f)
                    dve.tensor_copy(feat[:, 3:5], cols[:, 0:W:W - 1]).then_inc(S["features"], 1)
                    wait(dve, "features", i, f)
                    dve.tensor_tensor(fprod[:], feat[:], coef[:], ALU.mult).then_inc(S["products"], 1)
                    wait(dve, "products", i, f)
                    wait(dve, "mean_x2_filled", i, f - 1)
                    dve.tensor_reduce(mdw[:], fprod[:], X, ALU.add).then_inc(S["mean_dw"], 1)
                if on(GATE):
                    wait(dve, "row_exp", i, g)
                    dve.tensor_reduce(ssum[:], groups(srow_t[:]), X, ALU.add).then_inc(S["row_sum"], 1)
                    wait(dve, "row_sum", i, g)
                    dve.reciprocal(srec[:], ssum[:]).then_inc(S["row_inverse"], 1)
                    wait(dve, "row_inverse", i, g)
                    dve.tensor_tensor(groups(srow_t[:]), groups(srow_t[:]), spread_of(srec[:]), ALU.mult).then_inc(S["softmax_row"], 1)
                if on(FREQ):
                    for e in range(3):
                        wait(dve, "u_filled", i, f, e + 1, 3)
                        if e == 0:
                            shifted(dve, i, f - 1)
                        dst = up[:].rearrange("p (h w) -> p h w", w=WP)[:, 1 + 16 * e:17 + 16 * e, 1:1 + W]
                        dve.tensor_copy(dst.rearrange("p (a h) w -> p a h w", a=2),
                                        ring[e][0:TAPS * G, :, 0:HB].rearrange("p a (h w) -> p a h w", w=W)).then_inc(S["u_padded"], 1)
                    wait(dve, "mean_x2_filled", i, f)
                    wait(dve, "row_filled", i, f - 1)
                    dve.tensor_tensor(m2[:], m2_ps, vec[:, 4:5], ALU.add).then_inc(S["mean_x2"], 1)
                if on(GATE):
                    wait(dve, "softmax_filled", i, g)
                    dve.tensor_copy(s2[:], s2_ps).then_inc(S["softmax_ready"], 1)
                if on(STAT):
                    wait(dve, "std_ready", i, s_)
                    wait(dve, "gx_ready", i, s_ - 1)
                    dve.reciprocal(rstd[:], std[:]).then_inc(S["rstd_ready"], 1)
                    wait(dve, "rstd_ready", i, s_)
                    dve.scalar_tensor_tensor(out=nb[:], in0=gmean[:], scalar=-1.0, in1=rstd[:], op0=ALU.mult,
                                             op1=ALU.mult).then_inc(S["shift_ready"], 1)
                if on(GATE):
                    wait(dve, "mag_ready", i, g)
                    dve.tensor_reduce(fm[:], mag[:].rearrange("p k h -> p h k"), X, ALU.add).then_inc(S["fm_ready"], 1)
                    wait(dve, "fm_ready", i, g)
                    wait(dve, "fmap_filled", i, g - 1)
                    dve.tensor_tensor(fmx[:], fm[:].rearrange("p (o h) -> p o h", o=1).broadcast_to([P, G, H]),
                                      mask4[:].rearrange("p (g o) -> p g o", o=1).broadcast_to([P, G, H]), ALU.mult
                                      ).then_inc(S["fm_spread"], 1)
                if on(OUT):
                    wait(dve, "product_done", i, k)
                    slot_uses(dve, s_res[k % 2], i, k, 1)
                    dve.tensor_tensor(out[k % 2][:], out[k % 2][:], res[k % 2][:], ALU.add).then_inc(S["out_ready"], 1)
                if on(GATE):
                    wait(dve, "fmap_filled", i, g)
                    if not (isinstance(i, int) and g < 1):
                        dve.wait_ge(s_fd, i * (UN * 16) + g * 16)
                    dve.tensor_copy(fmap[:].rearrange("p g j -> p (g j)"), fmap_ps).then_inc(S["fmap_ready"], 1)
                    wait(dve, "gated_std", i, g)
                    dve.reciprocal(grstd[:], gstd[:]).then_inc(S["gated_rstd"], 1)
                    wait(dve, "gated_rstd", i, g)
                    dve.tensor_tensor(ga[:], grstd[:], vec[:, 1:2], ALU.mult).then_inc(S["gated_scale"], 1)
                    wait(dve, "gated_scale", i, g)
                    wait(dve, "softmax_ready", i, g)
                    dve.tensor_tensor(sa[:], ga[:], s2[:], ALU.mult)
                    dve.scalar_tensor_tensor(out=gc[:], in0=gmv[:, 0:1], scalar=ga[:], in1=vec[:, 2:3], op0=ALU.mult,
                                             op1=ALU.subtract).then_inc(S["gated_shift"], 1)
                    wait(dve, "gated_shift", i, g)
                    wait(dve, "bias_filled", i, g - 1)
                    dve.scalar_tensor_tensor(out=s2c[:], in0=gc[:], scalar=-1.0, in1=s2[:], op0=ALU.mult,
                                             op1=ALU.mult).then_inc(S["gated_bias"], 1)
                    wait(dve, "gsum_filled", i, g - 1, per=3)
                    dve.tensor_scalar(lhs_g[:], mask4[:], sa[:], None, ALU.mult).then_inc(S["gated_weights"], 1)

            steps(dve, step)

        @block.scalar
        def _(act):
            credit(act, "xt_copied gsum_copied sigmoid_done yt_copied z_squared std_ready row_exp gates_ready gated_std mag_ready")
            act.wait_ge(s_w, 16 * SETUP_LOADS)
            act.wait_ge(s_set, 4)
            act.activation(srow[:, 1, :], srow[:, 1, :], ACT.Exp).then_inc(s_seta, 1)
            act.wait_ge(s_setd, SETUP_OPS)

            def step(i, k, on):
                s_, f, g = k + STAT, k + FREQ, k + GATE
                if on(GATE):
                    wait(act, "gates_filled", i, g)
                    wait(act, "gated_ready", i, g - 1)
                    act.activation(gates[:], gates_ps, ACT.Sigmoid, bias=vec[:, 0:1]).then_inc(S["gates_ready"], 1)
                if on(FREQ):
                    for e in range(3):
                        wait(act, "xt_filled", i, f, e + 1, 3)
                        act.activation(two(xt[:, e * 1024:(e + 1) * 1024]), ring[e][0:96, :, :], ACT.Identity).then_inc(S["xt_copied"], 1)
                if on(OUT):
                    for e in range(3):
                        wait(act, "gsum_filled", i, k, e + 1, 3)
                        if e == 0:
                            wait(act, "sel_filled", i, k - 2, per=3)
                        dst = v[k % 2][64:64 + G, :].rearrange("p (h w) -> p h w", w=WP)[:, 16 * e:16 * e + 16, 0:W]
                        act.activation(dst.rearrange("p (a h) w -> p a h w", a=2),
                                       ring[e][0:G, :, 0:HB].rearrange("p a (h w) -> p a h w", w=W), ACT.Identity
                                       ).then_inc(S["gsum_copied"], 1)
                    for e in range(3):
                        wait(act, "sel_filled", i, k, e + 1, 3)
                        if e == 0:
                            wait(act, "bias_ready", i, k)
                            if not (isinstance(i, int) and k < 2):
                                slot_uses(act, s_st[k % 2], i, k - 2, 1)
                        act.activation(out[k % 2][:, e * LC:(e + 1) * LC].rearrange("p (a h w) -> p a h w", a=2, w=W),
                                       ring[e][:, :, 0:8 * WP].rearrange("p a (h w) -> p a h w", w=WP)[:, :, :, 0:W],
                                       ACT.Sigmoid, bias=bias[:]).then_inc(S["sigmoid_done"], 1)
                if on(GATE):
                    wait(act, "row_shifted", i, g)
                    act.activation(srow_t[:], srow_t[:], ACT.Exp).then_inc(S["row_exp"], 1)
                if on(FREQ):
                    for e in range(3):
                        wait(act, "yt_filled", i, f, e + 1, 3)
                        act.activation(two(yt[:, e * 1024:(e + 1) * 1024]), ring[e][0:96, :, :], ACT.Identity).then_inc(S["yt_copied"], 1)
                if on(STAT):
                    wait(act, "var_averaged", i, s_)
                    wait(act, "rstd_ready", i, s_ - 1)
                    act.activation(std[:], var_ps, ACT.Sqrt, bias=eps[:]).then_inc(S["std_ready"], 1)
                if on(GATE):
                    wait(act, "mag2_ready", i, g)
                    act.activation(mag[:], mag[:], ACT.Sqrt).then_inc(S["mag_ready"], 1)
                if on(GATE):
                    wait(act, "gated_stats", i, g)
                    wait(act, "gated_rstd", i, g - 1)
                    act.activation(gstd[:], gmv[:, 1:2], ACT.Sqrt, bias=eps[:]).then_inc(S["gated_std"], 1)
                if on(FREQ):
                    for e in range(3):
                        wait(act, "z_filled", i, f, e + 1, 3)
                        if e == 0:
                            wait(act, "mag2_ready", i, f - 1)
                        n = 2 if e < 2 else 1
                        dst = zsq[:, 10 * e:10 * e + 5 * n, :, :].rearrange("p k r h -> p (k r h)")
                        act.activation(dst.rearrange("p (a n) -> p a n", a=n), ring[e][:, 0:n, 0:480], ACT.Square).then_inc(S["z_squared"], 1)

            steps(act, step)

        @block.gpsimd
        def _(pool):
            credit(pool, "gx_ready gated_ready mag2_ready product_done")
            pool.wait_ge(s_setd, SETUP_OPS)

            def step(i, k, on):
                s_, f, g = k + STAT, k + FREQ, k + GATE
                if on(GATE):
                    wait(pool, "z_squared", i, g, per=3)
                    wait(pool, "fm_ready", i, g - 1)
                    pool.tensor_tensor(mag[:], zsq[:, :, 0, :], zsq[:, :, 1, :], ALU.add).then_inc(S["mag2_ready"], 1)
                    wait(pool, "gated_rows", i, g)
                    t = gated[g % 2][:].rearrange("p (h w) -> p h w", w=W)
                    pool.tensor_tensor(t, t, gates[:, H:H + W].rearrange("p (o w) -> p o w", o=1).broadcast_to([P, H, W]), ALU.mult
                                       ).then_inc(S["gated_ready"], 1)
                if on(OUT):
                    wait(pool, "sigmoid_done", i, k, per=3)
                    pool.tensor_tensor(out[k % 2][:], out[k % 2][:], gx[k % UN][:], ALU.mult).then_inc(S["product_done"], 1)
                if on(STAT):
                    wait(pool, "shift_ready", i, s_)
                    wait(pool, "product_done", i, s_ - UN)
                    pool.tensor_tensor(norm_in[:], rstd[:], nb[:], ALU.mult)
                    pool.tensor_scalar(gx[s_ % UN][:], x[s_ % 2][:], rstd[:], nb[:], ALU.mult, ALU.add).then_inc(S["gx_ready"], 1)

            steps(pool, step)


SETUP_LOADS = 11 + 12 * G
SETUP_OPS = 29


def gate_constants():
    f = np.float32
    eye = np.eye(G)
    w, kk = np.arange(W), np.arange(KW)
    th = 2 * np.pi * np.outer(w, kk) / W
    dw = np.zeros((W, W))
    dw[:, 0], dw[:, 1] = 1, np.cos(th[:, KW - 1])
    dw[:, 2::2], dw[:, 3::2] = np.cos(th[:, 1:KW - 1]), -np.sin(th[:, 1:KW - 1])
    dft_w = np.kron(np.eye(2), dw) / W
    ph = 2 * np.pi * np.outer(np.arange(H), np.arange(H)) / H
    dh = np.zeros((H, 2, 2, H))
    dh[:, 0, 0], dh[:, 0, 1] = np.cos(ph), -np.sin(ph)
    dh[:, 1, 0], dh[:, 1, 1] = np.sin(ph), np.cos(ph)
    d0 = np.zeros((H, 2, 2, 2, H))
    for q in range(2):
        d0[:, q, q, 0], d0[:, q, q, 1] = np.cos(ph), -np.sin(ph)
    pos = np.clip((np.arange(H) + 0.5) * (CG / H) - 0.5, 0, CG - 1)
    lo = np.floor(pos).astype(int)
    hi = np.minimum(lo + 1, CG - 1)
    r = np.zeros((H, CG))
    r[np.arange(H), lo] += 1 - (pos - lo)
    r[np.arange(H), hi] += pos - lo
    mask4 = np.kron(eye, np.ones((CG, 1)))
    sel_a, sel_b = np.zeros((VROWS, P)), np.zeros((VROWS, P))
    rows = np.kron(eye, np.ones((1, CG)))
    sel_b[:TAPS * G] = np.tile(rows, (TAPS, 1))
    sel_a[TAPS * G:TAPS * G + G] = rows
    sel_b[64:] = rows
    fp_rows = np.zeros((CG, VROWS))
    fp_rows[:, TAPS * G:TAPS * G + G] = 1
    c = dict(ident=np.eye(P), group=np.kron(eye, np.ones((CG, CG))) / CG, ones4=np.kron(eye, np.ones((CG, CG))), mask4=mask4,
             dft_w=dft_w, dft_h=dh.reshape(96, 96), dft_0=d0.reshape(96, 192), resize=np.tile(r.T, (G, 1)) / KW,
             sel_a=sel_a, sel_b=sel_b, fp_rows=fp_rows)
    return {k: np.ascontiguousarray(v, dtype=f) for k, v in c.items()}


def scan_constants():
    rows = SPLIT * NBC
    pick = np.zeros((rows, 2 * DB, P), np.float32)
    for r in range(rows):
        k, s = r % NBC, r % DS
        pick[r, k // DS * DB + s // SG, 32 * (s % SG):32 * (s % SG) + 32] = 1
    minus_hi, minus_mid = -np.eye(rows, dtype=np.float32), -np.eye(rows, dtype=np.float32)
    minus_hi[:NBC] = 0
    minus_mid[:2 * NBC] = 0
    return dict(fold=np.tile(np.eye(32, dtype=np.float32), (SG, 1)), ident=np.eye(P, dtype=np.float32),
                pick=pick.reshape(rows, -1), minus_hi=minus_hi, minus_mid=minus_mid)


def build(nc, d, out):
    def scratch(name, shape):
        return nc.dram_tensor(name, shape, fp32, kind="Internal").ap()

    xn, ym = scratch("normed_input", (NTILES, P, L)), scratch("mamba_output", (NTILES, P, L))
    yn, x1 = scratch("normed_output", (NTILES, P, L)), scratch("first_layer", (NTILES, P, L))
    spill, fmap = scratch("delta_spill", (2, 2, P, L)), scratch("frequency_map", (2, G, H, W))

    def rows(t):
        return t.rearrange("n p t -> (n p) t")

    normalise(nc, d, "norm0", d["x"], xn, True)
    mamba(nc, d | dict(xn=rows(xn), ym=rows(ym), spill=spill), B * C // DM // 2)
    normalise(nc, d, "norm1", ym, yn, False)
    project(nc, d, yn, d["x"], x1)
    gated_group(nc, d | dict(x1=x1, fmap=fmap, out=out))


def kernel(x, L0_conv_ln_gamma, L0_conv_ln_beta, L0_conv_skip_scale, L0_conv_in_proj_w, L0_conv_conv_w, L0_conv_conv_b,
           L0_conv_x_proj_w, L0_conv_dt_proj_w, L0_conv_dt_proj_b, L0_conv_A_log, L0_conv_D_p, L0_conv_out_proj_w,
           L0_conv_proj_w, L0_conv_proj_b, L1_conv_w1, L1_conv_b1, L1_conv_gn_gamma, L1_conv_gn_beta, L1_conv_w_dw,
           L1_conv_b_dw, L1_conv_w_pw, L1_conv_b_pw, L1_conv_w_fp, L1_conv_b_fp):
    import concourse.bacc as bacc
    from concourse.bass_utils import run_bass_kernel_spmd

    def column(v):
        return v.reshape(-1, 1)

    x = np.asarray(x)
    arrays = dict(
        x=x.reshape(NTILES, P, L),
        gamma=L0_conv_ln_gamma.reshape(NT, P).T, beta=L0_conv_ln_beta.reshape(NT, P).T,
        skip=L0_conv_skip_scale.reshape(1, 1), win_t=L0_conv_in_proj_w.T, wout_t=L0_conv_out_proj_w.T,
        conv_t=L0_conv_conv_w.T, conv_b=column(L0_conv_conv_b), xproj=L0_conv_x_proj_w, xproj_t=L0_conv_x_proj_w.T,
        dtw_t=L0_conv_dt_proj_w.T, dt_b=column(L0_conv_dt_proj_b), dp=column(L0_conv_D_p),
        a_log=L0_conv_A_log.reshape(DB, 32, DB, SG).transpose(3, 1, 2, 0).reshape(P, DS),
        proj_t=L0_conv_proj_w.T, proj_b=L0_conv_proj_b.reshape(NT, P).T,
        w1_t=L1_conv_w1.T, w_pw=L1_conv_w_pw, w_pw_t=L1_conv_w_pw.T, w_fp_t=L1_conv_w_fp.T,
        w_dw=L1_conv_w_dw.reshape(CG, TAPS), gn_beta_row=L1_conv_gn_beta.reshape(1, CG), b1=column(L1_conv_b1),
        gn_gamma=column(L1_conv_gn_gamma), gn_beta=column(L1_conv_gn_beta), b_dw=column(L1_conv_b_dw),
        b_pw=column(L1_conv_b_pw), b_fp=column(L1_conv_b_fp),
        ones=np.full((P, P), 1 / C, np.float32), **(scan_constants() | gate_constants()))
    arrays = {f"in_{n}": np.ascontiguousarray(a) for n, a in arrays.items()}

    nc = bacc.Bacc("TRN2", target_bir_lowering=False, num_devices=1)
    d = {n[3:]: nc.dram_tensor(n, a.shape, mybir.dt.from_np(a.dtype), kind="ExternalInput").ap() for n, a in arrays.items()}
    out = nc.dram_tensor("out", (NTILES, P, L), fp32, kind="ExternalOutput").ap()
    build(nc, d, out)
    return run_bass_kernel_spmd(nc, [arrays], core_ids=[0]).results[0]["out"].reshape(B, C, H, W)
```

```python
import concourse.bass as bass
from concourse import mybir
from contextlib import ExitStack
import numpy as np

fp32 = mybir.dt.float32
bf16 = mybir.dt.bfloat16
ALU = mybir.AluOpType
ACT = mybir.ActivationFunctionType

B, C, H, W = 8, 1024, 48, 48
L = H * W
P = 128
NT = C // P
DM = 64
DI = 128
DS = 16
RANK = 4
CH = 3
LC = L // CH
HB = LC // 2
NBC = 2 * DS
LOADS = 25
SPLIT = 3


STEPS = CH * DS
PAIR = 2 * STEPS
CREDIT = 96

SG = 4
DB = DI // 32
RUN = DB
DA_RING, DBU_RING = 6, 3
H_RING = 2 * RUN

LEAD_SCAN = 6
LEAD_C = 5
LEAD_KEEP = 5
LEAD_DBU = LEAD_SCAN + DBU_RING
LEAD_DA = LEAD_SCAN + DA_RING
LEAD_BC = LEAD_DBU + 3
LEAD_B = LEAD_BC + 1
GATE_AT, OUT_AT, OUT_READ_AT = DS - 4, DS - 4, DS - 3

PSUM_W = dict(zip((1, 3, 5), (("u", c) for c in range(CH)))) | dict(zip((7, 9, 11), (("z", c) for c in range(CH))))
PSUM_W |= dict(zip((15, 17, 19), (("v", c) for c in range(CH))))
PSUM_W |= dict(zip((21, 23, 25, 31, 33, 35, 37, 39, 41), ((f"p{r}", c) for c in range(CH) for r in range(SPLIT))))
READ_W = {k + 1: e for k, e in PSUM_W.items()}
SILU_AT, LN_AT, DELTA_AT, DU_AT = 12, 20, 23, 25
ORDER = [PSUM_W[k] for k in sorted(PSUM_W)]


def clear_semaphores(nc, sems):
    with nc.Block() as block:
        @block.sync
        def _(sp):
            for s in sems:
                sp.sem_clear(s)





def wait_for(eng, *pairs):
    values = [v if isinstance(v, int) else eng.to_reg(v) for _, v in pairs]
    for (s, _), v in zip(pairs, values):
        eng.wait_ge(s, v)


def mamba(nc, d, pairs):
    with ExitStack() as ctx:
        def sb(name, shape, dt=fp32):
            return ctx.enter_context(nc.sbuf_tensor(name, shape, dt))

        def ps(name):
            return ctx.enter_context(nc.psum_tensor(name, [P, 2, 512], fp32))

        sems = []

        def sem(name):
            sems.append(ctx.enter_context(nc.semaphore(name)))
            return sems[-1]

        w_conv_a, w_conv_b = sb("w_conv_a", [P, DI]), sb("w_conv_b", [P, DI])
        w_z = sb("w_z", [DM, DI])
        w_step = sb("w_step", [DI, DI])
        w_bc = sb("w_bc", [DI, SPLIT * NBC])
        w_out = sb("w_out", [DI, DM])
        w_skip = sb("w_skip", [DM, DM])
        diag_d = sb("diag_d", [P, P])
        ident = sb("ident", [P, P])
        pick = sb("pick", [SPLIT * NBC, 2 * DB, P], bf16)
        fold = sb("fold", [P, 32])
        minus_hi, minus_mid = sb("minus_hi", [96, 96], bf16), sb("minus_mid", [96, 96], bf16)
        conv_b, step_b, d_col, skip_col = (sb(n, [P, 1]) for n in ("conv_b", "step_b", "d_col", "skip_col"))
        a_neg = sb("a_neg", [P, DS])
        xs = [sb(f"xs{j}", [P, 3 + L]) for j in range(2)]
        u = [sb(f"u{j}", [P, L]) for j in range(2)]
        z = [sb(f"z{j}", [P, L]) for j in range(2)]
        parts = [sb(f"parts{j}", [96, L], bf16) for j in range(2)]
        hi, mid = sb("hi", [96, LC], bf16), sb("mid", [96, LC], bf16)
        delta = sb("delta", [P, L])
        du = sb("du", [P, L])
        delta4 = [sb(f"delta4_{j}", [P, DB, LC]) for j in range(2)]
        du4 = [sb(f"du4_{j}", [P, DB, LC]) for j in range(2)]
        da = [sb(f"da{j}", [P, LC]) for j in range(DA_RING)]
        bb = [sb(f"bb{j}", [P, LC]) for j in range(2)]
        dbu = [sb(f"dbu{j}", [P, LC]) for j in range(DBU_RING)]
        h = [sb(f"h{j}", [P, LC + 1]) for j in range(H_RING)]
        carry = sb("carry", [P, DS])
        ym = [sb(f"ym{j}", [DM, LC]) for j in range(2)]
        psum_b, psum_c, psum_y, psum_w = ps("psum_b"), ps("psum_c"), ps("psum_y"), ps("psum_w")
        wt = h[0]

        s_w, s_wd, s_wp, s_wa = (sem(n) for n in ("weights_loaded", "weights_by_vector", "weights_by_tensor", "decay_exp"))
        s_pad = sem("padding_cleared")
        s_xs = [sem("xs0_loaded"), sem("xs1_loaded")]
        s_fill = sem("prelude_filled")
        s_u, s_z, s_v, s_min, s_split = (sem(n) for n in (
            "u_evacuated", "z_evacuated", "v_evacuated", "min_done", "bc_split"))
        s_silu, s_exp, s_ln, s_delta, s_du = (sem(n) for n in (
            "silu_done", "exp_done", "ln_done", "delta_ready", "du_ready"))
        s_spilled = [sem("delta_in_dram"), sem("du_in_dram")]
        s_delta4 = [sem("delta4_0_filled"), sem("delta4_1_filled")]
        s_du4 = [sem("du4_0_filled"), sem("du4_1_filled")]
        s_bb, s_cb, s_y = (sem(n) for n in ("b_broadcast", "c_broadcast", "y_added"))
        s_bc, s_da, s_dbu, s_scan, s_carry, s_mul = (sem(n) for n in (
            "b_copied", "da_ready", "dbu_ready", "scan_done", "carry_kept", "hc_ready"))
        s_gate, s_of, s_oe = (sem(n) for n in ("gated_ready", "out_filled", "out_evacuated"))
        s_st = [sem("ym0_stored"), sem("ym1_stored")]

        def halves(t):
            return t.rearrange("p (a n) -> p a n", a=2)

        def cut(t, c, p=P):
            return t[0:p, c * LC:(c + 1) * LC]

        def banks(t, p=P):
            return t[0:p, :, 0:HB]

        def nth(e):
            return ORDER.index(e) + 1 + CREDIT

        def bodies(eng, body):
            if pairs > 1:
                with eng.Fori(0, pairs - 1) as i:
                    body(i, False)
            body(pairs - 1, True)

        def where(k):
            k %= PAIR
            return k // STEPS, k % STEPS // DS, k % DS // DB, k % DB

        def filled(i, k):
            return i * (3 * DB * 16) + (k // DS // 2 + 1) * DB * 16

        def copied(full, m, j):
            if isinstance(m, int) and m == 0:
                return ()
            return ((full[0], (m - j) * (3 * DB * 8) + 2 * DB * 16 * j), (full[1], (m - j) * (3 * DB * 8) + DB * 16 * j))

        ctx.callback(clear_semaphores, nc, sems)
        block = ctx.enter_context(nc.Block())

        @block.sync
        def _(sp):
            loads = [(w_conv_a[0:DM, :], d["win_t"][:, 0:DI]), (w_conv_a[DM:P, :], d["win_t"][:, 0:DI]),
                     (w_conv_b[0:DM, :], d["win_t"][:, 0:DI]), (w_conv_b[DM:P, :], d["win_t"][:, 0:DI]),
                     (w_z[:], d["win_t"][:, DI:2 * DI]),
                     (w_out[:], d["wout_t"]), (ident[:], d["ident"]), (fold[:], d["fold"]),
                     (z[0][0:96, 0:2 * DB * P], d["pick"]), (z[0][0:96, 1024:1120], d["minus_hi"]),
                     (z[0][0:96, 1120:1216], d["minus_mid"]),
                     (conv_b[:], d["conv_b"]), (step_b[:], d["dt_b"]), (d_col[:], d["dp"]),
                     (skip_col[:], d["skip"].broadcast_to([P, 1])), (a_neg[:], d["a_log"]),
                     (wt[0:RANK, 0:DI], d["xproj"][0:RANK, :]), (wt[0:RANK, DI:2 * DI], d["dtw_t"])]
            loads += [(wt[r * DM:(r + 1) * DM, (2 + q) * DI:(3 + q) * DI], d["conv_t"][3 - 2 * q - r:4 - 2 * q - r, :].broadcast_to([DM, DI]))
                      for q in range(2) for r in range(2)]
            loads += [(w_bc[:, r * NBC:(r + 1) * NBC], d["xproj_t"][:, RANK:RANK + NBC]) for r in range(SPLIT)]
            assert len(loads) == LOADS
            for dst, src in loads:
                sp.dma_start(dst, src).then_inc(s_w, 16)

            def load(n, j):
                sp.dma_start(xs[j][0:DM, 3:3 + L], d["xn"][bass.ds(n * DM, DM), :]).then_inc(s_xs[j], 16)
                sp.dma_start(xs[j][DM:P, 4:3 + L], d["xn"][bass.ds(n * DM, DM), 0:L - 1]).then_inc(s_xs[j], 16)

            def spill(m, j):
                for q, (src, ready, full) in enumerate(((delta, s_delta, s_delta4), (du, s_du, s_du4))):
                    wait_for(sp, (ready, m * 3 + (3 + CREDIT)), *copied(full, m, j))
                    sp.dma_start(d["spill"][q, j], src[:]).then_inc(s_spilled[q], 16)

            def copy4(i, k):
                j, c, _, _ = where(k)
                slot = k // DS % 2
                for q, (dst, used, full) in enumerate(((delta4, s_da, s_delta4), (du4, s_dbu, s_du4))):
                    wait_for(sp, (s_spilled[q], i * 32 + (k // STEPS + 1) * 16), (used, i * PAIR + (k - DS + CREDIT)))
                    for b in range(SG):
                        sp.dma_start(dst[slot][32 * b:32 * b + 32, :, :],
                                     d["spill"][q, j, :, c * LC:(c + 1) * LC].rearrange("(b q) t -> q b t", q=32)
                                     ).then_inc(full[slot], 16)

            sp.wait_ge(s_pad, 4)
            load(0, 0)
            load(1, 1)
            spill(0, 0)
            copy4(0, 0)
            copy4(0, DS)

            def body(i, last):
                for p in range(2):
                    n = i * 2 + p
                    for c in range(CH):
                        if c == 0:
                            copy4(i, p * STEPS + 2 * DS)
                        elif not (last and p == 1):
                            if c == 1:
                                spill(n + 1, 1 - p)
                            copy4(i, p * STEPS + (2 + c) * DS)
                        if c == CH - 1 and not last:
                            sp.wait_ge(s_of, n * 3 + (3 + CREDIT))
                            load(n + 2, p)
                        sp.wait_ge(s_oe, n * 3 + (c + 1 + CREDIT))
                        sp.dma_start(d["ym"][bass.ds(n * DM, DM), c * LC:(c + 1) * LC],
                                     ym[(3 * p + c) % 2][:]).then_inc(s_st[(3 * p + c) % 2], 16)

            bodies(sp, body)
            for j in range(2):
                sp.wait_ge(s_st[j], 16 * 3 * pairs + 16)

        @block.tensor
        def _(pe):
            for s in (s_bb, s_cb, s_y, s_of, s_fill):
                pe.sem_inc(s, CREDIT)
            pe.wait_ge(s_w, 16 * LOADS)
            pe.matmul(psum_b[:, 0, 0:DI], wt[0:RANK, 0:DI], wt[0:RANK, DI:2 * DI], start=True, stop=True).then_inc(s_wp, 1)
            pe.wait_ge(s_wd, 8)

            def freed(e, m, n):
                kind, c = e
                if kind == "u":
                    pe.wait_ge(s_u, m * 3 + (c + 1 + CREDIT))
                elif kind == "z":
                    pe.wait_ge(s_z, m * 3 + (c + 1 + CREDIT))
                elif kind == "v":
                    pe.wait_ge(s_v, m * 3 + (c + 1 + CREDIT))
                elif kind == "o":
                    pe.wait_ge(s_oe, n * 3 + (c + 1 + CREDIT))
                else:
                    pe.wait_ge(s_split, m * 9 + (3 * c + int(kind[1]) + 1 + CREDIT))

            def fill(e, m, j):
                kind, c = e
                for a in range(2):
                    t = c * LC + a * HB
                    now = u[j][:, t:t + HB]
                    if kind == "u":
                        if e == ("u", 0) and a == 0:
                            pe.wait_ge(s_xs[j], (m - j) * 16 + 32)
                        pe.matmul(psum_w[:, a, 0:HB], w_conv_a[:], xs[j][:, 3 + t:3 + t + HB], start=True, stop=False)
                        ins = pe.matmul(psum_w[:, a, 0:HB], w_conv_b[:], xs[j][:, 1 + t:1 + t + HB], start=False, stop=True)
                    elif kind == "z":
                        ins = pe.matmul(psum_w[:, a, 0:HB], w_z[:], xs[j][0:DM, 3 + t:3 + t + HB], start=True, stop=True)
                    elif kind == "v":
                        if a == 0:
                            pe.wait_ge(s_silu, m * 2 + (1 + CREDIT))
                        ins = pe.matmul(psum_w[:, a, 0:HB], w_step[:], now, start=True, stop=True)
                    elif kind == "p0":
                        ins = pe.matmul(psum_w[0:96, a, 0:HB], w_bc[:], now, start=True, stop=True)
                    else:
                        src, minus = (hi, minus_hi) if kind == "p1" else (mid, minus_mid)
                        ins = pe.matmul(psum_w[0:96, a, 0:HB], minus[:], src[:, a * HB:(a + 1) * HB], start=False,
                                        stop=True, skip_group_check=True)
                ins.then_inc(s_fill, 1)

            def b_row(i, k):
                j, c, g, _ = where(k)
                pe.wait_ge(s_bc, i * (PAIR // RUN) + (k // RUN + CREDIT))
                if g == 0:
                    pe.wait_ge(s_split, i * 18 + (k // STEPS * 9 + 3 * c + 3 + CREDIT))
                for a in range(2):
                    t = c * LC + a * HB
                    ins = pe.matmul(psum_b[:, a, 0:HB], pick[:, g, :], parts[j][:, t:t + HB], start=True, stop=True)
                ins.then_inc(s_bb, 1)

            def c_row(i, k):
                j, c, g, _ = where(k)
                pe.wait_ge(s_mul, i * PAIR + (k + CREDIT))
                for a in range(2):
                    t = c * LC + a * HB
                    ins = pe.matmul(psum_c[:, a, 0:HB], pick[:, DB + g, :], parts[j][:, t:t + HB], start=True, stop=True)
                ins.then_inc(s_cb, 1)

            def y_add(i, k):
                j, c, g, _ = where(k)
                if g == 0:
                    pe.wait_ge(s_gate, i * 6 + (k // DS + CREDIT))
                    for a in range(2):
                        pe.matmul(psum_y[:, a, 0:HB], diag_d[:], u[j][:, c * LC + a * HB:c * LC + (a + 1) * HB],
                                  start=True, stop=False)
                pe.wait_ge(s_mul, i * PAIR + (k + RUN + CREDIT))
                for a in range(2):
                    for b in range(DB):
                        ins = pe.matmul(psum_y[32 * b:32 * b + 32, a, 0:HB], fold[:],
                                        h[(k + b) % H_RING][:, a * HB:(a + 1) * HB], start=False, stop=(g == DB - 1),
                                        tile_position=(0, 32 * b))
                ins.then_inc(s_y, 1)

            def out(n, p, c):
                pe.wait_ge(s_gate, n * 3 + (c + 1 + CREDIT))
                for a in range(2):
                    t = 3 + c * LC + a * HB
                    pe.matmul(psum_w[0:DM, a, 0:HB], w_out[:], z[p][:, t - 3:t - 3 + HB], start=True, stop=False)
                    ins = pe.matmul(psum_w[0:DM, a, 0:HB], w_skip[:], xs[p][0:DM, t:t + HB], start=False, stop=True)
                ins.then_inc(s_of, 1)

            for q, e in enumerate(ORDER):
                if q:
                    freed(ORDER[q - 1], 0, 0)
                fill(e, 0, 0)

            def step(i, k, last):
                if (k + LEAD_C) % RUN == 0 and k + LEAD_C >= 0:
                    if not (last and k + LEAD_C >= PAIR):
                        c_row(i, k + LEAD_C)
                    if k + LEAD_C >= RUN and not (last and k + LEAD_C > PAIR):
                        y_add(i, k + LEAD_C - RUN)
                if (k + LEAD_B) % RUN == 0 and k + LEAD_B >= 0 and not (last and k + LEAD_B >= PAIR):
                    b_row(i, k + LEAD_B)

            for k in range(-LEAD_B, 0):
                step(0, k, False)

            def body(i, last):
                for p in range(2):
                    n = i * 2 + p
                    before = None
                    for st in range(STEPS):
                        step(i, p * STEPS + st, last)
                        if not (last and p == 1):
                            for e in [PSUM_W[st]] if st in PSUM_W else ():
                                if before is None:
                                    pe.wait_ge(s_oe, n * 3 + CREDIT)
                                    pe.wait_ge(s_split, n * 9 + (9 + CREDIT))
                                else:
                                    freed(before, n + 1, n)
                                fill(e, n + 1, 1 - p)
                                before = e
                        if st % DS == OUT_AT:
                            if before is not None:
                                freed(before, n + 1, n)
                            else:
                                pe.wait_ge(s_oe, n * 3 + CREDIT)
                                pe.wait_ge(s_split, n * 9 + (9 + CREDIT))
                            out(n, p, st // DS)
                            before = ("o", st // DS)

            bodies(pe, body)

        @block.scalar
        def _(act):
            for s in (s_bc, s_da, s_carry, s_u, s_z, s_v, s_split, s_silu, s_exp, s_ln, s_oe):
                act.sem_inc(s, CREDIT)
            for s in s_st:
                act.sem_inc(s, 16)
            act.wait_ge(s_w, 16 * LOADS)
            act.activation(a_neg[:], a_neg[:], ACT.Exp).then_inc(s_wa, 1)
            act.wait_ge(s_wd, 9)

            def evacuate_u(m, j, c):
                act.wait_ge(s_fill, m * 18 + nth(("u", c)))
                act.wait_ge(s_y, m * (STEPS // RUN) + (CREDIT - PAIR // RUN + 2 * DB + 1))
                act.activation(halves(cut(u[j], c)), banks(psum_w), ACT.Identity, bias=conv_b[:]).then_inc(s_u, 1)

            def evacuate_z(m, j, c):
                act.wait_ge(s_fill, m * 18 + nth(("z", c)))
                act.wait_ge(s_of, m * 3 + (CREDIT - 3))
                act.activation(halves(cut(z[j], c)), banks(psum_w), ACT.Identity).then_inc(s_z, 1)

            def evacuate_v(m, j, c):
                act.wait_ge(s_min, m * 3 + (c + 1 + CREDIT))
                act.wait_ge(s_spilled[0], m * 16)
                act.wait_ge(s_du, m * 3 + CREDIT)
                act.activation(halves(cut(delta, c)), banks(psum_w), ACT.Identity, bias=step_b[:]).then_inc(s_v, 1)

            def silus(m, j):
                act.wait_ge(s_u, m * 3 + (3 + CREDIT))
                act.activation(u[j][:], u[j][:], ACT.Silu).then_inc(s_silu, 1)
                act.wait_ge(s_z, m * 3 + (3 + CREDIT))
                act.activation(z[j][:], z[j][:], ACT.Silu).then_inc(s_silu, 1)

            def split(m, j, r, c):
                act.wait_ge(s_fill, m * 18 + nth((f"p{r}", c)))
                if r == SPLIT - 1:
                    act.wait_ge(s_cb, (m - 1) * (STEPS // RUN) + CREDIT)
                dst = (hi[:], mid[:], cut(parts[j], c, 96))[r]
                act.activation(halves(dst), banks(psum_w, 96), ACT.Identity).then_inc(s_split, 1)

            def softplus(m):
                act.wait_ge(s_min, m * 3 + (3 + CREDIT))
                act.activation(du[:], du[:], ACT.Exp).then_inc(s_exp, 1)
                act.wait_ge(s_exp, m + (1 + CREDIT))
                act.activation(du[:], du[:], ACT.Ln, bias=1.0).then_inc(s_ln, 1)

            def copy_b(i, k):
                run = k // RUN
                act.wait_ge(s_bb, i * (PAIR // RUN) + (run + 1 + CREDIT))
                act.wait_ge(s_dbu, i * PAIR + ((run - 1) * RUN + CREDIT))
                act.activation(halves(bb[run % 2][:]), banks(psum_b), ACT.Identity).then_inc(s_bc, 1)

            def decay(i, k):
                j, c, g, b = where(k)
                r = k % DA_RING
                if g == 0 and b == 0:
                    act.wait_ge(s_delta4[k // DS % 2], filled(i, k))
                act.wait_ge(s_scan, i * PAIR + (k + 1 - DA_RING + CREDIT))
                act.activation(da[r][:], delta4[k // DS % 2][:, b, :], ACT.Exp,
                               scale=a_neg[:, g * DB + b:g * DB + b + 1]).then_inc(s_da, 1)

            def keep(i, k):
                j, c, g, b = where(k)
                act.wait_ge(s_scan, i * PAIR + (k + 1 + CREDIT))
                act.activation(carry[:, g * DB + b:g * DB + b + 1], h[k % H_RING][:, LC:LC + 1], ACT.Identity).then_inc(s_carry, 1)

            def step(i, k, last):
                if (k + LEAD_BC) % RUN == 0 and k + LEAD_BC >= 0 and not (last and k + LEAD_BC >= PAIR):
                    copy_b(i, k + LEAD_BC)
                if k + LEAD_DA >= 0 and not (last and k + LEAD_DA >= PAIR):
                    decay(i, k + LEAD_DA)
                if k + LEAD_KEEP >= 0 and not (last and k + LEAD_KEEP >= PAIR):
                    keep(i, k + LEAD_KEEP)

            def out(n, p, c):
                q = (3 * p + c) % 2
                act.wait_ge(s_of, n * 3 + (c + 1 + CREDIT))
                act.wait_ge(s_st[q], (n - p) * 24 + (16 * ((3 * p + c) // 2) + 16))
                act.activation(halves(ym[q][:]), banks(psum_w, DM), ACT.Identity).then_inc(s_oe, 1)

            for kind, c in ORDER[:2 * CH]:
                (evacuate_u if kind == "u" else evacuate_z)(0, 0, c)
            silus(0, 0)
            for c in range(CH):
                evacuate_v(0, 0, c)
            softplus(0)
            for c in range(CH):
                for r in range(SPLIT):
                    split(0, 0, r, c)
            for k in range(-max(LEAD_BC, LEAD_DA), 0):
                step(0, k, False)

            def body(i, last):
                for p in range(2):
                    n = i * 2 + p
                    for st in range(STEPS):
                        step(i, p * STEPS + st, last)
                        if not (last and p == 1):
                            for kind, c in [READ_W[st]] if st in READ_W else ():
                                if kind == "u":
                                    evacuate_u(n + 1, 1 - p, c)
                                elif kind == "z":
                                    evacuate_z(n + 1, 1 - p, c)
                                elif kind == "v":
                                    evacuate_v(n + 1, 1 - p, c)
                                else:
                                    split(n + 1, 1 - p, int(kind[1]), c)
                            if st == SILU_AT:
                                silus(n + 1, 1 - p)
                            if st == LN_AT:
                                softplus(n + 1)
                        if st % DS == OUT_READ_AT:
                            out(n, p, st // DS)

            bodies(act, body)

        @block.gpsimd
        def _(pool):
            for s in (s_dbu, s_du):
                pool.sem_inc(s, CREDIT)

            def product(m, j, c):
                pool.wait_ge(s_delta, m * 3 + (c + 1 + CREDIT))
                pool.tensor_tensor(cut(du, c), cut(delta, c), cut(u[j], c), ALU.mult).then_inc(s_du, 1)

            def step(i, k):
                j, c, g, b = where(k)
                r = k % DBU_RING
                if b == 0:
                    pool.wait_ge(s_bc, i * (PAIR // RUN) + (k // RUN + 1 + CREDIT))
                    if g == 0:
                        pool.wait_ge(s_du4[k // DS % 2], filled(i, k))
                pool.wait_ge(s_scan, i * PAIR + (k + 1 - DBU_RING + CREDIT))
                pool.tensor_tensor(dbu[r][:], du4[k // DS % 2][:, b, :], bb[k // RUN % 2][:], ALU.mult).then_inc(s_dbu, 1)

            for c in range(CH):
                product(0, 0, c)
            for k in range(LEAD_DBU):
                step(0, k)

            def body(i, last):
                for p in range(2):
                    for st in range(STEPS):
                        k = p * STEPS + st
                        if not (last and k + LEAD_DBU >= PAIR):
                            step(i, k + LEAD_DBU)
                        if not (last and p == 1) and DU_AT <= st < DU_AT + CH:
                            product(i * 2 + (p + 1), 1 - p, st - DU_AT)

            bodies(pool, body)

        @block.vector
        def _(dve):
            for j in range(2):
                dve.memset(xs[j][0:DM, 0:3], 0.0).then_inc(s_pad, 1)
                dve.memset(xs[j][DM:P, 0:4], 0.0).then_inc(s_pad, 1)
            for s in (s_scan, s_mul, s_gate, s_min, s_delta):
                dve.sem_inc(s, CREDIT)
            dve.wait_ge(s_w, 16 * LOADS)
            dve.tensor_copy(pick[:].rearrange("p g q -> p (g q)"), z[0][0:96, 0:1024]).then_inc(s_wd, 1)
            dve.tensor_copy(minus_hi[:], z[0][0:96, 1024:1120]).then_inc(s_wd, 1)
            dve.tensor_copy(minus_mid[:], z[0][0:96, 1120:1216]).then_inc(s_wd, 1)
            dve.tensor_tensor(w_conv_a[:], w_conv_a[:], wt[:, 2 * DI:3 * DI], ALU.mult).then_inc(s_wd, 1)
            dve.tensor_tensor(w_conv_b[:], w_conv_b[:], wt[:, 3 * DI:4 * DI], ALU.mult).then_inc(s_wd, 1)
            dve.tensor_scalar(diag_d[:], ident[:], d_col[:], None, ALU.mult).then_inc(s_wd, 1)
            dve.tensor_scalar(w_skip[:], ident[0:DM, 0:DM], skip_col[0:DM, :], None, ALU.mult).then_inc(s_wd, 1)
            dve.wait_ge(s_wp, 1)
            dve.tensor_copy(w_step[:], psum_b[:, 0, 0:DI]).then_inc(s_wd, 1)
            dve.wait_ge(s_wa, 1)
            dve.tensor_scalar(a_neg[:], a_neg[:], -1.0, None, ALU.mult).then_inc(s_wd, 1)

            def clamp(m, j, c):
                dve.wait_ge(s_fill, m * 18 + nth(("v", c)))
                dve.wait_ge(s_spilled[1], m * 16)
                dve.tensor_scalar(halves(cut(du, c)), banks(psum_w), step_b[:], 40.0, ALU.add, ALU.min).then_inc(s_min, 1)

            def finish_delta(m, c):
                dve.wait_ge(s_ln, m + (1 + CREDIT))
                dve.wait_ge(s_v, m * 3 + (3 + CREDIT))
                dve.tensor_tensor(cut(delta, c), cut(delta, c), cut(du, c), ALU.max).then_inc(s_delta, 1)

            def scan(i, k):
                j, c, g, b = where(k)
                dve.wait_ge(s_da, i * PAIR + (k + 1 + CREDIT))
                dve.wait_ge(s_dbu, i * PAIR + (k + 1 + CREDIT))
                dve.wait_ge(s_carry, i * PAIR + (k + 1 - H_RING + CREDIT))
                dve.wait_ge(s_y, i * (PAIR // RUN) + (k // RUN - 1 + CREDIT))
                dve.tensor_tensor_scan(h[k % H_RING][:, 1:LC + 1], da[k % DA_RING][:], dbu[k % DBU_RING][:],
                                       carry[:, g * DB + b:g * DB + b + 1] if c else 0.0, ALU.mult,
                                       ALU.add).then_inc(s_scan, 1)

            def times_c(i, k):
                dve.wait_ge(s_scan, i * PAIR + (k + 1 + CREDIT))
                if k % RUN == 0:
                    dve.wait_ge(s_cb, i * (PAIR // RUN) + (k // RUN + 1 + CREDIT))
                hk = h[k % H_RING]
                dve.tensor_tensor(halves(hk[:, 0:LC]), halves(hk[:, 1:LC + 1]), banks(psum_c), ALU.mult).then_inc(s_mul, 1)

            def gate(i, n, p, c):
                dve.wait_ge(s_y, i * (PAIR // RUN) + (p * STEPS // RUN + (c + 1) * DB + CREDIT))
                dve.wait_ge(s_silu, n * 2 + (2 + CREDIT))
                zc = halves(cut(z[p], c))
                dve.tensor_tensor(zc, zc, banks(psum_y), ALU.mult).then_inc(s_gate, 1)

            def step(i, k, last):
                if not (last and k + LEAD_SCAN >= PAIR):
                    scan(i, k + LEAD_SCAN)
                if k % DS == GATE_AT and k >= 0:
                    gate(i, i * 2 + k // STEPS, k // STEPS, k % STEPS // DS)
                if k + LEAD_C >= 0 and not (last and k + LEAD_C >= PAIR):
                    times_c(i, k + LEAD_C)

            for c in range(CH):
                clamp(0, 0, c)
            for c in range(CH):
                finish_delta(0, c)
            for k in range(-LEAD_SCAN, 0):
                step(0, k, False)

            def body(i, last):
                for p in range(2):
                    n = i * 2 + p
                    for st in range(STEPS):
                        step(i, p * STEPS + st, last)
                        if not (last and p == 1):
                            for kind, c in [READ_W[st]] if st in READ_W else ():
                                if kind == "v":
                                    clamp(n + 1, 1 - p, c)
                            if DELTA_AT <= st < DELTA_AT + CH:
                                finish_delta(n + 1, st - DELTA_AT)

            bodies(dve, body)

EPS = 1e-5
TG = B // 2


def pair_bodies(eng, body, count=TG):
    with eng.Fori(0, count - 1) as i:
        body(i, False)
    body(count - 1, True)


def normalise(nc, d, name, src, dst):
    with ExitStack() as ctx:
        def sb(n, shape, dt=fp32):
            return ctx.enter_context(nc.sbuf_tensor(f"{name}_{n}", shape, dt))

        sems = []

        def sem(n):
            sems.append(ctx.enter_context(nc.semaphore(f"{name}_{n}")))
            return sems[-1]

        ones, group = sb("ones", [P, P]), sb("group", [P, P])
        gamma, beta = sb("gamma", [P, NT]), sb("beta", [P, NT])
        eps = sb("eps", [P, 1])
        chunks_in = sb("chunks_in", [P, 1])
        x = [[sb(f"x{j}_{k}", [P, L]) for k in range(NT)] for j in range(2)]
        sq = [sb(f"sq{r}", [P, LC]) for r in range(4)]
        rstd = [sb(f"rstd{r}", [P, LC]) for r in range(2)]
        stats, mv = sb("stats", [P, 6, 6]), sb("mv", [P, NT, 2])
        gmean, spread, scale, shift = (sb(n, [P, NT]) for n in ("gmean", "spread", "scale", "shift"))
        psum_mu = [ctx.enter_context(nc.psum_tensor(f"{name}_mu{r}", [P, 2, 512], fp32)) for r in range(2)]
        psum_var = [ctx.enter_context(nc.psum_tensor(f"{name}_var{r}", [P, 2, 512], fp32)) for r in range(2)]
        s_w, s_eps = sem("constants_loaded"), sem("eps_set")
        s_ld, s_st = [sem(f"x{j}_loaded") for j in range(2)], [sem(f"x{j}_stored") for j in range(2)]
        s_bn, s_stat, s_small = sem("bn_chunks"), sem("tile_stats"), sem("group_terms")
        s_bn2, s_lv = sem("spread_terms"), sem("log_variance")
        s_avg, s_rs, s_app = sem("group_averages"), sem("group_rstd"), sem("group_normed")
        s_mu, s_xc, s_sq, s_var = sem("mu_ready"), sem("centred"), sem("squared"), sem("variance_added")
        s_r, s_xn, s_af = sem("rstd_ready"), sem("normed"), sem("scaled")

        def cut(t, c):
            return t[:, c * LC:(c + 1) * LC]

        def halves(t):
            return t.rearrange("p (a n) -> p a n", a=2)

        def banks(t):
            return t[:, :, 0:HB]

        ctx.callback(clear_semaphores, nc, sems)
        block = ctx.enter_context(nc.Block())

        @block.sync
        def _(sp):
            for a, b in ((ones[:], d["ones"]), (group[:], d["group"]), (gamma[:], d["gamma"]), (beta[:], d["beta"])):
                sp.dma_start(a, b).then_inc(s_w, 16)

            def load(n, j, uses, fresh=False):
                if not fresh:
                    sp.wait_ge(s_st[j], uses * (16 * NT * CH))
                for k in range(NT):
                    sp.dma_start(x[j][k][:], src[bass.ds(n * NT + k, 1), :, :].rearrange("a p t -> (a p) t")).then_inc(s_ld[j], 16)

            def store(n, j):
                for c in range(CH):
                    for k in range(NT):
                        sp.wait_ge(s_af, n * 24 + (c * NT + k + 1 + CREDIT))
                        sp.dma_start(dst[bass.ds(n * NT + k, 1), :, c * LC:(c + 1) * LC].rearrange("a p t -> (a p) t"),
                                     cut(x[j][k], c)).then_inc(s_st[j], 16)

            load(0, 0, 0, True)
            load(1, 1, 0, True)

            def body(i, last):
                for j in range(2):
                    store(i * 2 + j, j)
                    if not last:
                        load(i * 2 + j + 2, j, i + 1)

            pair_bodies(sp, body)
            for j in range(2):
                sp.wait_ge(s_st[j], TG * 16 * NT * CH)

        @block.tensor
        def _(pe):
            for s in (s_avg, s_mu, s_var):
                pe.sem_inc(s, CREDIT)
            pe.wait_ge(s_w, 64)

            def average_means(n):
                pe.wait_ge(s_stat, n * NT + (NT + CREDIT))
                pe.wait_ge(s_xc, n * 24 + (CREDIT - NT))
                pe.matmul(psum_mu[1][:, 0, 0:NT], group[:], mv[:, :, 0], start=True, stop=True).then_inc(s_avg, 1)

            def average_spreads(n):
                pe.wait_ge(s_small, n * 3 + (2 + CREDIT))
                pe.matmul(psum_mu[1][:, 1, 0:NT], group[:], spread[:], start=True, stop=True).then_inc(s_avg, 1)

            def mean(n, c):
                r = c % 2
                if c < 2:
                    pe.wait_ge(s_xc, n * 24 + CREDIT)
                    if c == 1:
                        pe.wait_ge(s_small, n * 3 + (3 + CREDIT))
                else:
                    pe.wait_ge(s_xc, n * 24 + (NT + CREDIT))
                for k in range(NT):
                    if c == 0:
                        pe.wait_ge(s_app, n * NT + (k + 1 + CREDIT))
                    for a in range(2):
                        ins = pe.matmul(psum_mu[r][:, a, 0:HB], ones[:], x_of(n, k)[:, c * LC + a * HB:c * LC + (a + 1) * HB],
                                        start=(k == 0), stop=(k == NT - 1))
                ins.then_inc(s_mu, 1)

            def variance(n, c):
                r = c % 2
                pe.wait_ge(s_r, n * 3 + (max(0, c - 1) + CREDIT))
                for k in range(NT):
                    pe.wait_ge(s_sq, n * 24 + (c * NT + k + 1 + CREDIT))
                    for a in range(2):
                        ins = pe.matmul(psum_var[r][:, a, 0:HB], ones[:], sq[k % 4][:, a * HB:(a + 1) * HB],
                                        start=(k == 0), stop=(k == NT - 1))
                    ins.then_inc(s_var, 1)

            slot = [0]

            def x_of(n, k):
                return x[slot[0]][k]

            average_means(0)
            average_spreads(0)

            def body(i, last):
                for j in range(2):
                    n = i * 2 + j
                    slot[0] = j
                    mean(n, 0)
                    mean(n, 1)
                    variance(n, 0)
                    mean(n, 2)
                    variance(n, 1)
                    more = not (last and j == 1)
                    if more:
                        average_means(n + 1)
                    variance(n, 2)
                    if more:
                        average_spreads(n + 1)

            pair_bodies(pe, body)

        @block.vector
        def _(dve):
            for s in (s_bn, s_stat, s_small, s_xc):
                dve.sem_inc(s, CREDIT)
            dve.memset(eps[:], EPS).then_inc(s_eps, 1)

            def statistics(n, j, uses):
                for k in range(NT):
                    if k == 0:
                        dve.wait_ge(s_avg, n * 2 + CREDIT)
                        dve.wait_ge(s_ld[j], uses * (16 * NT) + 16 * NT)
                    dve.wait_ge(s_stat, n * NT + (k + CREDIT))
                    for q in range(6):
                        ins = dve.bn_stats(stats[:, q, :], x[j][k][:, q * HB:(q + 1) * HB])
                    ins.then_inc(s_bn, 1)
                    dve.wait_ge(s_bn, n * NT + (k + 1 + CREDIT))
                    dve.tensor_copy(chunks_in[:], stats[:, 5, 0:1])
                    dve.bn_aggr(mv[:, k, :], stats[:, :, :].rearrange("p a b -> p (a b)")).then_inc(s_stat, 1)

            def group_terms(n):
                dve.wait_ge(s_avg, n * 2 + (1 + CREDIT))
                dve.wait_ge(s_rs, n * 2 + CREDIT)
                dve.tensor_copy(gmean[:], psum_mu[1][:, 0, 0:NT]).then_inc(s_small, 1)
                dve.wait_ge(s_small, n * 3 + (1 + CREDIT))
                dve.tensor_tensor(shift[:], mv[:, :, 0], gmean[:], ALU.subtract).then_inc(s_bn2, 1)
                dve.wait_ge(s_bn2, n * 2 + 1)
                dve.tensor_tensor(shift[:], shift[:], shift[:], ALU.mult).then_inc(s_bn2, 1)
                dve.wait_ge(s_bn2, n * 2 + 2)
                dve.tensor_tensor(spread[:], shift[:], mv[:, :, 1], ALU.add).then_inc(s_small, 1)
                dve.wait_ge(s_rs, n * 2 + (2 + CREDIT))
                dve.scalar_tensor_tensor(out=shift[:], in0=gmean[:], scalar=-1.0, in1=scale[:], op0=ALU.mult,
                                         op1=ALU.mult).then_inc(s_small, 1)

            def centre(n, j, c):
                dve.wait_ge(s_mu, n * 3 + (c + 1 + CREDIT))
                for k in range(NT):
                    xc = halves(cut(x[j][k], c))
                    dve.tensor_tensor(xc, xc, banks(psum_mu[c % 2]), ALU.subtract).then_inc(s_xc, 1)

            statistics(0, 0, 0)
            group_terms(0)

            def body(i, last):
                for j in range(2):
                    n = i * 2 + j
                    more = not (last and j == 1)
                    centre(n, j, 0)
                    centre(n, j, 1)
                    if more:
                        statistics(n + 1, 1 - j, i + j)
                    centre(n, j, 2)
                    if more:
                        group_terms(n + 1)

            pair_bodies(dve, body)

        @block.scalar
        def _(act):
            for s in (s_rs, s_app, s_sq, s_r, s_af, s_lv):
                act.sem_inc(s, CREDIT)
            act.wait_ge(s_w, 64)
            act.wait_ge(s_eps, 1)

            def apply(n, j):
                act.wait_ge(s_avg, n * 2 + (2 + CREDIT))
                act.activation(scale[:], psum_mu[1][:, 1, 0:NT], ACT.Ln, bias=eps[:]).then_inc(s_rs, 1)
                act.wait_ge(s_rs, n * 2 + (1 + CREDIT))
                act.activation(scale[:], scale[:], ACT.Exp, scale=-0.5).then_inc(s_rs, 1)
                act.wait_ge(s_rs, n * 2 + (2 + CREDIT))
                act.wait_ge(s_small, n * 3 + (3 + CREDIT))
                for k in range(NT):
                    act.activation(x[j][k][:], x[j][k][:], ACT.Identity, scale=scale[:, k:k + 1],
                                   bias=shift[:, k:k + 1]).then_inc(s_app, 1)

            def square(n, j, c):
                for k in range(NT):
                    act.wait_ge(s_xc, n * 24 + (c * NT + k + 1 + CREDIT))
                    act.wait_ge(s_var, n * 24 + (c * NT + k - 3 + CREDIT))
                    act.activation(sq[k % 4][:], cut(x[j][k], c), ACT.Square).then_inc(s_sq, 1)

            def root(n, c):
                act.wait_ge(s_var, n * 24 + ((c + 1) * NT + CREDIT))
                act.wait_ge(s_xn, n * 24 + ((c - 1) * NT + CREDIT))
                act.activation(halves(rstd[c % 2][:]), banks(psum_var[c % 2]), ACT.Ln, bias=eps[:]).then_inc(s_lv, 1)
                act.wait_ge(s_lv, n * 3 + (c + 1 + CREDIT))
                act.activation(rstd[c % 2][:], rstd[c % 2][:], ACT.Exp, scale=-0.5).then_inc(s_r, 1)

            def affine(n, j, c):
                for k in range(NT):
                    act.wait_ge(s_xn, n * 24 + (c * NT + k + 1 + CREDIT))
                    act.activation(cut(x[j][k], c), cut(x[j][k], c), ACT.Identity, scale=gamma[:, k:k + 1],
                                   bias=beta[:, k:k + 1]).then_inc(s_af, 1)

            apply(0, 0)

            def body(i, last):
                for j in range(2):
                    n = i * 2 + j
                    square(n, j, 0)
                    root(n, 0)
                    square(n, j, 1)
                    affine(n, j, 0)
                    root(n, 1)
                    square(n, j, 2)
                    affine(n, j, 1)
                    if not (last and j == 1):
                        apply(n + 1, 1 - j)
                    root(n, 2)
                    affine(n, j, 2)

            pair_bodies(act, body)

        @block.gpsimd
        def _(pool):
            pool.sem_inc(s_xn, CREDIT)

            def body(i, last):
                for j in range(2):
                    n = i * 2 + j
                    for c in range(CH):
                        pool.wait_ge(s_r, n * 3 + (c + 1 + CREDIT))
                        for k in range(NT):
                            xc = cut(x[j][k], c)
                            pool.tensor_tensor(xc, xc, rstd[c % 2][:], ALU.mult).then_inc(s_xn, 1)

            pair_bodies(pool, body)


NORM_AT = 5
NORM_STEP = 6


def project(nc, d, src, res, dst):
    with ExitStack() as ctx:
        def sb(n, shape, dt=fp32):
            return ctx.enter_context(nc.sbuf_tensor(f"proj_{n}", shape, dt))

        sems = []

        def sem(n):
            sems.append(ctx.enter_context(nc.semaphore(f"proj_{n}")))
            return sems[-1]

        UNITS = NT * CH
        SLOTS = 3
        ADDS = NT - 1
        w = sb("w", [P, NT, C])
        ones = sb("ones", [P, P])
        bias, gamma, beta, eps = sb("bias", [P, NT]), sb("gamma", [P, NT]), sb("beta", [P, NT]), sb("eps", [P, 1])
        y = [[sb(f"y{j}_{k}", [P, L]) for k in range(NT)] for j in range(2)]
        xin = [sb(f"xin{r}", [P, LC]) for r in range(SLOTS)]
        tsum, sqsum, rstd = sb("tsum", [P, LC]), sb("sqsum", [P, LC]), sb("rstd", [P, LC])
        sq = [sb(f"sq{r}", [P, LC]) for r in range(2)]
        psum = [ctx.enter_context(nc.psum_tensor(f"proj_psum{r}", [P, 2, 512], fp32)) for r in range(2)]
        psum_mu = ctx.enter_context(nc.psum_tensor("proj_psum_mu", [P, 2, 512], fp32))
        psum_var = ctx.enter_context(nc.psum_tensor("proj_psum_var", [P, 2, 512], fp32))
        s_w, s_eps = sem("weights_loaded"), sem("eps_set")
        s_y = [sem(f"y{j}_loaded") for j in range(2)]
        s_x = [sem(f"x{r}_loaded") for r in range(SLOTS)]
        s_st = [sem(f"x{r}_stored") for r in range(SLOTS)]
        s_mm, s_ev = sem("products"), sem("evacuated")
        s_ts, s_mu, s_xc, s_sq = sem("tiles_added"), sem("mean_ready"), sem("centred"), sem("squared")
        s_ss, s_var, s_lv, s_r = sem("squares_added"), sem("variance_ready"), sem("log_variance"), sem("rstd_ready")
        s_xn, s_af = sem("normed"), sem("scaled")

        def cut(t, c):
            return t[:, c * LC:(c + 1) * LC]

        def halves(t):
            return t.rearrange("p (a n) -> p a n", a=2)

        def banks(t):
            return t[:, :, 0:HB]

        def chunk(q, after):
            c, r = divmod(q - NORM_AT - after, NORM_STEP)
            return c if r == 0 and 0 <= c < CH else None

        ctx.callback(clear_semaphores, nc, sems)
        block = ctx.enter_context(nc.Block())

        @block.sync
        def _(sp):
            for t, s in ((ones[:], d["ones"]), (bias[:], d["proj_b"]), (gamma[:], d["gamma"]), (beta[:], d["beta"])):
                sp.dma_start(t, s).then_inc(s_w, 16)

            def load(n, j):
                sp.wait_ge(s_mm, n * UNITS + (CREDIT - UNITS))
                for k in range(NT):
                    sp.dma_start(y[j][k][:], src[bass.ds(n * NT + k, 1), :, :].rearrange("a p t -> (a p) t")).then_inc(s_y[j], 16)

            def free(n, q):
                return s_st[q % SLOTS], n * (UNITS // SLOTS * 16) + (q // SLOTS + 1) * 16

            def residual(n, q):
                m, c = divmod(q % UNITS, CH)
                sp.dma_start(xin[q % SLOTS][:], res[bass.ds(n * NT + (q // UNITS * NT + m), 1), :, c * LC:(c + 1) * LC]
                             .rearrange("a p t -> (a p) t")).then_inc(s_x[q % SLOTS], 16)

            load(0, 0)
            for k in range(NT):
                sp.dma_start(w[:, k, :], d["proj_t"][k * P:(k + 1) * P, :]).then_inc(s_w, 16)
            for q in range(2):
                residual(0, q)

            def body(i, last):
                for j in range(2):
                    n = i * 2 + j
                    if not (last and j == 1):
                        load(n + 1, 1 - j)
                    for q in range(UNITS):
                        m, c = divmod(q, CH)
                        ready = s_ev, n * UNITS + (q + 1 + CREDIT)
                        if not (last and j == 1 and q + 2 >= UNITS):
                            wait_for(sp, ready, free(n, q + 2))
                            residual(n, q + 2)
                        else:
                            wait_for(sp, ready)
                        sp.dma_start(dst[bass.ds(n * NT + m, 1), :, c * LC:(c + 1) * LC].rearrange("a p t -> (a p) t"),
                                     xin[q % SLOTS][:]).then_inc(s_st[q % SLOTS], 16)

            pair_bodies(sp, body)
            for r in range(SLOTS):
                sp.wait_ge(s_st[r], (B * UNITS // SLOTS + 1) * 16)

        @block.tensor
        def _(pe):
            for s in (s_mm, s_mu, s_var):
                pe.sem_inc(s, CREDIT)
            pe.wait_ge(s_w, 16 * (NT + 4))

            def mean(n, c):
                pe.wait_ge(s_ts, n * (CH * ADDS) + ((c + 1) * ADDS + CREDIT))
                pe.wait_ge(s_xc, n * (CH * NT) + (c * NT + CREDIT))
                for a in range(2):
                    ins = pe.matmul(psum_mu[:, a, 0:HB], ones[:], tsum[:, a * HB:(a + 1) * HB], start=True, stop=True)
                ins.then_inc(s_mu, 1)

            def variance(n, c):
                pe.wait_ge(s_ss, n * (CH * ADDS) + ((c + 1) * ADDS + CREDIT))
                pe.wait_ge(s_lv, n * CH + (c + CREDIT))
                for a in range(2):
                    ins = pe.matmul(psum_var[:, a, 0:HB], ones[:], sqsum[:, a * HB:(a + 1) * HB], start=True, stop=True)
                ins.then_inc(s_var, 1)

            for c in range(CH):
                mean(0, c)
                variance(0, c)

            def body(i, last):
                for j in range(2):
                    n = i * 2 + j
                    pe.wait_ge(s_af, n * (CH * NT) + (CH * NT + CREDIT))
                    for q in range(UNITS):
                        m, c = divmod(q, CH)
                        pe.wait_ge(s_ev, n * UNITS + (q - 1 + CREDIT))
                        for k in range(NT):
                            for a in range(2):
                                t = c * LC + a * HB
                                ins = pe.matmul(psum[q % 2][:, a, 0:HB], w[:, k, m * P:(m + 1) * P], y[j][k][:, t:t + HB],
                                                start=(k == 0), stop=(k == NT - 1))
                        ins.then_inc(s_mm, 1)
                        if not (last and j == 1):
                            if chunk(q, 0) is not None:
                                mean(n + 1, chunk(q, 0))
                            if chunk(q, 3) is not None:
                                variance(n + 1, chunk(q, 3))

            pair_bodies(pe, body)

        @block.vector
        def _(dve):
            for s in (s_ev, s_xc, s_ss):
                dve.sem_inc(s, CREDIT)
            dve.memset(eps[:], EPS).then_inc(s_eps, 1)
            dve.wait_ge(s_w, 16 * (NT + 4))

            def centre(n, j, c):
                dve.wait_ge(s_mu, n * CH + (c + 1 + CREDIT))
                for k in range(NT):
                    yc = halves(cut(y[j][k], c))
                    dve.tensor_tensor(yc, yc, banks(psum_mu), ALU.subtract).then_inc(s_xc, 1)

            def add_squares(n, c, ops):
                for a in ops:
                    if a == 0:
                        dve.wait_ge(s_var, n * CH + (c + CREDIT))
                    dve.wait_ge(s_sq, n * (CH * NT) + (c * NT + a + 2 + CREDIT))
                    dve.wait_ge(s_ss, n * (CH * ADDS) + (c * ADDS + a + CREDIT))
                    dve.tensor_tensor(sqsum[:], (sqsum if a else sq[0])[:], sq[(a + 1) % 2][:], ALU.add).then_inc(s_ss, 1)

            for c in range(CH):
                centre(0, 0, c)
                add_squares(0, c, range(ADDS))

            def body(i, last):
                for j in range(2):
                    n = i * 2 + j
                    for q in range(UNITS):
                        m, r = q // CH, q % SLOTS
                        dve.wait_ge(s_mm, n * UNITS + (q + 1 + CREDIT))
                        dve.wait_ge(s_x[r], n * (UNITS // SLOTS * 16) + (q // SLOTS + 1) * 16)
                        xr = halves(xin[r][:])
                        dve.scalar_tensor_tensor(out=xr, in0=banks(psum[q % 2]), scalar=bias[:, m:m + 1], in1=xr,
                                                 op0=ALU.add, op1=ALU.add).then_inc(s_ev, 1)
                        if not (last and j == 1):
                            if chunk(q, 0) is not None:
                                centre(n + 1, 1 - j, chunk(q, 0))
                            if chunk(q, 1) is not None:
                                add_squares(n + 1, chunk(q, 1), range(0, 4))
                            if chunk(q, 2) is not None:
                                add_squares(n + 1, chunk(q, 2), range(4, ADDS))

            pair_bodies(dve, body)

        @block.scalar
        def _(act):
            for s in (s_sq, s_lv, s_r, s_af):
                act.sem_inc(s, CREDIT)
            act.wait_ge(s_w, 16 * (NT + 4))
            act.wait_ge(s_eps, 1)

            def norm(n, j, c):
                for k in range(NT):
                    act.wait_ge(s_xc, n * (CH * NT) + (c * NT + k + 1 + CREDIT))
                    act.wait_ge(s_ss, n * (CH * ADDS) + (c * ADDS + (max(1, k - 2) if k > 1 else 0) + CREDIT))
                    act.activation(sq[k % 2][:], cut(y[j][k], c), ACT.Square).then_inc(s_sq, 1)
                act.wait_ge(s_var, n * CH + (c + 1 + CREDIT))
                act.wait_ge(s_xn, n * (CH * NT) + (c * NT + CREDIT))
                act.activation(halves(rstd[:]), banks(psum_var), ACT.Ln, bias=eps[:]).then_inc(s_lv, 1)
                act.wait_ge(s_lv, n * CH + (c + 1 + CREDIT))
                act.activation(rstd[:], rstd[:], ACT.Exp, scale=-0.5).then_inc(s_r, 1)
                for k in range(NT):
                    act.wait_ge(s_xn, n * (CH * NT) + (c * NT + k + 1 + CREDIT))
                    act.activation(cut(y[j][k], c), cut(y[j][k], c), ACT.Identity, scale=gamma[:, k:k + 1],
                                   bias=beta[:, k:k + 1]).then_inc(s_af, 1)

            for c in range(CH):
                norm(0, 0, c)

            def body(i, last):
                for j in range(2):
                    if not (last and j == 1):
                        for c in range(CH):
                            norm(i * 2 + j + 1, 1 - j, c)

            pair_bodies(act, body)

        @block.gpsimd
        def _(pool):
            for s in (s_ts, s_xn):
                pool.sem_inc(s, CREDIT)
            for s in s_st:
                pool.sem_inc(s, 16)

            def norm(n, j, c, uses):
                for a in range(ADDS):
                    if a == 0:
                        if c == 0:
                            pool.wait_ge(s_y[j], uses * (16 * NT) + 16 * NT)
                        pool.wait_ge(s_mu, n * CH + (c + CREDIT))
                    pool.wait_ge(s_ts, n * (CH * ADDS) + (c * ADDS + a + CREDIT))
                    pool.tensor_tensor(tsum[:], tsum[:] if a else cut(y[j][0], c), cut(y[j][a + 1], c), ALU.add).then_inc(s_ts, 1)
                pool.wait_ge(s_r, n * CH + (c + 1 + CREDIT))
                for k in range(NT):
                    yc = cut(y[j][k], c)
                    pool.tensor_tensor(yc, yc, rstd[:], ALU.mult).then_inc(s_xn, 1)

            for c in range(CH):
                norm(0, 0, c, 0)

            def body(i, last):
                for j in range(2):
                    if not (last and j == 1):
                        for c in range(CH):
                            norm(i * 2 + j + 1, 1 - j, c, i + j)

            pair_bodies(pool, body)

G = 4
CG = P // G
KW = W // 2 + 1
NTILES = B * NT
WP = W + 2
TAPS = 9
VROWS = 68
UN = 4
STAT, FREQ, GATE, OUT, DONE = 3, 2, 1, 0, -1


def gated_group(nc, d):
    with ExitStack() as ctx:
        def sb(n, shape, dt=fp32):
            return ctx.enter_context(nc.sbuf_tensor(f"gate_{n}", shape, dt))

        sems = []

        def sem(n):
            sems.append(ctx.enter_context(nc.semaphore(f"gate_{n}")))
            return sems[-1]

        def ps(n):
            return ctx.enter_context(nc.psum_tensor(f"gate_{n}", [P, 2, 512], fp32))

        ident, group, ones4 = sb("ident", [P, P]), sb("group", [P, P]), sb("ones4", [P, P])
        mask4 = sb("mask4", [P, G])
        dft_w, dft_h, dft_0 = sb("dft_w", [96, 96]), sb("dft_h", [96, 96]), sb("dft_0", [96, 192])
        resize = sb("resize", [P, H])
        sel_a, sel_b, sel = sb("sel_a", [VROWS, P]), sb("sel_b", [VROWS, P]), sb("sel", [VROWS, P])
        fp_rows, wfp = sb("fp_rows", [CG, VROWS]), sb("wfp", [CG, P])
        w1a, w1b = sb("w1a", [P, P]), sb("w1b", [P, P])
        wpw, wpw_t = sb("wpw", [P, P]), sb("wpw_t", [P, P])
        taps = sb("taps", [P, TAPS])
        vec = sb("vec", [P, 6])
        srow = sb("srow", [1, 3, P])
        s1 = sb("s1", [P, 1])
        vcol, k1, b2, bias0 = sb("vcol", [P, 1]), sb("k1", [P, TAPS]), sb("b2", [P, 1]), sb("bias0", [P, 1])
        lhs_u = sb("lhs_u", [P, TAPS * G])
        coef = sb("coef", [P, 10])
        eps = sb("eps", [P, 1])
        x = [sb(f"x{j}", [P, L]) for j in range(2)]
        res = [sb(f"res{j}", [P, L]) for j in range(2)]
        gx = [sb(f"gx{j}", [P, L]) for j in range(UN)]
        gated = [sb(f"gated{j}", [P, L]) for j in range(2)]
        out = [sb(f"out{j}", [P, L]) for j in range(2)]
        xt = sb("xt", [96, 24 * P])
        y = sb("y", [P, KW - 1, H, 2])
        yt = sb("yt", [96, 24 * P])
        zsq = sb("zsq", [P, KW, 2, H])
        mag = sb("mag", [P, KW, H])
        up = sb("up", [TAPS * G, (H + 2) * WP])
        v = [sb(f"v{j}", [VROWS, H * WP]) for j in range(2)]
        fmap = sb("fmap", [H, G, W])
        stats, mv = sb("stats", [P, 6, 6]), sb("mv", [P, 2])
        gmean, diff, spread, std, rstd, nb = (sb(n, [P, 1]) for n in ("gmean", "diff", "spread", "std", "rstd", "nb"))
        gstats, gmv = sb("gstats", [P, 6, 6]), sb("gmv", [P, 2])
        gstd, grstd, ga, gc, sa, s2c = (sb(n, [P, 1]) for n in ("gstd", "grstd", "ga", "gc", "sa", "s2c"))
        chunks_in = sb("chunks_in", [P, 2])
        norm_in = sb("norm_in", [P, 1])
        cols = sb("cols", [P, W])
        feat, fprod, mdw, m2 = sb("feat", [P, 10]), sb("fprod", [P, 10]), sb("mdw", [P, 1]), sb("m2", [P, 1])
        srow_t = sb("srow_t", [1, P])
        smax, ssum, srec = (sb(n, [1, G]) for n in ("smax", "ssum", "srec"))
        s2 = sb("s2", [P, 1])
        gates = sb("gates", [P, H + W])
        fm, fmx = sb("fm", [P, H]), sb("fmx", [P, G, H])
        lhs_g = sb("lhs_g", [P, G])
        bias = sb("bias", [P, 1])
        ring = [ps(f"ring{r}") for r in range(3)]
        small = ps("small")
        mean_ps, m2_ps, bias_ps, gates_ps = small[:, 0, 0:1], small[:, 0, 1:2], small[:, 0, 2:3], small[:, 0, 8:8 + H + W]
        var_ps, s2_ps = small[:, 1, 0:1], small[:, 1, 1:2]
        row_ps, fmap_ps = small[0:1, 1, 128:256], small[0:H, 1, 256:256 + G * W]

        names = ("xt_filled xt_copied gsum_filled gsum_copied y_filled y_copied sel_filled sigmoid_done yt_filled yt_copied "
                 "u_filled u_padded z_filled z_squared "
                 "bn_chunks tile_stats fenced mean_averaged mean_read spread_ready var_averaged std_ready rstd_ready shift_ready "
                 "gx_ready cols_ready features products mean_dw mean_x2_filled mean_x2 row_filled row_max row_shifted "
                 "row_exp row_sum row_inverse softmax_row softmax_filled softmax_ready gates_filled gates_ready gated_rows "
                 "gated_ready gated_chunks gated_stats gated_std gated_rstd gated_scale gated_shift gated_weights gated_bias "
                 "bias_filled bias_ready mag2_ready mag_ready fm_ready fm_spread fmap_filled fmap_ready product_done out_ready")
        S = {n: sem(n) for n in names.split()}
        s_w, s_set, s_setd, s_seta, s_setp = (sem(n) for n in (
            "weights_loaded", "cleared", "set_by_vector", "set_by_scalar", "set_by_tensor"))
        s_x, s_res, s_st, s_v = ([sem(f"{n}{j}") for j in range(2)] for n in ("x_loaded", "res_loaded", "stored", "fmap_loaded"))
        s_fd, s_shift = sem("fmap_in_dram"), sem("taps_shifted")

        def wait(eng, name, i, k, n=None, per=1):
            eng.wait_ge(S[name], i * (UN * per) + (k * per + (per if n is None else n) + CREDIT))

        def slot_uses(eng, s, i, k, each):
            eng.wait_ge(s, i * (UN // 2 * each * 16) + (k // 2 + 1) * each * 16)

        def shifted(eng, i, k):
            if k >= 0 or not isinstance(i, int):
                eng.wait_ge(s_shift, i * (UN * TAPS * 16) + (k + 1) * TAPS * 16)

        def steps(eng, step):
            bodies = NTILES // UN
            for k in range(-STAT - 1, 1):
                step(0, k, lambda a, k=k: k + a >= 0)
            if bodies > 2:
                with eng.Fori(0, bodies - 2) as i:
                    for k in range(1, UN + 1):
                        step(i, k, lambda a: True)
            for left in (2, 1):
                for k in range(1, UN + 1):
                    step(bodies - left, k, lambda a, k=k, left=left: k + a < left * UN)

        def credit(eng, names):
            for n in names.split():
                eng.sem_inc(S[n], CREDIT)

        def two(t):
            return t.rearrange("p (a n) -> p a n", a=2)

        def tile_of(ap, i, k):
            return ap[bass.ds(i * UN + k, 1), :, :].rearrange("a p t -> (a p) t")

        ctx.callback(clear_semaphores, nc, sems)
        block = ctx.enter_context(nc.Block())

        @block.sync
        def _(sp):
            sp.wait_ge(s_set, 3)
            loads = [(ident[:], d["ident"]), (group[:], d["group"]), (ones4[:], d["ones4"]), (mask4[:], d["mask4"]),
                     (dft_w[:], d["dft_w"]), (dft_h[:], d["dft_h"]), (dft_0[:], d["dft_0"]), (resize[:], d["resize"]),
                     (sel_a[:], d["sel_a"]), (sel_b[:], d["sel_b"]), (fp_rows[:], d["fp_rows"])]
            for g in range(G):
                r = slice(g * CG, (g + 1) * CG)
                loads += [(w1a[r, r], d["w1_t"]), (wpw[r, r], d["w_pw"]), (wpw_t[r, r], d["w_pw_t"]), (wfp[:, r], d["w_fp_t"]),
                          (taps[r, :], d["w_dw"]), (srow[:, 0, r], d["gn_beta_row"])]
                loads += [(vec[r, q:q + 1], d[n]) for q, n in enumerate(("b1", "gn_gamma", "gn_beta", "b_dw", "b_pw", "b_fp"))]
            assert len(loads) == SETUP_LOADS
            for a, b in loads:
                sp.dma_start(a, b).then_inc(s_w, 16)

            def step(i, k, on):
                t = k + STAT + 1
                if on(STAT + 1):
                    if not (isinstance(i, int) and t < 2):
                        wait(sp, "gx_ready", i, t - 2)
                    sp.dma_start(x[t % 2][:], tile_of(d["x1"], i, t)).then_inc(s_x[t % 2], 16)
                if on(GATE):
                    t = k + GATE
                    wait_for(sp, (S["u_padded"], i * (UN * 3) + (t * 3 + 3 + CREDIT)),
                             (S["sel_filled"], i * (UN * 3) + ((t - 2) * 3 + 3 + CREDIT)))
                    for tap in range(TAPS):
                        off = tap // 3 * WP + tap % 3
                        r = slice(tap * G, (tap + 1) * G)
                        n = H * WP - 2
                        sp.dma_start(v[t % 2][r, 0:n], up[r, off:off + n]).then_inc(s_shift, 16)
                    wait(sp, "fmap_ready", i, t)
                    sp.dma_start(d["fmap"][t % 2].rearrange("g i j -> i g j"), fmap[:]).then_inc(s_fd, 16)
                    sp.wait_ge(s_fd, i * (UN * 16) + (t + 1) * 16)
                    sp.dma_start(v[t % 2][TAPS * G:TAPS * G + G, :].rearrange("g (i w) -> g i w", w=WP)[:, :, 0:W],
                                 d["fmap"][t % 2]).then_inc(s_v[t % 2], 16)
                if on(DONE):
                    wait(sp, "out_ready", i, k - 1)
                    sp.dma_start(tile_of(d["out"], i, k - 1), out[(k - 1) % 2][:]).then_inc(s_st[(k - 1) % 2], 16)
                if on(OUT + 1):
                    sp.dma_start(res[(k + 1) % 2][:], tile_of(d["x1"], i, k + 1)).then_inc(s_res[(k + 1) % 2], 16)

            steps(sp, step)
            for j in range(2):
                sp.wait_ge(s_st[j], NTILES // 2 * 16 + 16)

        @block.tensor
        def _(pe):
            credit(pe, "xt_filled gsum_filled y_filled sel_filled yt_filled u_filled z_filled mean_averaged var_averaged "
                       "mean_x2_filled row_filled softmax_filled gates_filled bias_filled fmap_filled")
            pe.wait_ge(s_w, 16 * SETUP_LOADS)
            pe.wait_ge(s_setd, 6)
            pe.matmul(s2_ps, srow[:, 0, :], srow[:, 2, 0:1], start=True, stop=True).then_inc(s_setp, 1)
            pe.wait_ge(s_setd, 7)
            pe.matmul(m2_ps, wpw[:], s1[:], start=True, stop=True)
            pe.matmul(bias_ps, wpw_t[:], vec[:, 3:4], start=True, stop=True)
            pe.matmul(small[0:VROWS, 1, 128:256], fp_rows[:], wfp[:], start=True, stop=True).then_inc(s_setp, 1)
            pe.wait_ge(s_setd, 11)
            pe.matmul(s2_ps, ones4[:], b2[:], start=True, stop=True).then_inc(s_setp, 1)
            pe.wait_ge(s_setd, SETUP_OPS)

            before = [()]
            reader = dict(xt="xt_copied", gsum="gsum_copied", y="y_copied", sel="sigmoid_done", yt="yt_copied",
                          u="u_padded", z="z_squared")

            def take(i, e, *users):
                for kind0, k0 in before[0]:
                    wait(pe, reader[kind0], i, k0, e + 1, 3)
                if e == 2:
                    before[0] = users
                return ring[e]

            def shift():
                before[0] = tuple((kind, k - UN) for kind, k in before[0])
                for b in range(2):
                    small_before[b] = (small_before[b][0], small_before[b][1] - UN)

            small_before = [None, None]
            small_reader = dict(bias="bias_ready", mean="mean_read", x2="mean_x2", gates="gates_ready", var="std_ready",
                                softmax="softmax_ready", fmap="fmap_ready", row="row_shifted")

            def take_small(bank, kind, i, k):
                if small_before[bank] is not None:
                    kind0, k0 = small_before[bank]
                    wait(pe, small_reader[kind0], i, k0)
                small_before[bank] = (kind, k)

            def step(i, k, on):
                f, g = k + FREQ, k + GATE
                if on(FREQ):
                    wait(pe, "gx_ready", i, f)
                    for e in range(3):
                        dst = take(i, e, ("xt", f))
                        for s in range(8):
                            ins = pe.transpose(dst[0:96, s // 4, s % 4 * P:(s % 4 + 1) * P],
                                               gx[f % UN][:, (8 * e + s) * 96:(8 * e + s + 1) * 96], ident[:])
                        ins.then_inc(S["xt_filled"], 1)
                if on(OUT):
                    wait(pe, "gated_bias", i, k)
                    take_small(0, "bias", i, k)
                    pe.matmul(bias_ps, ones4[:], s2c[:], start=True, stop=True).then_inc(S["bias_filled"], 1)
                if on(FREQ):
                    for e in range(3):
                        dst = take(i, e, ("y", f))
                        wait(pe, "xt_copied", i, f, e + 1, 3)
                        for s in range(8):
                            ins = pe.matmul(dst[:, s // 4, s % 4 * 96:(s % 4 + 1) * 96], xt[:, (8 * e + s) * P:(8 * e + s + 1) * P],
                                            dft_w[:], start=True, stop=True)
                        ins.then_inc(S["y_filled"], 1)
                if on(STAT):
                    wait(pe, "tile_stats", i, k + STAT)
                    take_small(0, "mean", i, k + STAT)
                    pe.matmul(mean_ps, group[:], mv[:, 0:1], start=True, stop=True).then_inc(S["mean_averaged"], 1)
                if on(FREQ):
                    for e in range(3):
                        dst = take(i, e, ("yt", f))
                        wait(pe, "y_copied", i, f, per=3)
                        for s in range(8):
                            q = 8 * e + s
                            ins = pe.transpose(dst[0:96, s // 4, s % 4 * P:(s % 4 + 1) * P],
                                               y[:, q, :, :].rearrange("p h r -> p (h r)"), ident[:])
                        ins.then_inc(S["yt_filled"], 1)
                if on(STAT):
                    wait(pe, "spread_ready", i, k + STAT)
                    take_small(1, "var", i, k + STAT)
                    pe.matmul(var_ps, group[:], spread[:], start=True, stop=True).then_inc(S["var_averaged"], 1)
                users = (("u", f),) * on(FREQ) + (("gsum", k),) * on(OUT)
                if on(OUT):
                    wait(pe, "gated_weights", i, k)
                for e in range(3 if users else 0):
                    dst = take(i, e, *users)
                    for a in range(2):
                        t = e * LC + a * HB
                        if on(FREQ):
                            taps_in = pe.matmul(dst[0:TAPS * G, a, 0:HB], lhs_u[:], gx[f % UN][:, t:t + HB], start=True, stop=True)
                        if on(OUT):
                            gated_in = pe.matmul(dst[64:64 + G, a, 0:HB], lhs_g[:], gated[k % 2][:, t:t + HB], start=True,
                                                 stop=True, tile_position=(0, 64))
                    if on(FREQ):
                        taps_in.then_inc(S["u_filled"], 1)
                    if on(OUT):
                        gated_in.then_inc(S["gsum_filled"], 1)
                if on(GATE):
                    wait(pe, "softmax_row", i, g)
                    take_small(1, "softmax", i, g)
                    pe.matmul(s2_ps, srow_t[:], ident[0:1, 0:1], start=True, stop=True).then_inc(S["softmax_filled"], 1)
                if on(FREQ):
                    wait(pe, "mean_dw", i, f)
                    take_small(0, "x2", i, f)
                    pe.matmul(m2_ps, wpw_t[:], mdw[:], start=True, stop=True).then_inc(S["mean_x2_filled"], 1)
                    for e in range(3):
                        dst = take(i, e, ("z", f))
                        wait(pe, "yt_copied", i, f, min(3, e + 2), 3)
                        for p in range(10 * e, min(10 * e + 10, KW)):
                            o = (p // 5 % 2, p % 5 * 96)
                            if p == 0:
                                ins = pe.matmul(dst[:, 0, 0:192], yt[:, 0:P], dft_0[:], start=True, stop=True)
                            elif p > 1:
                                ins = pe.matmul(dst[:, o[0], o[1]:o[1] + 96], yt[:, (p - 1) * P:p * P], dft_h[:], start=True, stop=True)
                        ins.then_inc(S["z_filled"], 1)
                if on(GATE):
                    wait(pe, "fm_spread", i, g)
                    take_small(1, "fmap", i, g)
                    pe.matmul(fmap_ps, resize[:], fmx[:].rearrange("p g j -> p (g j)"), start=True, stop=True).then_inc(S["fmap_filled"], 1)
                if on(FREQ):
                    wait(pe, "cols_ready", i, f)
                    take_small(0, "gates", i, f)
                    pe.matmul(small[:, 0, 8:8 + H], w1a[:], y[:, 0, :, 0], start=True, stop=True)
                    pe.matmul(small[:, 0, 8 + H:8 + H + W], w1b[:], cols[:], start=True, stop=True).then_inc(S["gates_filled"], 1)
                    take_small(1, "row", i, f)
                    pe.transpose(row_ps, m2[:], ident[:]).then_inc(S["row_filled"], 1)
                if on(OUT):
                    for e in range(3):
                        dst = take(i, e, ("sel", k))
                        if e == 0:
                            shifted(pe, i, k)
                            slot_uses(pe, s_v[k % 2], i, k, 1)
                            wait(pe, "gsum_copied", i, k, per=3)
                        for a in range(2):
                            r = (2 * e + a) * 8
                            ins = pe.matmul(dst[:, a, 0:8 * WP], sel[:], v[k % 2][:, r * WP:(r + 8) * WP], start=True, stop=True)
                        ins.then_inc(S["sel_filled"], 1)
                if k == UN:
                    shift()

            steps(pe, step)

        @block.vector
        def _(dve):
            dve.memset(w1a[:], 0.0).then_inc(s_set, 1)
            dve.memset(wpw[:], 0.0).then_inc(s_set, 1)
            dve.memset(wpw_t[:], 0.0).then_inc(s_set, 1)
            credit(dve, "y_copied u_padded bn_chunks tile_stats fenced mean_read spread_ready rstd_ready shift_ready cols_ready "
                        "features products mean_dw mean_x2 row_max row_shifted row_sum row_inverse softmax_row softmax_ready "
                        "gated_rows gated_chunks gated_stats gated_rstd gated_scale gated_shift gated_weights gated_bias bias_ready "
                        "fm_ready fm_spread fmap_ready out_ready")
            for t in (up, v[0], v[1]):
                dve.memset(t[:], 0.0).then_inc(s_setd, 1)
            dve.memset(eps[:], EPS)
            dve.memset(feat[:, 9:10], 1.0)
            dve.memset(srow[:, 2, 0:1], 1.0).then_inc(s_setd, 1)
            dve.wait_ge(s_w, 16 * SETUP_LOADS)
            dve.tensor_reduce(smax[:], srow[:, 0, :].rearrange("p (g c) -> p g c", g=G), mybir.AxisListType.X, ALU.max).then_inc(s_setd, 1)
            dve.wait_ge(s_setd, 5)
            dve.tensor_tensor(srow[:, 1, :].rearrange("p (g c) -> p g c", g=G), srow[:, 0, :].rearrange("p (g c) -> p g c", g=G),
                              smax[:].rearrange("p (g o) -> p g o", o=1).broadcast_to([1, G, CG]), ALU.subtract).then_inc(s_set, 1)
            dve.wait_ge(s_seta, 1)
            dve.tensor_reduce(ssum[:], srow[:, 1, :].rearrange("p (g c) -> p g c", g=G), mybir.AxisListType.X, ALU.add).then_inc(s_set, 1)
            dve.wait_ge(s_set, 5)
            dve.reciprocal(srec[:], ssum[:]).then_inc(s_set, 1)
            dve.wait_ge(s_set, 6)
            dve.tensor_tensor(srow[:, 0, :].rearrange("p (g c) -> p g c", g=G), srow[:, 1, :].rearrange("p (g c) -> p g c", g=G),
                              srec[:].rearrange("p (g o) -> p g o", o=1).broadcast_to([1, G, CG]), ALU.mult).then_inc(s_setd, 1)
            dve.wait_ge(s_setp, 1)
            dve.tensor_copy(s1[:], s2_ps).then_inc(s_setd, 1)
            dve.wait_ge(s_setp, 2)
            dve.tensor_copy(vcol[:], m2_ps).then_inc(s_setd, 1)
            dve.tensor_tensor(b2[:], bias_ps, vec[:, 4:5], ALU.add).then_inc(s_setd, 1)
            dve.wait_ge(s_setd, 9)
            dve.tensor_tensor(b2[:], b2[:], s1[:], ALU.mult).then_inc(s_setd, 1)
            dve.tensor_tensor(sel[:], small[0:VROWS, 1, 128:256], sel_a[:], ALU.mult).then_inc(s_setd, 1)
            dve.wait_ge(s_setd, 11)
            dve.tensor_tensor(sel[:], sel[:], sel_b[:], ALU.add).then_inc(s_setd, 1)
            dve.wait_ge(s_setp, 3)
            dve.tensor_tensor(bias0[:], s2_ps, vec[:, 5:6], ALU.add).then_inc(s_setd, 1)
            dve.tensor_scalar(k1[:], taps[:], vcol[:], None, ALU.mult).then_inc(s_setd, 1)
            dve.wait_ge(s_setd, 14)
            dve.tensor_tensor(lhs_u[:].rearrange("p (t g) -> p t g", g=G), k1[:].rearrange("p (t o) -> p t o", o=1).broadcast_to([P, TAPS, G]),
                              mask4[:].rearrange("p (o g) -> p o g", o=1).broadcast_to([P, TAPS, G]), ALU.mult).then_inc(s_setd, 1)
            dve.tensor_scalar(w1b[:], w1a[:], 1.0 / H, None, ALU.mult).then_inc(s_setd, 1)
            t33 = taps[:].rearrange("p (a b) -> p a b", a=3)
            X = mybir.AxisListType.X
            dve.tensor_reduce(coef[:, 0:1], taps[:], X, ALU.add).then_inc(s_setd, 1)
            dve.tensor_reduce(coef[:, 1:2], taps[:, 6:9], X, ALU.add).then_inc(s_setd, 1)
            dve.tensor_reduce(coef[:, 2:3], taps[:, 0:3], X, ALU.add).then_inc(s_setd, 1)
            dve.tensor_reduce(coef[:, 3:4], t33[:, :, 2], X, ALU.add).then_inc(s_setd, 1)
            dve.tensor_reduce(coef[:, 4:5], t33[:, :, 0], X, ALU.add).then_inc(s_setd, 1)
            dve.tensor_scalar(coef[:, 5:6], taps[:, 8:9], 1.0 / L, None, ALU.mult).then_inc(s_setd, 1)
            dve.tensor_scalar(coef[:, 6:7], taps[:, 6:7], 1.0 / L, None, ALU.mult).then_inc(s_setd, 1)
            dve.tensor_scalar(coef[:, 7:8], taps[:, 2:3], 1.0 / L, None, ALU.mult).then_inc(s_setd, 1)
            dve.tensor_scalar(coef[:, 8:9], taps[:, 0:1], 1.0 / L, None, ALU.mult).then_inc(s_setd, 1)
            dve.tensor_copy(coef[:, 9:10], vec[:, 3:4]).then_inc(s_setd, 1)
            dve.wait_ge(s_setd, 26)
            dve.tensor_scalar(coef[:, 0:1], coef[:, 0:1], 1.0 / H, None, ALU.mult).then_inc(s_setd, 1)
            dve.tensor_scalar(coef[:, 1:3], coef[:, 1:3], -1.0 / H, None, ALU.mult).then_inc(s_setd, 1)
            dve.tensor_scalar(coef[:, 3:5], coef[:, 3:5], -1.0 / L, None, ALU.mult).then_inc(s_setd, 1)
            dve.wait_ge(s_setd, SETUP_OPS)

            def groups(t):
                return t.rearrange("p (g c) -> p g c", g=G)

            def spread_of(t):
                return t.rearrange("p (g o) -> p g o", o=1).broadcast_to([1, G, CG])

            def image(t):
                return t.rearrange("p (h w) -> p h w", w=W)

            def step(i, k, on):
                s_, f, g = k + STAT, k + FREQ, k + GATE
                if on(GATE):
                    wait(dve, "row_filled", i, g)
                    dve.tensor_reduce(smax[:], groups(row_ps), X, ALU.max).then_inc(S["row_max"], 1)
                    wait(dve, "row_max", i, g)
                    wait(dve, "softmax_filled", i, g - 1)
                    dve.tensor_tensor(groups(srow_t[:]), groups(row_ps), spread_of(smax[:]), ALU.subtract).then_inc(S["row_shifted"], 1)
                    wait(dve, "gates_ready", i, g)
                    wait(dve, "gsum_filled", i, g - 2, per=3)
                    dve.tensor_tensor(image(gated[g % 2][:]), image(gx[g % UN][:]),
                                      gates[:, 0:H].rearrange("p (h o) -> p h o", o=1).broadcast_to([P, H, W]), ALU.mult
                                      ).then_inc(S["gated_rows"], 1)
                if on(STAT):
                    slot_uses(dve, s_x[s_ % 2], i, s_, 1)
                    wait(dve, "spread_ready", i, s_ - 1)
                    for q in range(6):
                        ins = dve.bn_stats(stats[:, q, :], x[s_ % 2][:, q * HB:(q + 1) * HB])
                    ins.then_inc(S["bn_chunks"], 1)
                    wait(dve, "bn_chunks", i, s_)
                    dve.tensor_copy(chunks_in[:, 0:1], stats[:, 5, 0:1])
                    dve.bn_aggr(mv[:], stats[:].rearrange("p a b -> p (a b)")).then_inc(S["tile_stats"], 1)
                if on(OUT):
                    wait(dve, "bias_filled", i, k)
                    wait(dve, "sigmoid_done", i, k - 1, per=3)
                    dve.tensor_tensor(bias[:], bias_ps, bias0[:], ALU.add).then_inc(S["bias_ready"], 1)
                if on(FREQ):
                    for e in range(3):
                        wait(dve, "y_filled", i, f, e + 1, 3)
                        if e == 0:
                            wait(dve, "gates_filled", i, f - 1)
                        for a in range(2):
                            r = 16 * e + 8 * a
                            ins = dve.tensor_copy(y[:, :, r:r + 8, :].rearrange("p k h r -> p h k r"),
                                                  ring[e][:, a, 0:HB].rearrange("p (h k r) -> p h k r", k=KW - 1, r=2))
                        ins.then_inc(S["y_copied"], 1)
                if on(STAT):
                    wait(dve, "mean_averaged", i, s_)
                    wait(dve, "shift_ready", i, s_ - 1)
                    dve.tensor_copy(gmean[:], mean_ps)
                    dve.tensor_tensor(diff[:], mv[:, 0:1], mean_ps, ALU.subtract).then_inc(S["mean_read"], 1)
                    wait(dve, "mean_read", i, s_)
                    wait(dve, "var_averaged", i, s_ - 1)
                    dve.scalar_tensor_tensor(out=spread[:], in0=diff[:], scalar=diff[:], in1=mv[:, 1:2], op0=ALU.mult,
                                             op1=ALU.add).then_inc(S["spread_ready"], 1)
                if on(GATE):
                    wait(dve, "gated_ready", i, g)
                    for q in range(6):
                        ins = dve.bn_stats(gstats[:, q, :], gated[g % 2][:, q * HB:(q + 1) * HB])
                    ins.then_inc(S["gated_chunks"], 1)
                    wait(dve, "gated_chunks", i, g)
                    dve.tensor_copy(chunks_in[:, 1:2], gstats[:, 5, 0:1])
                    dve.bn_aggr(gmv[:], gstats[:].rearrange("p a b -> p (a b)")).then_inc(S["gated_stats"], 1)
                if on(FREQ):
                    gf = image(gx[f % UN][:])
                    dve.tensor_reduce(cols[:], gf.rearrange("p h w -> p w h"), X, ALU.add).then_inc(S["cols_ready"], 1)
                    wait(dve, "y_copied", i, f, per=3)
                    wait(dve, "products", i, f - 1)
                    dve.tensor_reduce(feat[:, 0:1], y[:, 0, :, 0], X, ALU.add)
                    dve.tensor_copy(feat[:, 1:3], y[:, 0, 0:H:H - 1, 0])
                    dve.tensor_copy(feat[:, 5:9].rearrange("p (a b) -> p a b", a=2), gf[:, 0:H:H - 1, 0:W:W - 1])
                    wait(dve, "cols_ready", i, f)
                    dve.tensor_copy(feat[:, 3:5], cols[:, 0:W:W - 1]).then_inc(S["features"], 1)
                    wait(dve, "features", i, f)
                    dve.tensor_tensor(fprod[:], feat[:], coef[:], ALU.mult).then_inc(S["products"], 1)
                    wait(dve, "products", i, f)
                    wait(dve, "mean_x2_filled", i, f - 1)
                    dve.tensor_reduce(mdw[:], fprod[:], X, ALU.add).then_inc(S["mean_dw"], 1)
                if on(GATE):
                    wait(dve, "row_exp", i, g)
                    dve.tensor_reduce(ssum[:], groups(srow_t[:]), X, ALU.add).then_inc(S["row_sum"], 1)
                    wait(dve, "row_sum", i, g)
                    dve.reciprocal(srec[:], ssum[:]).then_inc(S["row_inverse"], 1)
                    wait(dve, "row_inverse", i, g)
                    dve.tensor_tensor(groups(srow_t[:]), groups(srow_t[:]), spread_of(srec[:]), ALU.mult).then_inc(S["softmax_row"], 1)
                if on(FREQ):
                    for e in range(3):
                        wait(dve, "u_filled", i, f, e + 1, 3)
                        if e == 0:
                            shifted(dve, i, f - 1)
                        dst = up[:].rearrange("p (h w) -> p h w", w=WP)[:, 1 + 16 * e:17 + 16 * e, 1:1 + W]
                        dve.tensor_copy(dst.rearrange("p (a h) w -> p a h w", a=2),
                                        ring[e][0:TAPS * G, :, 0:HB].rearrange("p a (h w) -> p a h w", w=W)).then_inc(S["u_padded"], 1)
                    wait(dve, "mean_x2_filled", i, f)
                    wait(dve, "row_filled", i, f - 1)
                    dve.tensor_tensor(m2[:], m2_ps, vec[:, 4:5], ALU.add).then_inc(S["mean_x2"], 1)
                if on(GATE):
                    wait(dve, "softmax_filled", i, g)
                    dve.tensor_copy(s2[:], s2_ps).then_inc(S["softmax_ready"], 1)
                if on(STAT):
                    wait(dve, "std_ready", i, s_)
                    wait(dve, "gx_ready", i, s_ - 1)
                    dve.reciprocal(rstd[:], std[:]).then_inc(S["rstd_ready"], 1)
                    wait(dve, "rstd_ready", i, s_)
                    dve.scalar_tensor_tensor(out=nb[:], in0=gmean[:], scalar=-1.0, in1=rstd[:], op0=ALU.mult,
                                             op1=ALU.mult).then_inc(S["shift_ready"], 1)
                if on(GATE):
                    wait(dve, "mag_ready", i, g)
                    dve.tensor_reduce(fm[:], mag[:].rearrange("p k h -> p h k"), X, ALU.add).then_inc(S["fm_ready"], 1)
                    wait(dve, "fm_ready", i, g)
                    wait(dve, "fmap_filled", i, g - 1)
                    dve.tensor_tensor(fmx[:], fm[:].rearrange("p (o h) -> p o h", o=1).broadcast_to([P, G, H]),
                                      mask4[:].rearrange("p (g o) -> p g o", o=1).broadcast_to([P, G, H]), ALU.mult
                                      ).then_inc(S["fm_spread"], 1)
                if on(DONE):
                    wait(dve, "product_done", i, k - 1)
                    dve.wait_ge(s_res[(k - 1) % 2], i * (UN // 2 * 16) + ((k - 1) // 2 + 1) * 16)
                    o = out[(k - 1) % 2]
                    dve.tensor_tensor(o[:], o[:], res[(k - 1) % 2][:], ALU.add).then_inc(S["out_ready"], 1)
                if on(GATE):
                    wait(dve, "fmap_filled", i, g)
                    if not (isinstance(i, int) and g < 1):
                        dve.wait_ge(s_fd, i * (UN * 16) + g * 16)
                    dve.tensor_copy(fmap[:].rearrange("p g j -> p (g j)"), fmap_ps).then_inc(S["fmap_ready"], 1)
                    wait(dve, "gated_std", i, g)
                    dve.reciprocal(grstd[:], gstd[:]).then_inc(S["gated_rstd"], 1)
                    wait(dve, "gated_rstd", i, g)
                    dve.tensor_tensor(ga[:], grstd[:], vec[:, 1:2], ALU.mult).then_inc(S["gated_scale"], 1)
                    wait(dve, "gated_scale", i, g)
                    wait(dve, "softmax_ready", i, g)
                    dve.tensor_tensor(sa[:], ga[:], s2[:], ALU.mult)
                    dve.scalar_tensor_tensor(out=gc[:], in0=gmv[:, 0:1], scalar=ga[:], in1=vec[:, 2:3], op0=ALU.mult,
                                             op1=ALU.subtract).then_inc(S["gated_shift"], 1)
                    wait(dve, "gated_shift", i, g)
                    wait(dve, "bias_filled", i, g - 1)
                    dve.scalar_tensor_tensor(out=s2c[:], in0=gc[:], scalar=-1.0, in1=s2[:], op0=ALU.mult,
                                             op1=ALU.mult).then_inc(S["gated_bias"], 1)
                    wait(dve, "gsum_filled", i, g - 1, per=3)
                    dve.tensor_scalar(lhs_g[:], mask4[:], sa[:], None, ALU.mult).then_inc(S["gated_weights"], 1)

            steps(dve, step)

        @block.scalar
        def _(act):
            credit(act, "xt_copied gsum_copied sigmoid_done yt_copied z_squared std_ready row_exp gates_ready gated_std mag_ready")
            for s in s_st:
                act.sem_inc(s, 16)
            act.wait_ge(s_w, 16 * SETUP_LOADS)
            act.wait_ge(s_set, 4)
            act.activation(srow[:, 1, :], srow[:, 1, :], ACT.Exp).then_inc(s_seta, 1)
            act.wait_ge(s_setd, SETUP_OPS)

            def step(i, k, on):
                s_, f, g = k + STAT, k + FREQ, k + GATE
                if on(FREQ):
                    for e in range(3):
                        wait(act, "xt_filled", i, f, e + 1, 3)
                        act.activation(two(xt[:, e * 1024:(e + 1) * 1024]), ring[e][0:96, :, :], ACT.Identity).then_inc(S["xt_copied"], 1)
                if on(GATE):
                    wait(act, "row_shifted", i, g)
                    act.activation(srow_t[:], srow_t[:], ACT.Exp).then_inc(S["row_exp"], 1)
                if on(FREQ):
                    for e in range(3):
                        wait(act, "yt_filled", i, f, e + 1, 3)
                        act.activation(two(yt[:, e * 1024:(e + 1) * 1024]), ring[e][0:96, :, :], ACT.Identity).then_inc(S["yt_copied"], 1)
                if on(STAT):
                    wait(act, "var_averaged", i, s_)
                    wait(act, "rstd_ready", i, s_ - 1)
                    act.activation(std[:], var_ps, ACT.Sqrt, bias=eps[:]).then_inc(S["std_ready"], 1)
                if on(GATE):
                    wait(act, "mag2_ready", i, g)
                    act.activation(mag[:], mag[:], ACT.Sqrt).then_inc(S["mag_ready"], 1)
                if on(GATE):
                    wait(act, "gated_stats", i, g)
                    wait(act, "gated_rstd", i, g - 1)
                    act.activation(gstd[:], gmv[:, 1:2], ACT.Sqrt, bias=eps[:]).then_inc(S["gated_std"], 1)
                if on(OUT):
                    for e in range(3):
                        wait(act, "gsum_filled", i, k, e + 1, 3)
                        if e == 0:
                            wait(act, "sel_filled", i, k - 2, per=3)
                        dst = v[k % 2][64:64 + G, :].rearrange("p (h w) -> p h w", w=WP)[:, 16 * e:16 * e + 16, 0:W]
                        act.activation(dst.rearrange("p (a h) w -> p a h w", a=2),
                                       ring[e][64:64 + G, :, 0:HB].rearrange("p a (h w) -> p a h w", w=W), ACT.Identity
                                       ).then_inc(S["gsum_copied"], 1)
                if on(FREQ):
                    for e in range(3):
                        wait(act, "z_filled", i, f, e + 1, 3)
                        if e == 0:
                            wait(act, "mag2_ready", i, f - 1)
                        n = 2 if e < 2 else 1
                        dst = zsq[:, 10 * e:10 * e + 5 * n, :, :].rearrange("p k r h -> p (k r h)")
                        act.activation(dst.rearrange("p (a n) -> p a n", a=n), ring[e][:, 0:n, 0:480], ACT.Square).then_inc(S["z_squared"], 1)
                if on(FREQ):
                    wait(act, "gates_filled", i, f)
                    wait(act, "gated_ready", i, f - 1)
                    act.activation(gates[:], gates_ps, ACT.Sigmoid, bias=vec[:, 0:1]).then_inc(S["gates_ready"], 1)
                if on(OUT):
                    for e in range(3):
                        wait(act, "sel_filled", i, k, e + 1, 3)
                        if e == 0:
                            wait(act, "bias_ready", i, k)
                            act.wait_ge(s_st[k % 2], i * (UN // 2 * 16) + (k // 2 * 16 + 16))
                        act.activation(out[k % 2][:, e * LC:(e + 1) * LC].rearrange("p (a h w) -> p a h w", a=2, w=W),
                                       ring[e][:, :, 0:8 * WP].rearrange("p a (h w) -> p a h w", w=WP)[:, :, :, 0:W],
                                       ACT.Sigmoid, bias=bias[:]).then_inc(S["sigmoid_done"], 1)

            steps(act, step)

        @block.gpsimd
        def _(pool):
            credit(pool, "gx_ready gated_ready mag2_ready product_done")
            pool.wait_ge(s_setd, SETUP_OPS)

            def step(i, k, on):
                s_, f, g = k + STAT, k + FREQ, k + GATE
                if on(GATE):
                    wait(pool, "z_squared", i, g, per=3)
                    wait(pool, "fm_ready", i, g - 1)
                    pool.tensor_tensor(mag[:], zsq[:, :, 0, :], zsq[:, :, 1, :], ALU.add).then_inc(S["mag2_ready"], 1)
                    wait(pool, "gated_rows", i, g)
                    t = gated[g % 2][:].rearrange("p (h w) -> p h w", w=W)
                    pool.tensor_tensor(t, t, gates[:, H:H + W].rearrange("p (o w) -> p o w", o=1).broadcast_to([P, H, W]), ALU.mult
                                       ).then_inc(S["gated_ready"], 1)
                if on(DONE):
                    wait(pool, "sigmoid_done", i, k - 1, per=3)
                    o = out[(k - 1) % 2]
                    pool.tensor_tensor(o[:], o[:], gx[(k - 1) % UN][:], ALU.mult).then_inc(S["product_done"], 1)
                if on(STAT):
                    wait(pool, "shift_ready", i, s_)
                    wait(pool, "product_done", i, s_ - UN)
                    pool.tensor_tensor(norm_in[:], rstd[:], nb[:], ALU.mult)
                    pool.tensor_scalar(gx[s_ % UN][:], x[s_ % 2][:], rstd[:], nb[:], ALU.mult, ALU.add).then_inc(S["gx_ready"], 1)

            steps(pool, step)


SETUP_LOADS = 11 + 12 * G
SETUP_OPS = 29


def gate_constants():
    f = np.float32
    eye = np.eye(G)
    w, kk = np.arange(W), np.arange(KW)
    th = 2 * np.pi * np.outer(w, kk) / W
    dw = np.zeros((W, W))
    dw[:, 0], dw[:, 1] = 1, np.cos(th[:, KW - 1])
    dw[:, 2::2], dw[:, 3::2] = np.cos(th[:, 1:KW - 1]), -np.sin(th[:, 1:KW - 1])
    dft_w = np.kron(np.eye(2), dw) / W
    ph = 2 * np.pi * np.outer(np.arange(H), np.arange(H)) / H
    dh = np.zeros((H, 2, 2, H))
    dh[:, 0, 0], dh[:, 0, 1] = np.cos(ph), -np.sin(ph)
    dh[:, 1, 0], dh[:, 1, 1] = np.sin(ph), np.cos(ph)
    d0 = np.zeros((H, 2, 2, 2, H))
    for q in range(2):
        d0[:, q, q, 0], d0[:, q, q, 1] = np.cos(ph), -np.sin(ph)
    pos = np.clip((np.arange(H) + 0.5) * (CG / H) - 0.5, 0, CG - 1)
    lo = np.floor(pos).astype(int)
    hi = np.minimum(lo + 1, CG - 1)
    r = np.zeros((H, CG))
    r[np.arange(H), lo] += 1 - (pos - lo)
    r[np.arange(H), hi] += pos - lo
    mask4 = np.kron(eye, np.ones((CG, 1)))
    sel_a, sel_b = np.zeros((VROWS, P)), np.zeros((VROWS, P))
    rows = np.kron(eye, np.ones((1, CG)))
    sel_b[:TAPS * G] = np.tile(rows, (TAPS, 1))
    sel_a[TAPS * G:TAPS * G + G] = rows
    sel_b[64:] = rows
    fp_rows = np.zeros((CG, VROWS))
    fp_rows[:, TAPS * G:TAPS * G + G] = 1
    c = dict(ident=np.eye(P), group=np.kron(eye, np.ones((CG, CG))) / CG, ones4=np.kron(eye, np.ones((CG, CG))), mask4=mask4,
             dft_w=dft_w, dft_h=dh.reshape(96, 96), dft_0=d0.reshape(96, 192), resize=np.tile(r.T, (G, 1)) / KW,
             sel_a=sel_a, sel_b=sel_b, fp_rows=fp_rows)
    return {k: np.ascontiguousarray(v, dtype=f) for k, v in c.items()}


def scan_constants():
    rows = SPLIT * NBC
    pick = np.zeros((rows, 2 * DB, P), np.float32)
    for r in range(rows):
        k, s = r % NBC, r % DS
        pick[r, k // DS * DB + s // SG, 32 * (s % SG):32 * (s % SG) + 32] = 1
    minus_hi, minus_mid = -np.eye(rows, dtype=np.float32), -np.eye(rows, dtype=np.float32)
    minus_hi[:NBC] = 0
    minus_mid[:2 * NBC] = 0
    return dict(fold=np.tile(np.eye(32, dtype=np.float32), (SG, 1)), ident=np.eye(P, dtype=np.float32),
                pick=pick.reshape(rows, -1), minus_hi=minus_hi, minus_mid=minus_mid)


def build(nc, d, out):
    def scratch(name, shape):
        return nc.dram_tensor(name, shape, fp32, kind="Internal").ap()

    xn, ym = scratch("normed_input", (NTILES, P, L)), scratch("mamba_output", (NTILES, P, L))
    x1 = scratch("first_layer", (NTILES, P, L))
    spill, fmap = scratch("delta_spill", (2, 2, P, L)), scratch("frequency_map", (2, G, H, W))

    def rows(t):
        return t.rearrange("n p t -> (n p) t")

    normalise(nc, d, "norm0", d["x"], xn)
    mamba(nc, d | dict(xn=rows(xn), ym=rows(ym), spill=spill), B * C // DM // 2)
    project(nc, d, ym, d["x"], x1)
    gated_group(nc, d | dict(x1=x1, fmap=fmap, out=out))


def kernel(x, L0_conv_ln_gamma, L0_conv_ln_beta, L0_conv_skip_scale, L0_conv_in_proj_w, L0_conv_conv_w, L0_conv_conv_b,
           L0_conv_x_proj_w, L0_conv_dt_proj_w, L0_conv_dt_proj_b, L0_conv_A_log, L0_conv_D_p, L0_conv_out_proj_w,
           L0_conv_proj_w, L0_conv_proj_b, L1_conv_w1, L1_conv_b1, L1_conv_gn_gamma, L1_conv_gn_beta, L1_conv_w_dw,
           L1_conv_b_dw, L1_conv_w_pw, L1_conv_b_pw, L1_conv_w_fp, L1_conv_b_fp):
    import concourse.bacc as bacc
    from concourse.bass_utils import run_bass_kernel_spmd

    def column(v):
        return v.reshape(-1, 1)

    x = np.asarray(x)
    arrays = dict(
        x=x.reshape(NTILES, P, L),
        gamma=L0_conv_ln_gamma.reshape(NT, P).T, beta=L0_conv_ln_beta.reshape(NT, P).T,
        skip=L0_conv_skip_scale.reshape(1, 1), win_t=L0_conv_in_proj_w.T, wout_t=L0_conv_out_proj_w.T,
        conv_t=L0_conv_conv_w.T, conv_b=column(L0_conv_conv_b), xproj=L0_conv_x_proj_w, xproj_t=L0_conv_x_proj_w.T,
        dtw_t=L0_conv_dt_proj_w.T, dt_b=column(L0_conv_dt_proj_b), dp=column(L0_conv_D_p),
        a_log=L0_conv_A_log.reshape(DB, 32, DB, SG).transpose(3, 1, 2, 0).reshape(P, DS),
        proj_t=L0_conv_proj_w.T, proj_b=L0_conv_proj_b.reshape(NT, P).T,
        w1_t=L1_conv_w1.T, w_pw=L1_conv_w_pw, w_pw_t=L1_conv_w_pw.T, w_fp_t=L1_conv_w_fp.T,
        w_dw=L1_conv_w_dw.reshape(CG, TAPS), gn_beta_row=L1_conv_gn_beta.reshape(1, CG), b1=column(L1_conv_b1),
        gn_gamma=column(L1_conv_gn_gamma), gn_beta=column(L1_conv_gn_beta), b_dw=column(L1_conv_b_dw),
        b_pw=column(L1_conv_b_pw), b_fp=column(L1_conv_b_fp),
        ones=np.full((P, P), 1 / C, np.float32), **(scan_constants() | gate_constants()))
    arrays = {f"in_{n}": np.ascontiguousarray(a) for n, a in arrays.items()}

    nc = bacc.Bacc("TRN2", target_bir_lowering=False, num_devices=1)
    d = {n[3:]: nc.dram_tensor(n, a.shape, mybir.dt.from_np(a.dtype), kind="ExternalInput").ap() for n, a in arrays.items()}
    out = nc.dram_tensor("out", (NTILES, P, L), fp32, kind="ExternalOutput").ap()
    build(nc, d, out)
    return run_bass_kernel_spmd(nc, [arrays], core_ids=[0]).results[0]["out"].reshape(B, C, H, W)
```
